# Optimizing a Trainium2 kernel written in Bass

```python
import numpy as np
import jax
import jax.numpy as jnp

def _softmax(x, axis=-1):
    return jax.nn.softmax(x, axis=axis)

def _gelu(x):
    return jax.nn.gelu(x, approximate=True)

def _silu(x):
    return jax.nn.silu(x)

def _sigmoid(x):
    return jax.nn.sigmoid(x)

def _layernorm(x, axis=-1, eps=1e-05):
    m = jnp.mean(x, axis=axis, keepdims=True)
    v = jnp.var(x, axis=axis, keepdims=True)
    return (x - m) / jnp.sqrt(v + eps)

def _scatter_add(tgt, idx, src, axis=0):
    return tgt.at[idx].add(src)

def _segment_sum(src, seg, n):
    return jax.ops.segment_sum(src, seg, n)
kernel_name = 'mk_gps_d1_gnn_r8_197595'

def setup_inputs(seed: int=0):
    np.random.seed(seed)
    _w = jnp.asarray

    def _rec_inputs():
        import jax
        import jax.numpy as jnp
        _gk = jax.random.key(seed)
        x = -0.0002117 + 1 * jax.random.normal(jax.random.fold_in(_gk, 1), (6250, 256), jnp.float32)
        src = jax.random.randint(jax.random.fold_in(_gk, 2), (100000,), 0, 6250, jnp.int32)
        dst = jax.random.randint(jax.random.fold_in(_gk, 3), (100000,), 0, 6250, jnp.int32)
        _o = jnp.argsort(dst, stable=True)
        src = src[_o]
        dst = dst[_o]
        return (x, src, dst)
    x, src, dst = _rec_inputs()

    def _L0_gnn_setup():
        import jax, jax.numpy as jnp
        import numpy as np
        N_NODES = 12500
        CHANNELS = 256
        N_EDGES = 400000
        key = jax.random.key(seed)
        ks = jax.random.split(key, 7)
        C = CHANNELS
        x = jax.random.normal(ks[0], (N_NODES, C), dtype=jnp.float32)
        edge_index = jax.random.randint(ks[1], (2, N_EDGES), 0, N_NODES, dtype=jnp.int64)
        s = 1.0 / np.sqrt(C)
        W_l = jax.random.uniform(ks[2], (C, C), jnp.float32, -s, s)
        b_l = jax.random.uniform(ks[3], (C,), jnp.float32, -s, s)
        W_r = jax.random.uniform(ks[4], (C, C), jnp.float32, -s, s)
        gamma = jnp.ones((C,), jnp.float32)
        beta = jnp.zeros((C,), jnp.float32)
        return {'x': x, 'edge_index': edge_index, 'W_l': W_l, 'b_l': b_l, 'W_r': W_r, 'gamma': gamma, 'beta': beta}
    _L0_gnn_all = _L0_gnn_setup()
    _L0_gnn_in = {k: v for k, v in _L0_gnn_all.items() if k in ('W_l', 'b_l', 'W_r', 'gamma', 'beta')}
    del _L0_gnn_all

    def _L0_mix_setup():
        import jax, jax.numpy as jnp
        import numpy as np
        BN_EPS = 1e-05
        key = jax.random.key(seed)
        ks = jax.random.split(key, 4)
        B, N, D = (8, 1024, 256)
        outD = 256
        s = 1.0 / np.sqrt(D)
        return {'feature': jax.random.normal(ks[0], (B, N, D), dtype=jnp.float32), 'W_qk': jax.random.normal(ks[1], (2, D, D), dtype=jnp.float32) * s, 'b_qk': jnp.zeros((2, D), dtype=jnp.float32), 'W_v': jax.random.normal(ks[2], (D, outD), dtype=jnp.float32) * s, 'b_v': jnp.zeros((outD,), dtype=jnp.float32), 'gamma': jnp.ones((D,), dtype=jnp.float32), 'beta': jnp.zeros((D,), dtype=jnp.float32)}
    _L0_mix_all = _L0_mix_setup()
    _L0_mix_in = {k: v for k, v in _L0_mix_all.items() if k in ('W_qk', 'b_qk', 'W_v', 'b_v', 'gamma', 'beta')}
    del _L0_mix_all

    def _L0_ffn_setup():
        import jax, jax.numpy as jnp
        import numpy as np
        B, A = (512, 8)
        IN, OUT = (256, 256)
        SH1, SH2 = (256, 128)
        EH1, EH2 = (128, 64)
        E, TOPK = (4, 2)

        def _shared_mlp(x, W1, b1, W2, b2, W3, b3):
            h = jax.nn.relu(x @ W1 + b1)
            h = jax.nn.relu(h @ W2 + b2)
            return h @ W3 + b3

        def _experts_mlp(x, eW1, eb1, eW2, eb2, eW3, eb3):
            h = jax.nn.relu(jnp.einsum('baf,efh->ebah', x, eW1) + eb1[:, None, None, :])
            h = jax.nn.relu(jnp.einsum('ebah,ehg->ebag', h, eW2) + eb2[:, None, None, :])
            o = jnp.einsum('ebag,ego->ebao', h, eW3) + eb3[:, None, None, :]
            return jnp.moveaxis(o, 0, -1)
        key = jax.random.key(seed)
        ks = jax.random.split(key, 16)
        s = 0.05
        return {'x': jax.random.normal(ks[0], (B, A, IN), jnp.float32), 'sW1': jax.random.normal(ks[1], (IN, SH1), jnp.float32) * s, 'sb1': jnp.zeros((SH1,), jnp.float32), 'sW2': jax.random.normal(ks[2], (SH1, SH2), jnp.float32) * s, 'sb2': jnp.zeros((SH2,), jnp.float32), 'sW3': jax.random.normal(ks[3], (SH2, OUT), jnp.float32) * s, 'sb3': jnp.zeros((OUT,), jnp.float32), 'eW1': jax.random.normal(ks[4], (E, IN, EH1), jnp.float32) * s, 'eb1': jnp.zeros((E, EH1), jnp.float32), 'eW2': jax.random.normal(ks[5], (E, EH1, EH2), jnp.float32) * s, 'eb2': jnp.zeros((E, EH2), jnp.float32), 'eW3': jax.random.normal(ks[6], (E, EH2, OUT), jnp.float32) * s, 'eb3': jnp.zeros((E, OUT), jnp.float32), 'gW': jax.random.normal(ks[7], (IN, E), jnp.float32) * s, 'gb': jnp.zeros((E,), jnp.float32)}
    _L0_ffn_all = _L0_ffn_setup()
    _L0_ffn_in = {k: v for k, v in _L0_ffn_all.items() if k in ('sW1', 'sb1', 'sW2', 'sb2', 'sW3', 'sb3', 'eW1', 'eb1', 'eW2', 'eb2', 'eW3', 'eb3', 'gW', 'gb')}
    del _L0_ffn_all
    return {'x': x, 'src': src, 'dst': dst, 'L0_gnn_W_l': _L0_gnn_in['W_l'], 'L0_gnn_b_l': _L0_gnn_in['b_l'], 'L0_gnn_W_r': _L0_gnn_in['W_r'], 'L0_gnn_gamma': _L0_gnn_in['gamma'], 'L0_gnn_beta': _L0_gnn_in['beta'], 'L0_mix_W_qk': _L0_mix_in['W_qk'], 'L0_mix_b_qk': _L0_mix_in['b_qk'], 'L0_mix_W_v': _L0_mix_in['W_v'], 'L0_mix_b_v': _L0_mix_in['b_v'], 'L0_mix_gamma': _L0_mix_in['gamma'], 'L0_mix_beta': _L0_mix_in['beta'], 'L0_ffn_sW1': _L0_ffn_in['sW1'], 'L0_ffn_sb1': _L0_ffn_in['sb1'], 'L0_ffn_sW2': _L0_ffn_in['sW2'], 'L0_ffn_sb2': _L0_ffn_in['sb2'], 'L0_ffn_sW3': _L0_ffn_in['sW3'], 'L0_ffn_sb3': _L0_ffn_in['sb3'], 'L0_ffn_eW1': _L0_ffn_in['eW1'], 'L0_ffn_eb1': _L0_ffn_in['eb1'], 'L0_ffn_eW2': _L0_ffn_in['eW2'], 'L0_ffn_eb2': _L0_ffn_in['eb2'], 'L0_ffn_eW3': _L0_ffn_in['eW3'], 'L0_ffn_eb3': _L0_ffn_in['eb3'], 'L0_ffn_gW': _L0_ffn_in['gW'], 'L0_ffn_gb': _L0_ffn_in['gb']}

def reference(x, src, dst, L0_gnn_W_l, L0_gnn_b_l, L0_gnn_W_r, L0_gnn_gamma, L0_gnn_beta, L0_mix_W_qk, L0_mix_b_qk, L0_mix_W_v, L0_mix_b_v, L0_mix_gamma, L0_mix_beta, L0_ffn_sW1, L0_ffn_sb1, L0_ffn_sW2, L0_ffn_sb2, L0_ffn_sW3, L0_ffn_sb3, L0_ffn_eW1, L0_ffn_eb1, L0_ffn_eW2, L0_ffn_eb2, L0_ffn_eW3, L0_ffn_eb3, L0_ffn_gW, L0_ffn_gb):
    import jax
    import jax.numpy as jnp

    def _L0_gnn_ref(x, edge_index, W_l, b_l, W_r, gamma, beta):
        import jax, jax.numpy as jnp
        import numpy as np
        N_NODES = 12500
        CHANNELS = 256
        N_EDGES = 400000
        src, dst = (edge_index[0], edge_index[1])
        agg = jax.ops.segment_sum(x[src], dst, num_segments=x.shape[0])
        cnt = jax.ops.segment_sum(jnp.ones((edge_index.shape[1],), x.dtype), dst, num_segments=x.shape[0])
        agg = agg / jnp.maximum(cnt, 1.0)[:, None]
        h = agg @ W_l.T + b_l + x @ W_r.T
        mu = h.mean(axis=-1, keepdims=True)
        var = h.var(axis=-1, keepdims=True)
        hn = (h - mu) * jax.lax.rsqrt(var + 1e-05) * gamma + beta
        return x + jax.nn.relu(hn)

    def _L0_mix_ref(feature, W_qk, b_qk, W_v, b_v, gamma, beta):
        import jax, jax.numpy as jnp
        import numpy as np
        BN_EPS = 1e-05
        QK = jnp.einsum('bnd,kde->bkne', feature, W_qk) + b_qk[None, :, None, :]
        value = jnp.einsum('bnd,de->bne', feature, W_v) + b_v
        query = QK[:, 0]
        key = QK[:, 1]
        sm = jax.nn.softmax(key, axis=1)
        lam = jnp.einsum('bnd,bne->bde', sm, value)
        mean = jnp.mean(lam, axis=(0, 2), keepdims=True)
        var = jnp.var(lam, axis=(0, 2), keepdims=True)
        bn = (lam - mean) * jax.lax.rsqrt(var + BN_EPS)
        bn = bn * gamma[None, :, None] + beta[None, :, None]
        return jnp.einsum('bnd,bde->bne', query, bn)

    def _L0_ffn_ref(x, sW1, sb1, sW2, sb2, sW3, sb3, eW1, eb1, eW2, eb2, eW3, eb3, gW, gb):
        import jax, jax.numpy as jnp
        import numpy as np
        B, A = (512, 8)
        IN, OUT = (256, 256)
        SH1, SH2 = (256, 128)
        EH1, EH2 = (128, 64)
        E, TOPK = (4, 2)

        def _shared_mlp(x, W1, b1, W2, b2, W3, b3):
            h = jax.nn.relu(x @ W1 + b1)
            h = jax.nn.relu(h @ W2 + b2)
            return h @ W3 + b3

        def _experts_mlp(x, eW1, eb1, eW2, eb2, eW3, eb3):
            h = jax.nn.relu(jnp.einsum('baf,efh->ebah', x, eW1) + eb1[:, None, None, :])
            h = jax.nn.relu(jnp.einsum('ebah,ehg->ebag', h, eW2) + eb2[:, None, None, :])
            o = jnp.einsum('ebag,ego->ebao', h, eW3) + eb3[:, None, None, :]
            return jnp.moveaxis(o, 0, -1)
        all_out = _experts_mlp(x, eW1, eb1, eW2, eb2, eW3, eb3)
        shared = _shared_mlp(x, sW1, sb1, sW2, sb2, sW3, sb3)
        gates = jax.nn.softmax(x @ gW + gb, axis=-1)
        topv, topi = jax.lax.top_k(gates, TOPK)
        topw = jax.nn.softmax(topv, axis=-1)
        sel = jnp.take_along_axis(all_out, topi[:, :, None, :], axis=-1)
        gated = jnp.sum(sel * topw[:, :, None, :], axis=-1)
        return shared + gated
    edge_index = jnp.stack([src, dst])
    xn = _layernorm(x, axis=-1)
    x = x + _L0_gnn_ref(xn, edge_index, L0_gnn_W_l, L0_gnn_b_l, L0_gnn_W_r, L0_gnn_gamma, L0_gnn_beta) + _L0_mix_ref(xn[None], L0_mix_W_qk, L0_mix_b_qk, L0_mix_W_v, L0_mix_b_v, L0_mix_gamma, L0_mix_beta)[0]
    x = x + _L0_ffn_ref(_layernorm(x, axis=-1)[None], L0_ffn_sW1, L0_ffn_sb1, L0_ffn_sW2, L0_ffn_sb2, L0_ffn_sW3, L0_ffn_sb3, L0_ffn_eW1, L0_ffn_eb1, L0_ffn_eW2, L0_ffn_eb2, L0_ffn_eW3, L0_ffn_eb3, L0_ffn_gW, L0_ffn_gb)[0]
    return x

_drawn_inputs = setup_inputs


def setup_inputs(seed=0):
    import zlib

    import numpy as np

    out = dict(_drawn_inputs(seed))
    spreads = {'L0_gnn_gamma': (1.0, 0.6),
     'L0_gnn_beta': (0.0, 0.8),
     'L0_mix_b_qk': (0.0, 0.1),
     'L0_mix_b_v': (0.0, 0.1),
     'L0_mix_gamma': (1.0, 0.2),
     'L0_mix_beta': (0.0, 0.352),
     'L0_ffn_sb1': (0.0, 0.8),
     'L0_ffn_sb2': (0.0, 0.8),
     'L0_ffn_sb3': (0.0, 2.0),
     'L0_ffn_eb1': (0.0, 0.8),
     'L0_ffn_eb2': (0.0, 2.0),
     'L0_ffn_eb3': (0.0, 2.0),
     'L0_ffn_gb': (0.0, 0.8)}
    factors = {'L0_gnn_W_l': 5.686,
     'L0_gnn_b_l': 8.0,
     'L0_ffn_sW1': 8.0,
     'L0_ffn_sW2': 6.872,
     'L0_ffn_sW3': 5.679,
     'L0_ffn_eW1': 8.0,
     'L0_ffn_eW2': 8.0,
     'L0_ffn_eW3': 8.0,
     'L0_ffn_gW': 8.0}
    for name, (base, spread) in spreads.items():
        noise = np.random.default_rng([zlib.crc32(name.encode()), seed]).standard_normal(out[name].shape)
        drawn = base * np.exp(spread * noise) if base else spread * noise
        out[name] = jnp.asarray(drawn.astype(out[name].dtype))
    for name, factor in factors.items():
        out[name] = (out[name] * factor).astype(out[name].dtype)
    return out
```

```python
from contextlib import ExitStack

import concourse.bass as bass
from concourse import mybir
from concourse.alu_op_type import AluOpType as ALU

F32 = mybir.dt.float32
F16 = mybir.dt.float16
I32 = mybir.dt.int32
ACT = mybir.ActivationFunctionType
AX = mybir.AxisListType

C = 256
HALVES = C // 128
NT = 125
ROWS_A = 112
EB = 128
G = 4
H = 4
RING = G * H
GROUP = 5
SLOTS = 2
SCALE = 1024.0
ROW = 2 * C + 2
EPS = 1e-5
NO_NODE = 1.0e6
EXPERTS = 4
TOPK = 2
DVE_LINKS = 22


def gps_layer(nc, x, src, dst, W_l, b_l, W_r, gamma_g, beta_g, W_qk, b_qk, W_v, b_v, gamma_m, beta_m,
              sW1, sb1, sW2, sb2, sW3, sb3, eW1, eb1, eW2, eb2, eW3, eb3, gW, gb, out):
    N = x.shape[0]
    E = src.shape[0]
    T = N // NT
    FULL = E // EB
    REST = E - FULL * EB
    CHUNKS = -(-E // (EB * G * H)) * H
    J = CHUNKS * G
    NB = -(-J // 128)
    assert T * NT == N and T % (GROUP * SLOTS) == 0 and C == 256
    EH1, EH2 = eW1.shape[2], eW2.shape[2]
    assert EH1 == 128 and EH2 == 64 and sW2.shape[1] == 128

    gather_rows = nc.dram_tensor("gather_rows", (N, 2 * C), F16).ap()

    with ExitStack() as ctx:
        def sb(name, shape, dt=F32):
            return ctx.enter_context(nc.sbuf_tensor(name, shape, dt))

        def ps(name, shape):
            return ctx.enter_context(nc.psum_tensor(name, shape, F32))

        ps_agg = ps("ps_agg", [128, 2, 512])
        ps_turn = ps("ps_turn", [128, 512])
        ps_hm = ps("ps_hm", [128, 512])
        ps_wide = ps("ps_wide", [128, 4, 512])
        ps_l1 = ps_wide[:, 0:2, :]
        ps_l2 = ps_wide[:, 2, :]
        ps_l3 = ps_wide[:, 3, :]

        xs = sb("xs", [NT, T, C])
        xnT = sb("xnT", [128, HALVES, N])
        arena = sb("arena", [128, T * C])
        kst = arena[0:NT, :].rearrange("p (t c) -> p t c", t=T)
        AREA = SLOTS * GROUP * C * 2
        area = sb("area", [128, AREA])
        xn = area[0:NT, 0:AREA // 2].rearrange("p (s k c) -> p s k c", s=SLOTS, k=GROUP)
        xhl = area[0:NT, AREA // 2:AREA].bitcast(F16).rearrange("p (s k c) -> p s k c", s=SLOTS, k=GROUP)
        assert RING * ROW // 2 <= AREA
        ring = area[:, 0:RING * ROW // 2].bitcast(F16).rearrange("p (r c) -> p r c", r=RING)

        wlT = sb("wlT", [128, HALVES, C])
        wrT = sb("wrT", [128, HALVES, C])
        wk = sb("wk", [128, HALVES, C])
        wv = sb("wv", [128, HALVES, C])
        wqT = sb("wqT", [128, HALVES, C])
        wmix = sb("wmix", [128, HALVES, C])
        VEC = 15
        V_SB1, V_EB1, V_SB2, V_EB2, V_GM, V_BM, V_BQ = 0, 2, 6, 7, 9, 11, 13
        vec_rows = sb("vec_rows", [VEC, 128])
        vec = sb("vec", [128, VEC])
        BC = 4 * C + EXPERTS
        bc_row = sb("bc_row", [1, BC + C])
        bc = sb("bc", [128, BC])
        bl_b, gg_b, bg_b, bv_b = (bc[:, q * C:(q + 1) * C] for q in range(4))
        gb_b = bc[0:NT, 4 * C:BC]
        bk_row = bc_row[:, BC:BC + C]
        ident = sb("ident", [128, 128])
        ones = sb("ones", [128, 128])
        zero16 = sb("zero16", [128, 260], F16)
        eps = sb("eps", [128, 1])
        iota = sb("iota", [128, NT])
        tile_base = sb("tile_base", [128, T + 1])
        srcT = sb("srcT", [128, J], I32)
        dstT = sb("dstT", [128, J])
        cuts = sb("cuts", [1, T + 1], I32)
        idx = sb("idx", [128, RING], I32)
        lower = sb("lower", [NT, EXPERTS, EXPERTS])
        pick = sb("pick", [EXPERTS + 1, 2, 128])
        stats = sb("stats", [128, SLOTS, GROUP, 6])
        mv = sb("mv", [128, SLOTS, GROUP, 2])
        sm = sb("sm", [128, 8, SLOTS * GROUP])
        xT = sb("xT", [128, SLOTS, HALVES, NT])
        vs = area[0:NT, 0:SLOTS * (C + 1)].rearrange("p (u c) -> p u c", u=SLOTS)
        ek = area[0:NT, 1024:1024 + SLOTS * C].rearrange("p (u c) -> p u c", u=SLOTS)
        kmax = sb("kmax", [NT, C])
        kpart = sb("kpart", [NT, C])
        spare = area[:, RING * ROW // 2:]
        wide = spare[:, 0:HALVES * NT].rearrange("p (h n) -> p h n", h=HALVES)
        lam = spare[:, HALVES * NT:HALVES * (NT + C)].rearrange("p (h c) -> p h c", h=HALVES)

        edge_i = arena[:, 0:2 * NB * EB].bitcast(I32).rearrange("p (l b e) -> p l b e", l=2, b=NB)
        edge_f = arena[:, 2 * NB * EB:4 * NB * EB].rearrange("p (l b e) -> p l b e", l=2, b=NB)
        nat0 = 4 * NB * EB
        w_nat = arena[:, nat0:nat0 + 3 * HALVES * C].rearrange("p (w h c) -> p w h c", w=3, h=HALVES)
        cut0 = nat0 + 3 * HALVES * C
        under = arena[:, cut0:cut0 + T * NB].rearrange("p (t b) -> p t b", t=T)
        n_under = arena[:, cut0 + T * NB:cut0 + T * NB + T]
        limit = arena[:, cut0 + T * NB + T:cut0 + T * NB + 2 * T]
        row_end = arena[:, cut0 + T * NB + 2 * T:cut0 + T * NB + 2 * T + NB]
        keep = arena[:, cut0 + T * NB + 2 * T + NB:cut0 + T * NB + 2 * T + NB + 1]

        at = [0]

        def part(cols, rows=128, dt=F32):
            a = arena[0:rows, at[0]:at[0] + cols]
            at[0] += cols
            return a if dt == F32 else a.bitcast(dt)

        hot = part(H * G * 64, dt=F16).rearrange("p (h g n) -> p h g n", h=H, g=G)
        hot_next = part(G * 64, dt=F16).rearrange("p (g n) -> p g n", g=G)
        dst_rel = part(G)
        dst_rel_next = part(G)
        s1w = part(HALVES * C).rearrange("p (h c) -> p h c", h=HALVES)
        s2w = part(HALVES * 128).rearrange("p (h c) -> p h c", h=HALVES)
        s3w = part(C)
        e1w = part(HALVES * EXPERTS * EH1).rearrange("p (h e c) -> p h e c", h=HALVES, e=EXPERTS)
        e2w = part(EXPERTS * EH2).rearrange("p (e c) -> p e c", e=EXPERTS)
        e3w = part(EXPERTS // 2 * C).rearrange("p (r c) -> p r c", c=C)
        gw = part(HALVES * EXPERTS).rearrange("p (h e) -> p h e", h=HALVES)
        b35 = part(C, EXPERTS + 1)
        bmix = part(C, NT)
        agg_mean = part(C, NT)
        turned = part(4 * NT).rearrange("p (h n) -> p h n", h=4)
        aggT, x2T = turned[:, 0:2, :], turned[:, 2:4, :]
        xTc = part(2 * NT).rearrange("p (h n) -> p h n", h=2)
        hh = part(C, NT)
        hn = part(C, NT)
        x1 = part(C, NT)
        x2 = part(C, NT)
        sh1 = part(2 * NT).rearrange("p (h n) -> p h n", h=2)
        eh1 = part(EXPERTS * NT).rearrange("p (h n) -> p h n", h=EXPERTS)
        sh2 = part(NT)
        eh2 = part(2 * NT).rearrange("p (h n) -> p h n", h=2)
        eh2g = part(2 * NT).rearrange("p (h n) -> p h n", h=2)
        y = part(C, NT)
        gate5 = part(EXPERTS + 1, NT)
        gateT = part(NT, EXPERTS + 1)
        col = part(96, NT)
        (deg, rc, lmax, esum, rsum, wsum, rw) = (col[:, q:q + 1] for q in range(7))
        lv1, g1a, g1b, rs1, lv2, g2a, g2b, rs2, nt1, nt2 = (col[:, 8 + q:9 + q] for q in range(10))
        lg, ex, gt, ez, rank = (col[:, 20 + 4 * q:24 + 4 * q] for q in range(5))
        gt_m = col[:, 40:56].rearrange("p (e f) -> p e f", e=EXPERTS)
        eq_m = col[:, 56:72].rearrange("p (e f) -> p e f", e=EXPERTS)
        st1, st2 = col[:, 72:78], col[:, 78:84]
        mv1, mv2 = col[:, 84:86], col[:, 86:88]
        assert at[0] <= T * C

        names = """
            weights_in ffn_in vs_ones edges_in ident_made pad_made consts_made iota_made edges_float keep_made keep_neg
            row_end_made under_made under_reduced cuts_clean cuts_summed cuts_made vec_turned vec_made
            bc_spread bc_made nat_turned nat_copied src_turned src_copied dst_turned dst_copied
            kpart_made kmax_merged kmax_turned kmax_reduced kmax_col_wide kmax_spread kmax_made
            lam_link lam_ln lam_guess lam_done wmix_done wmix_made bmix_spread bmix_made
            ring_ones idx_copied slots_freed x2_zeroed
            rel_made hot_built rel_next_made hot_next_built tile_summed
            deg_read rc_made agg_scaled both_turned both_made xTc_made mix_done gnn_done h_made
            x2_made logits_done l1s_done l1e_done sh1_made eh1_made l2_done sh2_made eh2_made
            gate_made gate_turned gateT_made gates_spread eh2g_made l3_done y_made y_stored
            dve_link lg_made lg_shifted lg_exp z_made z_exp st1_made st2_made mv1_made ln1 guess1 x1_made mv2_made ln2 guess2
        """
        s = {name: ctx.enter_context(nc.semaphore(name)) for name in names.split()}

        def per_slot(names):
            return {n: [ctx.enter_context(nc.semaphore(f"{n}{u}")) for u in range(SLOTS)] for n in names.split()}

        a = per_slot("""x_in stats_made mv_made ln_made guess_made na nb nc rstd_made xn_made high_made
                        low_made rows_stored sum_made turned evacuated kept k_summed k_stored""")
        b = per_slot("k_shifted exp_made xT_made v_summed v_made lam_added")
        landed = [ctx.enter_context(nc.semaphore(f"landed{h}")) for h in range(H)]

        A_STEPS = T // (GROUP * SLOTS)
        PER_SLOT = GROUP * A_STEPS
        B_STEPS = T // SLOTS

        def tile_rows(dram, t, r0, r1, count=1):
            return dram.rearrange("(t p) c -> p t c", p=NT)[r0:r1, bass.ds(t, count), :]

        weight_loads = [
            (w_nat[:, 0], W_l.rearrange("(h p) c -> p h c", p=128)),
            (w_nat[:, 1], W_r.rearrange("(h p) c -> p h c", p=128)),
            (w_nat[:, 2], W_qk[0].rearrange("(h p) c -> p h c", p=128)),
            (wk[:], W_qk[1].rearrange("(h p) c -> p h c", p=128)),
            (wv[:], W_v.rearrange("(h p) c -> p h c", p=128)),
        ]
        ffn_loads = [
            (s1w, sW1.rearrange("(h p) c -> p h c", p=128)),
            (s2w, sW2.rearrange("(h p) c -> p h c", p=128)),
            (s3w, sW3),
            (e2w, eW2.rearrange("e p c -> p e c")),
            (gw, gW.rearrange("(h p) c -> p h c", p=128)),
            (b35[0:EXPERTS, :], eb3), (b35[EXPERTS:EXPERTS + 1, :], sb3.rearrange("(o c) -> o c", o=1)),
        ]
        weight_loads += [
            (vec_rows[V_SB1:V_SB1 + 2, :], sb1.rearrange("(r c) -> r c", c=128)),
            (vec_rows[V_EB1:V_EB1 + 4, :], eb1),
            (vec_rows[V_SB2:V_SB2 + 1, :], sb2.rearrange("(r c) -> r c", c=128)),
            (vec_rows[V_EB2:V_EB2 + 2, :], eb2.rearrange("(r a) c -> r (a c)", a=2)),
            (vec_rows[V_GM:V_GM + 2, :], gamma_m.rearrange("(r c) -> r c", c=128)),
            (vec_rows[V_BM:V_BM + 2, :], beta_m.rearrange("(r c) -> r c", c=128)),
            (vec_rows[V_BQ:V_BQ + 2, :], b_qk[0:1].rearrange("o (r c) -> (o r) c", c=128)),
            (bc_row[:, 0:C], b_l.rearrange("(o c) -> o c", o=1)),
            (bc_row[:, C:2 * C], gamma_g.rearrange("(o c) -> o c", o=1)),
            (bc_row[:, 2 * C:3 * C], beta_g.rearrange("(o c) -> o c", o=1)),
            (bc_row[:, 3 * C:4 * C], b_v.rearrange("(o c) -> o c", o=1)),
            (bc_row[:, 4 * C:BC], gb.rearrange("(o c) -> o c", o=1)),
            (bc_row[:, BC:BC + C], b_qk[1:2, :]),
        ]
        ffn_loads += [(e1w[:, h], eW1.rearrange("e (h p) c -> h p e c", p=128)[h]) for h in range(HALVES)]
        ffn_loads += [(e3w[64 * q:64 * q + 64], eW3.rearrange("(r a) p c -> a p r c", a=2)[q]) for q in range(2)]
        WEIGHTS_IN = 16 * len(weight_loads)
        FFN_IN = 16 * len(ffn_loads)
        WHOLE = FULL // 128 * 128
        edge_loads = []
        for l, edges in enumerate((src, dst)):
            edge_loads.append((edge_i[:, l, 0:WHOLE // 128, :],
                               edges[0:WHOLE * EB].rearrange("(b p e) -> p b e", p=128, e=EB)))
            if FULL > WHOLE:
                edge_loads.append((edge_i[0:FULL - WHOLE, l, NB - 1, :],
                                   edges[WHOLE * EB:FULL * EB].rearrange("(p e) -> p e", e=EB)))
            if REST:
                edge_loads.append((edge_i[FULL - WHOLE:FULL - WHOLE + 1, l, NB - 1, 0:REST],
                                   edges[FULL * EB:E].rearrange("(o e) -> o e", o=1)))
        EDGES_IN = 16 * len(edge_loads)
        assert WHOLE // 128 == NB - 1

        block = ctx.enter_context(nc.Block())

        @block.sync
        def _(sp):
            def load_x(g, u, seen):
                for r0, r1 in ((0, ROWS_A), (ROWS_A, NT)):
                    sp.dma_start(xs[r0:r1, bass.ds(g * GROUP, GROUP), :],
                                 tile_rows(x, g * GROUP, r0, r1, GROUP)).then_inc(a["x_in"][u], 16)

            for u in range(SLOTS):
                load_x(u, u, 0)
            sp.wait_ge(s["pad_made"], 2)
            for to, of in edge_loads:
                sp.dma_start(to, of).then_inc(s["edges_in"], 16)
            for to, of in weight_loads:
                sp.dma_start(to, of).then_inc(s["weights_in"], 16)
            for i in range(1, A_STEPS):
                for u in range(SLOTS):
                    sp.wait_ge(a["x_in"][u], 32 * i)
                    load_x(SLOTS * i + u, u, 32 * i)

            with sp.Fori(0, A_STEPS) as i:
                for u in range(SLOTS):
                    sp.wait_ge(a["low_made"][u], i + 1)
                    for r0, r1 in ((0, ROWS_A), (ROWS_A, NT)):
                        sp.dma_start(tile_rows(gather_rows, (i * SLOTS + u) * GROUP, r0, r1, GROUP),
                                     xhl[r0:r1, u]).then_inc(a["rows_stored"][u], 16)

            for u in range(SLOTS):
                sp.wait_ge(b["lam_added"][u], B_STEPS)
            for to, of in ffn_loads:
                sp.dma_start(to, of).then_inc(s["ffn_in"], 16)

        @block.gpsimd
        def _(pool):
            nc.gpsimd.memset(edge_i[:, 0, NB - 1, :], 0).then_inc(s["pad_made"], 1)
            nc.gpsimd.memset(edge_i[:, 1, NB - 1, :], int(NO_NODE)).then_inc(s["pad_made"], 1)
            nc.gpsimd.memset(ones[:], 1.0).then_inc(s["consts_made"], 1)
            nc.gpsimd.memset(zero16[:], 0.0).then_inc(s["consts_made"], 1)
            nc.gpsimd.memset(eps[:], EPS).then_inc(s["consts_made"], 1)
            pool.wait_ge(s["consts_made"], 3)
            nc.gpsimd.affine_select(out=ident[:], in_=ones[:], pattern=[[-1, 128]], compare_op=ALU.is_equal,
                                    fill=0.0, base=0, channel_multiplier=1).then_inc(s["ident_made"], 1)
            nc.gpsimd.affine_select(
                out=lower[:], in_=ones[0:NT, 0:EXPERTS * EXPERTS].rearrange("p (e f) -> p e f", e=EXPERTS),
                pattern=[[1, EXPERTS], [-1, EXPERTS]], compare_op=ALU.is_gt, fill=0.0, base=0,
                channel_multiplier=0).then_inc(s["ident_made"], 1)
            for r in range(2):
                nc.gpsimd.affine_select(
                    out=pick[:, r, :], in_=ones[0:EXPERTS + 1, :], pattern=[[-1, 2], [0, 64]],
                    compare_op=ALU.is_equal, fill=0.0, base=-2 * r, channel_multiplier=1).then_inc(s["ident_made"], 1)
            nc.gpsimd.iota(iota[:], pattern=[[1, NT]], base=0, channel_multiplier=0,
                           allow_small_or_imprecise_dtypes=True).then_inc(s["iota_made"], 1)
            nc.gpsimd.iota(tile_base[:], pattern=[[-NT, T + 1]], base=0, channel_multiplier=0,
                           allow_small_or_imprecise_dtypes=True).then_inc(s["iota_made"], 1)
            nc.gpsimd.iota(limit, pattern=[[NT, T]], base=NT, channel_multiplier=0,
                           allow_small_or_imprecise_dtypes=True).then_inc(s["iota_made"], 1)
            with pool.Fori(0, A_STEPS) as i:
                for u in range(SLOTS):
                    pool.wait_ge(a["xn_made"][u], i + 1)
                    grp = xs[:, bass.ds((i * SLOTS + u) * GROUP, GROUP), :]
                    nc.gpsimd.tensor_tensor(grp, grp, xn[:, u], ALU.add).then_inc(a["sum_made"][u], 1)
                for v in range(GROUP * SLOTS):
                    u = v % SLOTS
                    pool.wait_ge(a["evacuated"][u], i * GROUP + v // SLOTS + 1)
                    nc.gpsimd.tensor_copy(xnT[:, :, bass.ds((i * GROUP * SLOTS + v) * NT, NT)],
                                          xT[:, u]).then_inc(a["kept"][u], 1)

            for u in range(SLOTS):
                pool.wait_ge(a["rows_stored"][u], 32 * A_STEPS)
                pool.wait_ge(a["turned"][u], PER_SLOT)
                pool.wait_ge(a["k_summed"][u], PER_SLOT)
            nc.gpsimd.memset(vs[:, :, C:C + 1], 1.0).then_inc(s["vs_ones"], 1)
            with pool.Fori(0, B_STEPS) as i:
                for u in range(SLOTS):
                    if u == 0:
                        pool.wait_ge(a["kept"][SLOTS - 1], PER_SLOT)
                    pool.wait_ge(b["v_summed"][u], i)
                    nc.gpsimd.tensor_copy(xT[:, u], xnT[:, :, bass.ds((i * SLOTS + u) * NT, NT)]
                                          ).then_inc(b["xT_made"][u], 1)

            for u in range(SLOTS):
                pool.wait_ge(b["lam_added"][u], B_STEPS)
            pool.wait_ge(s["src_copied"], NB)
            nc.gpsimd.memset(ring[:, :, 2 * C:ROW], 1.0).then_inc(s["ring_ones"], 1)
            with pool.Fori(0, CHUNKS // H) as i:
                for h in range(H):
                    pool.wait_ge(s["slots_freed"], i * H + h + 1)
                    nc.gpsimd.tensor_copy(idx[:, h * G:(h + 1) * G], srcT[:, bass.ds(i * RING + h * G, G)]
                                          ).then_inc(s["idx_copied"], 1)
                    pool.wait_ge(s["ring_ones"], 1)
                    pool.wait_ge(s["idx_copied"], i * H + h + 1)
                    for g in range(G):
                        k = h * G + g
                        nc.gpsimd.indirect_dma_start(
                            ring[:, k, 0:2 * C], None, gather_rows,
                            bass.IndirectOffsetOnAxis(idx[:, k:k + 1], 0)).then_inc(landed[h], 16)

        @block.tensor
        def _(pe):
            mm = nc.tensor.matmul
            pe.wait_ge(s["ident_made"], 4)
            pe.wait_ge(s["weights_in"], WEIGHTS_IN)
            for w in range(3):
                for h in range(HALVES):
                    for k in range(HALVES):
                        last = pe.transpose(ps_wide[:, w, k * C + h * 128:k * C + h * 128 + 128],
                                            w_nat[:, w, h, k * 128:(k + 1) * 128], ident[:])
                last.then_inc(s["nat_turned"], 1)
            pe.transpose(ps_wide[:, 3, 0:VEC], vec_rows[:], ident[0:VEC, 0:VEC]).then_inc(s["vec_turned"], 1)
            mm(ps_agg[:, 0, 0:512], ones[0:1, :], bc_row[:, 0:512], start=True, stop=True)
            mm(ps_agg[:, 1, 0:512], ones[0:1, :], bc_row[:, 512:1024], start=True, stop=True)
            mm(ps_hm[:, 0:EXPERTS], ones[0:1, :], bc_row[:, 1024:BC], start=True, stop=True).then_inc(s["bc_spread"], 1)
            pe.wait_ge(s["under_reduced"], 1)
            pe.wait_ge(s["bc_made"], 2)
            mm(ps_hm[0:1, 128:128 + T], ones[:, 0:1], n_under, start=True, stop=True).then_inc(s["cuts_summed"], 1)
            pe.wait_ge(s["edges_float"], 2)
            pe.wait_ge(s["cuts_made"], 1)
            for blk in range(NB):
                if blk:
                    pe.wait_ge(s["src_copied"], blk)
                pe.transpose(ps_turn[:, 0:128], edge_f[:, 0, blk, :], ident[:]).then_inc(s["src_turned"], 1)
                if blk:
                    pe.wait_ge(s["dst_copied"], blk)
                pe.transpose(ps_hm[:, 0:128], edge_f[:, 1, blk, :], ident[:]).then_inc(s["dst_turned"], 1)

            pe.wait_ge(s["nat_copied"], 3)
            pe.wait_ge(s["vec_made"], 1)
            with pe.Fori(0, A_STEPS) as i:
                for v in range(GROUP * SLOTS + 1):
                    if v < GROUP * SLOTS:
                        u, t = v % SLOTS, v // SLOTS
                        if v % GROUP == 0:
                            pe.wait_ge(a["xn_made"][v // GROUP], i + 1)
                        pe.wait_ge(a["evacuated"][u], i * GROUP + t)
                        for h in range(HALVES):
                            last = pe.transpose(ps_wide[:, u, h * NT:(h + 1) * NT],
                                                xn[:, v // GROUP, v % GROUP, h * 128:(h + 1) * 128],
                                                ident[0:NT, 0:NT])
                        last.then_inc(a["turned"][u], 1)
                    if v:
                        u, t = (v - 1) % SLOTS, (v - 1) // SLOTS
                        pe.wait_ge(a["evacuated"][u], i * GROUP + t + 1)
                        pe.wait_ge(a["k_stored"][u], i * GROUP + t)
                        kk = ps_wide[0:NT, 2 + u, 0:C]
                        mm(kk, ones[0:1, 0:NT], bk_row, start=True, stop=False)
                        for h in range(HALVES):
                            last = mm(kk, xT[:, u, h, :], wk[:, h, :], start=False, stop=(h == HALVES - 1))
                        last.then_inc(a["k_summed"][u], 1)

            pe.wait_ge(s["kmax_merged"], A_STEPS + 1)
            pe.wait_ge(s["src_copied"], NB)
            pe.wait_ge(s["dst_copied"], NB)
            for h in range(HALVES):
                last = pe.transpose(ps_turn[:, h * NT:(h + 1) * NT], kmax[:, h * 128:(h + 1) * 128], ident[0:NT, 0:NT])
            last.then_inc(s["kmax_turned"], 1)
            pe.wait_ge(s["kmax_col_wide"], 1)
            for h in range(HALVES):
                last = mm(ps_hm[0:NT, h * 128:(h + 1) * 128], wide[:, h, :], ident[:], start=True, stop=True)
            last.then_inc(s["kmax_spread"], 1)
            for h in range(HALVES):
                mm(ps_agg[:, h, 0:C + 1], zero16[:, 0:128], zero16[:, 0:C + 1], start=True, stop=False,
                   skip_group_check=True)
            pe.wait_ge(s["vs_ones"], 1)
            with pe.Fori(0, B_STEPS) as i:
                for u in range(SLOTS):
                    pe.wait_ge(b["xT_made"][u], i + 1)
                    pe.wait_ge(b["v_made"][u], i)
                    for h in range(HALVES):
                        last = mm(ps_wide[0:NT, u, 0:C], xT[:, u, h, :], wv[:, h, :], start=(h == 0),
                                  stop=(h == HALVES - 1))
                    last.then_inc(b["v_summed"][u], 1)
                for u in range(SLOTS):
                    pe.wait_ge(b["exp_made"][u], i + 1)
                    pe.wait_ge(b["v_made"][u], i + 1)
                    for h in range(HALVES):
                        last = mm(ps_agg[:, h, 0:C + 1], ek[:, u, h * 128:(h + 1) * 128], vs[:, u, :],
                                  start=False, stop=False, skip_group_check=True)
                    last.then_inc(b["lam_added"][u], 1)
            pe.wait_ge(s["lam_done"], 1)
            for k in range(HALVES):
                for h in range(HALVES):
                    last = mm(ps_wide[:, k, 0:C], wqT[:, h, k * 128:(k + 1) * 128], lam[:, h, :], start=(h == 0),
                              stop=(h == HALVES - 1))
            last.then_inc(s["wmix_done"], 1)
            for h in range(HALVES):
                last = mm(ps_wide[0:NT, 2, 0:C], wide[:, h, :], lam[:, h, :], start=(h == 0), stop=(h == HALVES - 1))
            last.then_inc(s["bmix_spread"], 1)
            pe.wait_ge(s["wmix_made"], 1)
            pe.wait_ge(s["bmix_made"], 1)

            nn, cut, bank = (pe.alloc_register(q) for q in ("pe_tile", "pe_cut", "pe_bank"))
            pe.wait_ge(s["cuts_made"], 1)
            pe.wait_ge(s["ffn_in"], FFN_IN)
            pe.sem_inc(s["slots_freed"], H)
            pe.reg_mov(nn, 0)
            pe.reg_mov(bank, 0)
            pe.reg_load(cut, cuts[0:1, 0:1])
            sums = ps_agg.rearrange("p b c -> p (b c)")

            def clear(bank_v):
                return mm(sums[0:NT, bass.ds(bank_v, C + 1)], zero16[:, 0:NT], zero16[:, 0:C + 1],
                          start=True, stop=False, skip_group_check=True)

            def add_chunk(h, onehot, bank_v):
                for g in range(G):
                    w = onehot[:, g, 0:NT]
                    m = mm(sums[0:NT, bass.ds(bank_v, C)], w, ring[:, h * G + g, 0:C], start=False, stop=False,
                           skip_group_check=True)
                    last = mm(sums[0:NT, bass.ds(bank_v, C + 1)], w, ring[:, h * G + g, C:2 * C + 1], start=False,
                              stop=False, skip_group_check=True)
                return last

            def stage2_l1(v, prev):
                pe.wait_ge(s["both_made"], v)
                pe.wait_ge(s["sh1_made"], prev)
                for h in range(HALVES):
                    last = mm(ps_turn[0:NT, 500:500 + EXPERTS], x2T[:, h, :], gw[:, h, :], start=(h == 0), stop=(h == 1))
                last.then_inc(s["logits_done"], 1)
                for o in range(2):
                    for h in range(HALVES):
                        last = mm(ps_l1[:, 0, o * NT:(o + 1) * NT], s1w[:, h, o * 128:(o + 1) * 128], x2T[:, h, :],
                                  start=(h == 0), stop=(h == 1))
                last.then_inc(s["l1s_done"], 1)
                pe.wait_ge(s["eh1_made"], prev)
                for e in range(EXPERTS):
                    for h in range(HALVES):
                        last = mm(ps_l1[:, 1, e * NT:(e + 1) * NT], e1w[:, h, e, :], x2T[:, h, :],
                                  start=(h == 0), stop=(h == 1))
                last.then_inc(s["l1e_done"], 1)

            def stage2_l2(v, prev):
                pe.wait_ge(s["gate_made"], v)
                pe.transpose(ps_turn[0:EXPERTS + 1, 0:NT], gate5[:], ident[0:NT, 0:NT]).then_inc(s["gate_turned"], 1)
                pe.wait_ge(s["sh1_made"], v)
                for h in range(2):
                    last = mm(ps_l2[:, 0:NT], s2w[:, h, :], sh1[:, h, :], start=(h == 0), stop=(h == 1))
                pe.wait_ge(s["eh1_made"], v)
                for e in range(EXPERTS):
                    q = 64 * (e % 2)
                    c0 = NT * (1 + e // 2)
                    last = mm(ps_l2[q:q + 64, c0:c0 + NT], e2w[:, e, :], eh1[:, e, :], start=True, stop=True)
                last.then_inc(s["l2_done"], 1)
                pe.wait_ge(s["gateT_made"], v)
                pe.wait_ge(s["y_made"], prev)
                for r in range(2):
                    last = mm(ps_l3[:, C + r * NT:C + (r + 1) * NT], pick[:, r, :], gateT, start=True, stop=True)
                last.then_inc(s["gates_spread"], 1)

            def stage2_l3(v):
                o = ps_l3[0:NT, 0:C]
                pe.wait_ge(s["sh2_made"], v)
                pe.wait_ge(s["eh2g_made"], v)
                mm(o, gateT, b35, start=True, stop=False)
                mm(o, sh2, s3w, start=False, stop=False)
                for r in range(2):
                    last = mm(o, eh2g[:, r, :], e3w[:, r, :], start=False, stop=(r == 1))
                last.then_inc(s["l3_done"], 1)

            def turn_x2(v, prev):
                pe.wait_ge(s["x2_made"], v)
                pe.wait_ge(s["gateT_made"], prev)
                for h in range(HALVES):
                    last = pe.transpose(ps_turn[:, (2 + h) * NT:(3 + h) * NT], x2[:, h * 128:(h + 1) * 128],
                                        ident[0:NT, 0:NT])
                return last

            def node_tile(v, prev):
                turn_x2(v, prev)
                pe.wait_ge(s["agg_scaled"], v)
                for h in range(HALVES):
                    last = pe.transpose(ps_turn[:, h * NT:(h + 1) * NT], agg_mean[:, h * 128:(h + 1) * 128],
                                        ident[0:NT, 0:NT])
                last.then_inc(s["both_turned"], 1)
                pe.wait_ge(s["xTc_made"], v)
                pe.wait_ge(s["x1_made"], prev)
                for h in range(HALVES):
                    last = mm(ps_hm[0:NT, C:2 * C], xTc[:, h, :], wmix[:, h, :], start=(h == 0), stop=(h == 1))
                last.then_inc(s["mix_done"], 1)
                stage2_l1(v, prev)
                pe.wait_ge(s["h_made"], prev)
                for h in range(HALVES):
                    mm(ps_hm[0:NT, 0:C], xTc[:, h, :], wrT[:, h, :], start=(h == 0), stop=False)
                for h in range(HALVES):
                    last = mm(ps_hm[0:NT, 0:C], aggT[:, h, :], wlT[:, h, :], start=False, stop=(h == 1))
                last.then_inc(s["gnn_done"], 1)
                stage2_l2(v, prev)
                stage2_l3(v)

            clear(0)
            with pe.Fori(0, CHUNKS // H) as i:
                for h in range(H):
                    bank_v = pe.snap(bank, min_val=0, max_val=512)
                    pe.wait_ge(landed[h], (i + 1) * (16 * G))
                    pe.wait_ge(s["hot_built"], i * H + h + 1)
                    add_chunk(h, hot[:, h], bank_v)
                    with pe.While(lambda: pe.snap(cut, min_val=-1, max_val=CHUNKS) == i * H + h):
                        prev = pe.snap(nn, min_val=0, max_val=T - 1)
                        v = pe.snap(prev + 1, min_val=1, max_val=T)
                        pe.reg_sub(bank, 512, bank)
                        bank_w = pe.snap(bank, min_val=0, max_val=512)
                        pe.wait_ge(s["agg_scaled"], prev)
                        pe.wait_ge(s["deg_read"], prev)
                        clear(bank_w).then_inc(s["tile_summed"], 1)
                        node_tile(v, prev)
                        pe.wait_ge(s["hot_next_built"], v)
                        add_chunk(h, hot_next, bank_w)
                        pe.reg_load(cut, cuts[0:1, bass.ds(v, 1)])
                        pe.reg_add(nn, nn, 1)
                    mm(sums[0:1, bass.ds(pe.snap(bank, min_val=0, max_val=512) + C + 2, 1)], zero16[:, 0:1],
                       zero16[:, 0:1], start=False, stop=False, skip_group_check=True).then_inc(s["slots_freed"], 1)
            turn_x2(T + 1, T).then_inc(s["both_turned"], 1)
            stage2_l1(T + 1, T)
            stage2_l2(T + 1, T)
            stage2_l3(T + 1)

        v2 = nc.vector
        op = v2.tensor_tensor

        @block.vector
        def _(dve):
            dve.wait_ge(s["edges_in"], EDGES_IN)
            v2.tensor_copy(edge_f[:, 1], edge_i[:, 1]).then_inc(s["edges_float"], 1)
            v2.tensor_copy(edge_f[:, 0], edge_i[:, 0]).then_inc(s["edges_float"], 1)
            v2.memset(cuts[:], -1).then_inc(s["cuts_clean"], 1)
            dve.wait_ge(s["ident_made"], 4)
            v2.tensor_reduce(keep, ident.rearrange("p (k g) -> p g k", g=G)[:, G - 1, :], AX.X, ALU.add
                             ).then_inc(s["keep_made"], 1)
            dve.wait_ge(s["keep_made"], 1)
            v2.tensor_scalar(keep, keep, -NO_NODE, NO_NODE, ALU.mult, ALU.add).then_inc(s["keep_neg"], 1)
            dve.wait_ge(s["keep_neg"], 1)
            dve.wait_ge(s["edges_float"], 1)
            v2.tensor_scalar(row_end, edge_f[:, 1, :, EB - 1], keep, None, ALU.max).then_inc(s["row_end_made"], 1)
            dve.wait_ge(s["row_end_made"], 1)
            dve.wait_ge(s["iota_made"], 3)
            op(under, row_end.unsqueeze(1).broadcast_to([128, T, NB]), limit.unsqueeze(2).broadcast_to([128, T, NB]),
               ALU.is_lt).then_inc(s["under_made"], 1)
            dve.wait_ge(s["under_made"], 1)
            v2.tensor_reduce(n_under, under, AX.X, ALU.add).then_inc(s["under_reduced"], 1)
            dve.wait_ge(s["vec_turned"], 1)
            v2.tensor_copy(vec[:], ps_wide[:, 3, 0:VEC]).then_inc(s["vec_made"], 1)
            dve.wait_ge(s["bc_spread"], 1)
            v2.tensor_copy(bc[:, 0:4 * C].rearrange("p (b c) -> p b c", b=2), ps_agg[:]).then_inc(s["bc_made"], 1)
            v2.tensor_copy(bc[:, 4 * C:BC], ps_hm[:, 0:EXPERTS]).then_inc(s["bc_made"], 1)
            dve.wait_ge(s["cuts_summed"], 1)
            dve.wait_ge(s["cuts_clean"], 1)
            v2.tensor_copy(cuts[:, 0:T], ps_hm[0:1, 128:128 + T]).then_inc(s["cuts_made"], 1)
            for blk in range(NB):
                n = min(128, J - blk * 128)
                dve.wait_ge(s["src_turned"], blk + 1)
                v2.tensor_copy(srcT[:, blk * 128:blk * 128 + n], ps_turn[:, 0:n]).then_inc(s["src_copied"], 1)

            var = mv[0:NT, :, :, 1]
            ln_a, guess_a, tmp_a, rstd_a = (sm[0:NT, q].rearrange("p (u k) -> p u k", u=SLOTS) for q in range(4))

            def stage_a(i):
                for u in range(SLOTS):
                    t0 = (i * SLOTS + u) * GROUP
                    dve.wait_ge(a["x_in"][u], (i + 1) * 32)
                    for k in range(GROUP):
                        last = v2.bn_stats(stats[0:NT, u, k, :], xs[:, bass.ds(t0 + k, 1), :])
                    last.then_inc(a["stats_made"][u], 1)
                    dve.wait_ge(s["iota_made"], 3)
                    dve.wait_ge(a["stats_made"][u], i + 1)
                    for k in range(GROUP):
                        last = v2.bn_aggr(mv[0:NT, u, k, :], stats[0:NT, u, k, :])
                    last.then_inc(a["mv_made"][u], 1)
                for u in range(SLOTS):
                    t0 = (i * SLOTS + u) * GROUP
                    dve.wait_ge(a["guess_made"][u], i + 1)
                    op(tmp_a[:, u], guess_a[:, u], guess_a[:, u], ALU.mult).then_inc(a["na"][u], 1)
                    dve.wait_ge(a["na"][u], i + 1)
                    v2.scalar_tensor_tensor(tmp_a[:, u], var[:, u], EPS, tmp_a[:, u], ALU.add, ALU.mult
                                            ).then_inc(a["nb"][u], 1)
                    dve.wait_ge(a["nb"][u], i + 1)
                    v2.tensor_scalar(tmp_a[:, u], tmp_a[:, u], -0.5, 1.5, ALU.mult, ALU.add).then_inc(a["nc"][u], 1)
                    dve.wait_ge(a["nc"][u], i + 1)
                    op(rstd_a[:, u], guess_a[:, u], tmp_a[:, u], ALU.mult).then_inc(a["rstd_made"][u], 1)
                    dve.wait_ge(a["rstd_made"][u], i + 1)
                    dve.wait_ge(a["sum_made"][u], i)
                    dve.wait_ge(a["high_made"][u], i)
                    dve.wait_ge(a["low_made"][u], i)
                    for w in range(SLOTS):
                        dve.wait_ge(a["turned"][w], i * GROUP)
                    for k in range(GROUP):
                        last = v2.tensor_scalar(xn[:, u, k, :], xs[:, bass.ds(t0 + k, 1), :].squeeze(1),
                                                mv[0:NT, u, k, 0:1], rstd_a[:, u, k:k + 1], ALU.subtract, ALU.mult)
                    last.then_inc(a["xn_made"][u], 1)
                for u in range(SLOTS):
                    dve.wait_ge(a["high_made"][u], i + 1)
                    v2.scalar_tensor_tensor(xhl[:, u, :, C:2 * C], xn[:, u], SCALE, xhl[:, u, :, 0:C], ALU.mult,
                                            ALU.subtract).then_inc(a["low_made"][u], 1)

            def k_of_step(i, out_ap):
                for w in range(SLOTS):
                    dve.wait_ge(a["k_stored"][w], (i + 1) * GROUP)
                tiles = kst[:, bass.ds(i * GROUP * SLOTS, GROUP * SLOTS), :]
                return v2.tensor_reduce(out_ap, tiles.rearrange("p t c -> p c t"), AX.X, ALU.max)

            stage_a(0)
            v2.memset(kmax[:], -3.0e38).then_inc(s["kmax_merged"], 1)
            with dve.Fori(1, A_STEPS) as i:
                stage_a(i)
                dve.wait_ge(s["kmax_merged"], i)
                k_of_step(i - 1, kpart[:]).then_inc(s["kpart_made"], 1)
                dve.wait_ge(s["kpart_made"], i)
                op(kmax[:], kmax[:], kpart[:], ALU.max).then_inc(s["kmax_merged"], 1)
            dve.wait_ge(s["kmax_merged"], A_STEPS)
            k_of_step(A_STEPS - 1, kpart[:]).then_inc(s["kpart_made"], 1)
            dve.wait_ge(s["kpart_made"], A_STEPS)
            op(kmax[:], kmax[:], kpart[:], ALU.max).then_inc(s["kmax_merged"], 1)

            kcol = sm[:, 4, 0:HALVES]
            dve.wait_ge(s["kmax_turned"], 1)
            v2.tensor_reduce(kcol, ps_turn[:, 0:HALVES * NT].rearrange("p (h n) -> p h n", h=HALVES), AX.X, ALU.max
                             ).then_inc(s["kmax_reduced"], 1)
            dve.wait_ge(s["kmax_reduced"], 1)
            for u in range(SLOTS):
                dve.wait_ge(a["rows_stored"][u], 32 * A_STEPS)
            for h in range(HALVES):
                last = v2.tensor_scalar(wide[:, h, :], ones[:, 0:NT], kcol[:, h:h + 1], None, ALU.mult)
            last.then_inc(s["kmax_col_wide"], 1)
            dve.wait_ge(s["kmax_spread"], 1)
            v2.tensor_copy(kmax[:], ps_hm[0:NT, 0:C]).then_inc(s["kmax_made"], 1)
            dve.wait_ge(s["kmax_made"], 1)
            with dve.Fori(0, B_STEPS) as i:
                for u in range(SLOTS):
                    k_t = kst[:, bass.ds(i * SLOTS + u, 1), :].squeeze(1)
                    op(k_t, k_t, kmax[:], ALU.subtract).then_inc(b["k_shifted"][u], 1)

            links = [0]

            def link(ins):
                links[0] += 1
                ins.then_inc(s["lam_link"], 1)
                dve.wait_ge(s["lam_link"], links[0])

            for u in range(SLOTS):
                dve.wait_ge(b["lam_added"][u], B_STEPS)
            den, st, mvl = sm[:, 4, 2:4], stats[:, 0, 0:2, :], mv[:, 0, 0:2, :]
            ln_b, guess_b, tmp_b, rstd_b = (sm[:, 5, 2 * q:2 * q + 2] for q in range(4))
            link(v2.reciprocal(den, ps_agg[:, :, C]))
            for h in range(HALVES):
                link(v2.scalar_tensor_tensor(lam[:, h, :], ps_agg[:, h, 0:C], den[:, h:h + 1], bv_b, ALU.mult, ALU.add))
                link(v2.bn_stats(st[:, h, :], lam[:, h, :]))
                v2.bn_aggr(mvl[:, h, :], st[:, h, :]).then_inc(s["lam_ln"], 1)
            dve.wait_ge(s["lam_guess"], 1)
            link(op(tmp_b, guess_b, guess_b, ALU.mult))
            link(v2.scalar_tensor_tensor(tmp_b, mvl[:, :, 1], EPS, tmp_b, ALU.add, ALU.mult))
            link(v2.tensor_scalar(tmp_b, tmp_b, -0.5, 1.5, ALU.mult, ALU.add))
            link(op(tmp_b, tmp_b, guess_b, ALU.mult))
            link(op(rstd_b, tmp_b, vec[:, V_GM:V_GM + 2], ALU.mult))
            for h in range(HALVES):
                v2.tensor_scalar(wide[:, h, :], ones[:, 0:NT], vec[:, V_BQ + h:V_BQ + h + 1], None, ALU.mult)
                link(v2.tensor_scalar(lam[:, h, :], lam[:, h, :], mvl[:, h, 0:1], rstd_b[:, h:h + 1], ALU.subtract,
                                      ALU.mult))
                link(v2.tensor_scalar(lam[:, h, :], lam[:, h, :], vec[:, V_BM + h:V_BM + h + 1], None, ALU.add))
            dve.sem_inc(s["lam_done"], 1)
            dve.wait_ge(s["bmix_spread"], 1)
            v2.tensor_copy(bmix, ps_wide[0:NT, 2, 0:C]).then_inc(s["bmix_made"], 1)

            v2.memset(x1, 0.0).then_inc(s["x2_zeroed"], 1)
            v2.memset(gate5, 1.0).then_inc(s["x2_zeroed"], 1)
            v2.memset(x2, 0.0).then_inc(s["x2_made"], 1)
            dve.wait_ge(s["dst_copied"], NB)
            dve.wait_ge(s["x2_zeroed"], 2)
            dve.wait_ge(s["x2_made"], 1)
            dve.wait_ge(s["bmix_made"], 1)
            sums = ps_agg.rearrange("p b c -> p (b c)")

            def one_hot(to, rel, h_c, tile, rel_made, made, seen):
                v2.tensor_scalar(rel, dstT[:, bass.ds(h_c * G, G)], tile_base[:, bass.ds(tile, 1)], None, ALU.add
                                 ).then_inc(rel_made, 1)
                dve.wait_ge(rel_made, seen)
                op(to[:, :, 0:NT], iota[:].unsqueeze(1).broadcast_to([128, G, NT]),
                   rel.unsqueeze(2).broadcast_to([128, G, NT]), ALU.is_equal).then_inc(made, 1)

            done = [0]

            def after(base, ins):
                done[0] += 1
                ins.then_inc(s["dve_link"], 1)
                dve.wait_ge(s["dve_link"], base + done[0])

            def gates(v, prev, base):
                dve.wait_ge(s["logits_done"], v)
                op(lg, ps_turn[0:NT, 500:500 + EXPERTS], gb_b, ALU.add).then_inc(s["lg_made"], 1)
                dve.wait_ge(s["lg_made"], v)
                after(base, v2.tensor_reduce(lmax, lg, AX.X, ALU.max))
                v2.tensor_scalar(lg, lg, lmax, None, ALU.subtract).then_inc(s["lg_shifted"], 1)
                dve.wait_ge(s["lg_exp"], v)
                after(base, v2.reciprocal(rsum, esum))
                after(base, v2.tensor_scalar(gt, ex, rsum, None, ALU.mult))
                v2.tensor_scalar(ez, gt, rsum, None, ALU.subtract).then_inc(s["z_made"], 1)
                g_e = gt.unsqueeze(2).broadcast_to([NT, EXPERTS, EXPERTS])
                g_f = gt.unsqueeze(1).broadcast_to([NT, EXPERTS, EXPERTS])
                op(gt_m, g_f, g_e, ALU.is_gt)
                after(base, op(eq_m, g_f, g_e, ALU.is_equal))
                after(base, op(eq_m, eq_m, lower[:], ALU.mult))
                after(base, op(gt_m, gt_m, eq_m, ALU.add))
                after(base, v2.tensor_reduce(rank, gt_m, AX.X, ALU.add))
                dve.wait_ge(s["z_exp"], v)
                after(base, v2.scalar_tensor_tensor(ez, rank, float(TOPK), ez, ALU.is_lt, ALU.mult, accum_out=wsum))
                after(base, v2.reciprocal(rw, wsum))
                dve.wait_ge(s["gate_turned"], prev)
                v2.tensor_scalar(gate5[:, 0:EXPERTS], ez, rw, None, ALU.mult).then_inc(s["gate_made"], 1)

            def stage2_weigh(v, prev):
                dve.wait_ge(s["eh2_made"], v)
                dve.wait_ge(s["gates_spread"], v)
                dve.wait_ge(s["l3_done"], prev)
                op(eh2g, ps_l3[:, C:C + 2 * NT].rearrange("p (h n) -> p h n", h=2), eh2, ALU.mult
                   ).then_inc(s["eh2g_made"], 1)

            def stage2_out(v, prev):
                dve.wait_ge(s["l3_done"], v)
                dve.wait_ge(s["y_stored"], prev * 32)
                op(y, ps_l3[0:NT, 0:C], x1, ALU.add).then_inc(s["y_made"], 1)

            def newton(base, guess, variance, tmp, to):
                after(base, op(tmp, guess, guess, ALU.mult))
                after(base, v2.scalar_tensor_tensor(tmp, variance, EPS, tmp, ALU.add, ALU.mult))
                after(base, v2.tensor_scalar(tmp, tmp, -0.5, 1.5, ALU.mult, ALU.add))
                after(base, op(to, guess, tmp, ALU.mult))

            def node_tile(v, prev, bank_v):
                done[0] = 0
                base = dve.snap(prev * DVE_LINKS, min_val=0, max_val=T * DVE_LINKS)
                dve.wait_ge(s["tile_summed"], v)
                dve.wait_ge(s["agg_scaled"], prev)
                v2.tensor_scalar(deg, sums[0:NT, bass.ds(bank_v + C, 1)], 1.0, SCALE, ALU.max, ALU.mult
                                 ).then_inc(s["deg_read"], 1)
                dve.wait_ge(s["deg_read"], v)
                v2.reciprocal(rc, deg).then_inc(s["rc_made"], 1)
                gates(v, prev, base)
                dve.wait_ge(s["gnn_done"], v)
                op(hh, ps_hm[0:NT, 0:C], bl_b[0:NT], ALU.add).then_inc(s["h_made"], 1)
                dve.wait_ge(s["h_made"], v)
                v2.bn_stats(st1, hh).then_inc(s["st1_made"], 1)
                dve.wait_ge(s["x2_zeroed"], 2)
                dve.wait_ge(s["st1_made"], v)
                v2.bn_aggr(mv1, st1).then_inc(s["mv1_made"], 1)
                stage2_weigh(v, prev)
                dve.wait_ge(s["guess1"], v)
                newton(base, g1a, mv1[:, 1:2], nt1, rs1)
                after(base, v2.tensor_scalar(hn, hh, mv1[:, 0:1], rs1, ALU.subtract, ALU.mult))
                after(base, op(hn, hn, gg_b[0:NT], ALU.mult))
                after(base, op(hn, hn, bg_b[0:NT], ALU.add))
                stage2_out(v, prev)
                dve.wait_ge(s["y_made"], v)
                after(base, v2.scalar_tensor_tensor(x1, hn, 0.0, xs[:, bass.ds(prev, 1), :].squeeze(1),
                                                    ALU.max, ALU.add))
                dve.wait_ge(s["mix_done"], v)
                after(base, op(x1, ps_hm[0:NT, C:2 * C], x1, ALU.add))
                op(x1, x1, bmix, ALU.add).then_inc(s["x1_made"], 1)
                dve.wait_ge(s["x1_made"], v)
                v2.bn_stats(st2, x1).then_inc(s["st2_made"], 1)
                dve.wait_ge(s["x2_zeroed"], 2)
                dve.wait_ge(s["st2_made"], v)
                v2.bn_aggr(mv2, st2).then_inc(s["mv2_made"], 1)
                dve.wait_ge(s["guess2"], v)
                newton(base, g2a, mv2[:, 1:2], nt2, rs2)
                dve.wait_ge(s["both_turned"], v)
                v2.tensor_scalar(x2, x1, mv2[:, 0:1], rs2, ALU.subtract, ALU.mult).then_inc(s["x2_made"], 1)
                assert done[0] == DVE_LINKS, done

            nn, cut, bank = (dve.alloc_register(q) for q in ("dve_tile", "dve_cut", "dve_bank"))
            dve.reg_mov(nn, 0)
            dve.reg_mov(bank, 0)
            dve.wait_ge(s["cuts_made"], 1)
            dve.reg_load(cut, cuts[0:1, 0:1])
            with dve.Fori(0, CHUNKS // H) as i:
                for h in range(H):
                    c = i * H + h
                    dve.wait_ge(s["slots_freed"], c + 1)
                    dve.wait_ge(s["hot_built"], c)
                    one_hot(hot[:, h], dst_rel, c, dve.snap(nn, min_val=0, max_val=T), s["rel_made"], s["hot_built"], c + 1)
                    with dve.While(lambda: dve.snap(cut, min_val=-1, max_val=CHUNKS) == c):
                        prev = dve.snap(nn, min_val=0, max_val=T - 1)
                        v = dve.snap(prev + 1, min_val=1, max_val=T)
                        dve.wait_ge(s["tile_summed"], v)
                        dve.wait_ge(s["hot_next_built"], prev)
                        one_hot(hot_next, dst_rel_next, c, v, s["rel_next_made"], s["hot_next_built"], v)
                        node_tile(v, prev, dve.snap(bank, min_val=0, max_val=512))
                        dve.reg_sub(bank, 512, bank)
                        dve.reg_load(cut, cuts[0:1, bass.ds(v, 1)])
                        dve.reg_add(nn, nn, 1)
            v = T + 1
            done[0] = 0
            gates(v, T, T * DVE_LINKS)
            stage2_weigh(v, T)
            stage2_out(v, T)

        @block.scalar
        def _(act):
            f = nc.scalar.activation
            act.preload_act_table_set("natural_log_exp_and_others")
            for w, to in enumerate((wlT, wrT, wqT)):
                act.wait_ge(s["nat_turned"], w + 1)
                f(to[:], ps_wide[:, w, :].rearrange("p (k c) -> p k c", k=HALVES), ACT.Copy).then_inc(s["nat_copied"], 1)
            for blk in range(NB):
                n = min(128, J - blk * 128)
                act.wait_ge(s["dst_turned"], blk + 1)
                f(dstT[:, blk * 128:blk * 128 + n], ps_hm[:, 0:n], ACT.Copy).then_inc(s["dst_copied"], 1)

            var = mv[0:NT, :, :, 1]
            ln_a, guess_a = (sm[0:NT, q].rearrange("p (u k) -> p u k", u=SLOTS) for q in range(2))
            act.wait_ge(s["consts_made"], 3)
            with act.Fori(0, A_STEPS) as i:
                for u in range(SLOTS):
                    act.wait_ge(a["mv_made"][u], i + 1)
                    f(ln_a[:, u], var[:, u], ACT.Ln, bias=eps[0:NT]).then_inc(a["ln_made"][u], 1)
                    act.wait_ge(a["ln_made"][u], i + 1)
                    act.wait_ge(a["rstd_made"][u], i)
                    f(guess_a[:, u], ln_a[:, u], ACT.Exp, scale=-0.5).then_inc(a["guess_made"][u], 1)
                for v in range(GROUP * SLOTS + 1):
                    if v < GROUP * SLOTS:
                        u, t = v % SLOTS, v // SLOTS
                        if v % GROUP == 0:
                            g = v // GROUP
                            act.wait_ge(a["xn_made"][g], i + 1)
                            act.wait_ge(a["rows_stored"][g], i * 32)
                            f(xhl[:, g, :, 0:C], xn[:, g], ACT.Copy, scale=SCALE).then_inc(a["high_made"][g], 1)
                        act.wait_ge(a["turned"][u], i * GROUP + t + 1)
                        act.wait_ge(a["kept"][u], i * GROUP + t)
                        act.wait_ge(a["k_summed"][u], i * GROUP + t)
                        f(xT[:, u], ps_wide[:, u, 0:HALVES * NT].rearrange("p (h n) -> p h n", h=HALVES), ACT.Copy
                          ).then_inc(a["evacuated"][u], 1)
                    if v:
                        u, t = (v - 1) % SLOTS, (v - 1) // SLOTS
                        act.wait_ge(a["k_summed"][u], i * GROUP + t + 1)
                        f(kst[:, bass.ds(i * GROUP * SLOTS + v - 1, 1), :].squeeze(1), ps_wide[0:NT, 2 + u, 0:C],
                          ACT.Copy).then_inc(a["k_stored"][u], 1)

            for u in range(SLOTS):
                act.wait_ge(a["rows_stored"][u], 32 * A_STEPS)
            with act.Fori(0, B_STEPS) as i:
                for u in range(SLOTS):
                    act.wait_ge(b["k_shifted"][u], i + 1)
                    act.wait_ge(b["lam_added"][u], i)
                    f(ek[:, u, :], kst[:, bass.ds(i * SLOTS + u, 1), :].squeeze(1), ACT.Exp
                      ).then_inc(b["exp_made"][u], 1)
                    act.wait_ge(b["v_summed"][u], i + 1)
                    f(vs[:, u, 0:C], ps_wide[0:NT, u, 0:C], ACT.Copy).then_inc(b["v_made"][u], 1)
            ln_b, guess_b = (sm[:, 5, 2 * q:2 * q + 2] for q in range(2))
            act.wait_ge(s["lam_ln"], 2)
            f(ln_b, mv[:, 0, 0:2, 1], ACT.Ln, bias=eps[:]).then_inc(s["lam_ln"], 1)
            act.wait_ge(s["lam_ln"], 3)
            f(guess_b, ln_b, ACT.Exp, scale=-0.5).then_inc(s["lam_guess"], 1)
            act.wait_ge(s["wmix_done"], 1)
            f(wmix[:], ps_wide[:, 0:2, 0:C], ACT.Copy).then_inc(s["wmix_made"], 1)
            act.wait_ge(s["bmix_made"], 1)

            def rsqrt(v, variance, ln, guess, ready, ln_made, made):
                act.wait_ge(ready, v)
                f(ln, variance, ACT.Ln, bias=eps[0:NT]).then_inc(ln_made, 1)
                act.wait_ge(ln_made, v)
                f(guess, ln, ACT.Exp, scale=-0.5).then_inc(made, 1)

            def stage2_exps(v):
                act.wait_ge(s["lg_shifted"], v)
                f(ex, lg, ACT.Exp, accum_out=esum).then_inc(s["lg_exp"], 1)
                act.wait_ge(s["l1s_done"], v)
                act.wait_ge(s["l2_done"], v - 1)
                for o in range(2):
                    last = f(sh1[:, o, :], ps_l1[:, 0, o * NT:(o + 1) * NT], ACT.Relu, bias=vec[:, V_SB1 + o:V_SB1 + o + 1])
                last.then_inc(s["sh1_made"], 1)
                act.wait_ge(s["z_made"], v)
                f(ez, ez, ACT.Exp).then_inc(s["z_exp"], 1)
                act.wait_ge(s["l1e_done"], v)
                for e in range(EXPERTS):
                    last = f(eh1[:, e, :], ps_l1[:, 1, e * NT:(e + 1) * NT], ACT.Relu, bias=vec[:, V_EB1 + e:V_EB1 + e + 1])
                last.then_inc(s["eh1_made"], 1)
                act.wait_ge(s["gate_turned"], v)
                act.wait_ge(s["l3_done"], v - 1)
                f(gateT, ps_turn[0:EXPERTS + 1, 0:NT], ACT.Copy).then_inc(s["gateT_made"], 1)

            def stage2_relu(v):
                act.wait_ge(s["l2_done"], v)
                act.wait_ge(s["eh2g_made"], v - 1)
                for r in range(2):
                    last = f(eh2[:, r, :], ps_l2[:, (1 + r) * NT:(2 + r) * NT], ACT.Relu,
                             bias=vec[:, V_EB2 + r:V_EB2 + r + 1])
                last.then_inc(s["eh2_made"], 1)
                f(sh2, ps_l2[:, 0:NT], ACT.Relu, bias=vec[:, V_SB2:V_SB2 + 1]).then_inc(s["sh2_made"], 1)

            def turn_back(v):
                act.wait_ge(s["both_turned"], v)
                act.wait_ge(s["l1e_done"], v - 1)
                act.wait_ge(s["gnn_done"], v - 1)
                f(turned, ps_turn[:, 0:4 * NT].rearrange("p (h n) -> p h n", n=NT), ACT.Copy
                  ).then_inc(s["both_made"], 1)

            def store(v):
                act.wait_ge(s["y_made"], v)
                for r0, r1 in ((0, ROWS_A), (ROWS_A, NT)):
                    act.dma_start(tile_rows(out, v - 2, r0, r1), y[r0:r1].unsqueeze(1)).then_inc(s["y_stored"], 16)

            def node_tile(v, bank_v, first=False):
                act.wait_ge(s["gnn_done"], v - 1)
                f(xTc, xnT[:, :, bass.ds((v - 1) * NT, NT)], ACT.Copy).then_inc(s["xTc_made"], 1)
                act.wait_ge(s["tile_summed"], v)
                act.wait_ge(s["rc_made"], v)
                act.wait_ge(s["both_turned"], v - 1)
                f(agg_mean, ps_agg[0:NT, bank_v, 0:C], ACT.Copy, scale=rc).then_inc(s["agg_scaled"], 1)
                turn_back(v)
                stage2_exps(v)
                rsqrt(v, mv1[:, 1:2], lv1, g1a, s["mv1_made"], s["ln1"], s["guess1"])
                stage2_relu(v)
                if first:
                    act.sem_inc(s["y_stored"], 32)
                else:
                    store(v)
                rsqrt(v, mv2[:, 1:2], lv2, g2a, s["mv2_made"], s["ln2"], s["guess2"])

            node_tile(1, 0, first=True)
            with act.Fori(0, T // 2 - 1) as i:
                for u in range(2):
                    node_tile(act.snap(i * 2 + 2 + u, min_val=2, max_val=T), 1 - u)
            node_tile(T, (T - 1) % 2)
            v = T + 1
            act.wait_ge(s["both_turned"], v)
            f(x2T, ps_turn[:, 2 * NT:4 * NT].rearrange("p (h n) -> p h n", n=NT), ACT.Copy).then_inc(s["both_made"], 1)
            stage2_exps(v)
            stage2_relu(v)
            store(v)
            act.wait_ge(s["y_stored"], 32 * (T + 1))


_INS = ["x", "src", "dst"] + [f"L0_gnn_{n}" for n in ("W_l", "b_l", "W_r", "gamma", "beta")] + \
       [f"L0_mix_{n}" for n in ("W_qk", "b_qk", "W_v", "b_v", "gamma", "beta")] + \
       [f"L0_ffn_{n}" for n in ("sW1", "sb1", "sW2", "sb2", "sW3", "sb3", "eW1", "eb1", "eW2", "eb2", "eW3", "eb3",
                                "gW", "gb")]


def kernel(**inputs):
    import numpy as _np
    import concourse.bacc as _bacc
    from concourse import mybir as _mybir
    from concourse.bass_utils import run_bass_kernel_spmd as _run

    nc = _bacc.Bacc("TRN2", target_bir_lowering=False, num_devices=1)
    arrays, args = {}, []
    for name in _INS:
        a = _np.ascontiguousarray(inputs[name])
        arrays[f"in_{name}_dram"] = a
        args.append(nc.dram_tensor(f"in_{name}_dram", a.shape, _mybir.dt.from_np(a.dtype), kind="ExternalInput").ap())
    args.append(nc.dram_tensor("out_dram", inputs["x"].shape, F32, kind="ExternalOutput").ap())
    gps_layer(nc, *args)
    r = _run(nc, [arrays], core_ids=[0])
    return r.results[0]["out_dram"]
```

```python
from contextlib import ExitStack

import concourse.bass as bass
from concourse import mybir
from concourse.alu_op_type import AluOpType as ALU

F32 = mybir.dt.float32
F16 = mybir.dt.float16
I32 = mybir.dt.int32
I16 = mybir.dt.int16
ACT = mybir.ActivationFunctionType
AX = mybir.AxisListType

C = 256
HALVES = C // 128
NT = 125
ROWS_A = 112
EB = 128
G = 4
H = 7
RING = G * H
HOTS = 8
GROUP = 5
SLOTS = 2
SCALE = 1024.0
ROW = 2 * C + 2
EPS = 1e-5
NO_NODE = 30000.0
EXPERTS = 4
TOPK = 2
DVE_LINKS = 12


def gps_layer(nc, x, src, dst, W_l, b_l, W_r, gamma_g, beta_g, W_qk, b_qk, W_v, b_v, gamma_m, beta_m,
              sW1, sb1, sW2, sb2, sW3, sb3, eW1, eb1, eW2, eb2, eW3, eb3, gW, gb, out):
    N = x.shape[0]
    E = src.shape[0]
    T = N // NT
    FULL = E // EB
    REST = E - FULL * EB
    CHUNKS = -(-E // (EB * G * H)) * H
    J = CHUNKS * G
    NB = -(-J // 128)
    assert T * NT == N and T % (GROUP * SLOTS) == 0 and C == 256 and CHUNKS % 2 == 0 and N < NO_NODE < 2 ** 15
    EH1, EH2 = eW1.shape[2], eW2.shape[2]
    assert EH1 == 128 and EH2 == 64 and sW2.shape[1] == 128

    gather_rows = nc.dram_tensor("gather_rows", (N, 2 * C), F16).ap()

    with ExitStack() as ctx:
        def sb(name, shape, dt=F32):
            return ctx.enter_context(nc.sbuf_tensor(name, shape, dt))

        def ps(name, shape):
            return ctx.enter_context(nc.psum_tensor(name, shape, F32))

        ps_agg = ps("ps_agg", [128, 2, 512])
        ps_turn = ps("ps_turn", [128, 512])
        ps_hm = ps("ps_hm", [128, 512])
        ps_wide = ps("ps_wide", [128, 4, 512])
        ps_l1 = ps_wide[:, 0:2, :]
        ps_mix = ps_wide[0:NT, 0, C:2 * C]
        ps_l2 = ps_wide[:, 2, :]
        ps_l3 = ps_wide[:, 3, :]

        xs = sb("xs", [NT, T, C + 1])
        xnT = sb("xnT", [128, HALVES, N])
        arena = sb("arena", [128, T * C])
        kst = arena[0:NT, :].rearrange("p (t c) -> p t c", t=T)
        AREA = RING * ROW // 2
        GROUPS = SLOTS * GROUP * C
        area = sb("area", [128, AREA])
        assert 2 * GROUPS <= AREA
        xn = area[0:NT, 0:GROUPS].rearrange("p (s k c) -> p s k c", s=SLOTS, k=GROUP)
        xhl = area[0:NT, GROUPS:2 * GROUPS].bitcast(F16).rearrange("p (s k c) -> p s k c", s=SLOTS, k=GROUP)
        ring = area[:].bitcast(F16).rearrange("p (r c) -> p r c", r=RING)

        wlT = sb("wlT", [128, HALVES, C])
        wrT = sb("wrT", [128, HALVES, C])
        wk = sb("wk", [128, HALVES, C])
        wv = sb("wv", [128, HALVES, C])
        wqT = sb("wqT", [128, HALVES, C])
        wmix = sb("wmix", [128, HALVES, C])
        VEC = 15
        V_SB1, V_EB1, V_SB2, V_EB2, V_GM, V_BM, V_BQ = 0, 2, 6, 7, 9, 11, 13
        vec = sb("vec", [128, VEC])
        BC = 4 * C + EXPERTS
        bk_row = sb("bk_row", [1, C])
        bc = sb("bc", [128, BC])
        bl_b, gg_b, bg_b, bv_b = (bc[:, q * C:(q + 1) * C] for q in range(4))
        gb_b = bc[0:NT, 4 * C:BC]
        ident = sb("ident", [128, 128])
        ones = sb("ones", [128, 128])
        zero16 = sb("zero16", [128, 260], F16)
        eps = sb("eps", [128, 1])
        iota = sb("iota", [128, NT])
        tile_base = sb("tile_base", [128, T + 1])
        srcT = sb("srcT", [128, J], I16)
        dst_in = sb("dst_in", [128, J + HOTS * G])
        cuts = sb("cuts", [1, T + 1], I32)
        idx = sb("idx", [128, RING], I32)
        lower = sb("lower", [NT, EXPERTS, EXPERTS])
        pick = sb("pick", [EXPERTS + 1, 2, 128])
        stats = sb("stats", [128, SLOTS, GROUP, 6])
        mv = sb("mv", [128, SLOTS, GROUP, 2])
        sm = sb("sm", [128, 8, SLOTS * GROUP])
        pad = sb("pad", [128, SLOTS * C])
        xT = pad[:, 0:SLOTS * HALVES * NT].rearrange("p (u h n) -> p u h n", u=SLOTS, h=HALVES)
        wide = xT[:, 0]
        ek = pad[0:NT, :].rearrange("p (u c) -> p u c", u=SLOTS)
        kmax = sb("kmax", [NT, C])
        kpart = sb("kpart", [NT, C])

        edge_i = arena[:, 0:2 * NB * EB].bitcast(I32).rearrange("p (l b e) -> p l b e", l=2, b=NB)
        edge_f = arena[:, 2 * NB * EB:4 * NB * EB].rearrange("p (l b e) -> p l b e", l=2, b=NB)
        nat0 = 4 * NB * EB
        w_nat = arena[:, nat0:nat0 + 3 * HALVES * C].rearrange("p (w h c) -> p w h c", w=3, h=HALVES)
        cut0 = nat0 + 3 * HALVES * C
        under = arena[:, cut0:cut0 + T * NB].rearrange("p (t b) -> p t b", t=T)
        n_under = arena[:, cut0 + T * NB:cut0 + T * NB + T]
        limit = arena[:, cut0 + T * NB + T:cut0 + T * NB + 2 * T]
        row_end = arena[:, cut0 + T * NB + 2 * T:cut0 + T * NB + 2 * T + NB]
        keep = arena[:, cut0 + T * NB + 2 * T + NB:cut0 + T * NB + 2 * T + NB + 1]
        row0 = cut0 + T * NB + 2 * T + NB + 1
        bc_row = arena[0:1, row0:row0 + BC]
        vec_rows = arena[0:VEC, row0 + BC:row0 + BC + 128]
        chunk0 = row0 + BC + 128
        chunk_no = arena[0:T, chunk0:chunk0 + CHUNKS]
        begun = arena[0:T, chunk0 + CHUNKS:chunk0 + 2 * CHUNKS]
        begun_all = arena[:, chunk0 + 2 * CHUNKS + 1:chunk0 + 3 * CHUNKS + 1]
        assert chunk0 + 3 * CHUNKS + 1 <= T * C
        cut_col = arena[0:T, chunk0 + 2 * CHUNKS:chunk0 + 2 * CHUNKS + 1]

        at = [0]

        def part(cols, rows=128, dt=F32):
            a = arena[0:rows, at[0]:at[0] + cols]
            at[0] += cols
            return a if dt == F32 else a.bitcast(dt)

        hot_all = part(HOTS * G * 64, dt=F16)
        hot_next = part(G * 64, dt=F16).rearrange("p (g n) -> p g n", g=G)
        lam_n = part(HALVES * C).rearrange("p (h c) -> p h c", h=HALVES)
        lam_nT = part(HALVES * C).rearrange("p (h c) -> p h c", h=HALVES)
        lam = part(HALVES * C).rearrange("p (h c) -> p h c", h=HALVES)
        x_rows = part(2 * C, NT).rearrange("p (u c) -> p u c", u=2)
        dst_rel_next = part(G)
        s1w = part(HALVES * C).rearrange("p (h c) -> p h c", h=HALVES)
        s2w = part(HALVES * 128).rearrange("p (h c) -> p h c", h=HALVES)
        s3w = part(C)
        e1w = part(HALVES * EXPERTS * EH1).rearrange("p (h e c) -> p h e c", h=HALVES, e=EXPERTS)
        e2w = part(EXPERTS * EH2).rearrange("p (e c) -> p e c", e=EXPERTS)
        e3w = part(EXPERTS // 2 * C).rearrange("p (r c) -> p r c", c=C)
        gw = part(HALVES * EXPERTS).rearrange("p (h e) -> p h e", h=HALVES)
        b35 = part(C, EXPERTS + 1)
        bmix = part(C, NT)
        agg_mean = part(C, NT)
        turned = part(4 * NT).rearrange("p (h n) -> p h n", h=4)
        aggT, x2T = turned[:, 0:2, :], turned[:, 2:4, :]
        xTc = part(2 * NT).rearrange("p (h n) -> p h n", h=2)
        hh = part(C, NT)
        hn = part(C, NT)
        x1 = part(C, NT)
        x2 = part(C, NT)
        sh1 = part(2 * NT).rearrange("p (h n) -> p h n", h=2)
        eh1 = part(EXPERTS * NT).rearrange("p (h n) -> p h n", h=EXPERTS)
        sh2 = part(NT)
        eh2 = part(2 * NT).rearrange("p (h n) -> p h n", h=2)
        eh2g = part(2 * NT).rearrange("p (h n) -> p h n", h=2)
        y = part(C, NT)
        gate5 = part(EXPERTS + 1, NT)
        gateT = part(NT, EXPERTS + 1)
        col = part(96, NT)
        (deg, rc, lmax, esum, rsum, wsum, rw) = (col[:, q:q + 1] for q in range(7))
        lv1, rs1, lv2, rs2 = (col[:, 8 + q:9 + q] for q in range(4))
        lg, ex, gt, ez, rank = (col[:, 20 + 4 * q:24 + 4 * q] for q in range(5))
        gt_m = col[:, 40:56].rearrange("p (e f) -> p e f", e=EXPERTS)
        eq_m = col[:, 56:72].rearrange("p (e f) -> p e f", e=EXPERTS)
        st1, st2 = col[:, 72:78], col[:, 78:84]
        mv1, mv2 = col[:, 84:86], col[:, 86:88]
        assert at[0] <= T * C

        names = """
            weights_in ffn_in xs_ones x_row_used lam_n_made lam_turned lam_nT_made lam_v edges_in ident_made pad_made consts_made iota_made edges_float keep_made keep_neg
            row_end_made under_made under_reduced cuts_clean cuts_summed cuts_made cut_col_made begun_made begun_summed begun_copied dst_shifted vec_turned vec_made
            bc_spread bc_made nat_turned nat_copied src_turned src_copied dst_turned dst_copied
            kpart_made kmax_merged kmax_turned kmax_reduced kmax_col_wide kmax_spread kmax_made
            lam_link lam_ln lam_guess lam_done wmix_done wmix_made bmix_spread bmix_made
            ring_ones idx_copied slots_freed x2_zeroed
            hot_built rel_next_made hot_next_built tile_summed next_summed
            deg_read rc_made agg_scaled both_turned both_made xTc_made mix_done gnn_done h_made
            x2_made logits_done l1s_done l1e_done sh1_made eh1_made l2_done sh2_made eh2_made
            gate_made gate_turned gateT_made gates_spread eh2g_made l3_done y_made y_stored
            dve_link lg_made lg_shifted lg_exp z_made z_exp st1_made st2_made mv1_made ln1 rs1_made x1_made mv2_made ln2 rs2_made
        """
        s = {name: ctx.enter_context(nc.semaphore(name)) for name in names.split()}

        def per_slot(names):
            return {n: [ctx.enter_context(nc.semaphore(f"{n}{u}")) for u in range(SLOTS)] for n in names.split()}

        a = per_slot("""x_in stats_made mv_made ln_made rstd_made xn_made high_made
                        low_made rows_stored rows_kept turned evacuated kept k_summed k_stored""")
        b = per_slot("k_shifted exp_made lam_added")
        x_row_in = [ctx.enter_context(nc.semaphore(f"x_row_in{u}")) for u in range(2)]
        landed = [ctx.enter_context(nc.semaphore(f"landed{h}")) for h in range(H)]

        A_STEPS = T // (GROUP * SLOTS)
        PER_SLOT = GROUP * A_STEPS
        B_STEPS = T // SLOTS

        def tile_rows(dram, t, r0, r1, count=1):
            return dram.rearrange("(t p) c -> p t c", p=NT)[r0:r1, bass.ds(t, count), :]

        weight_loads = [
            (w_nat[:, 0], W_l.rearrange("(h p) c -> p h c", p=128)),
            (w_nat[:, 1], W_r.rearrange("(h p) c -> p h c", p=128)),
            (w_nat[:, 2], W_qk[0].rearrange("(h p) c -> p h c", p=128)),
            (wk[:], W_qk[1].rearrange("(h p) c -> p h c", p=128)),
            (wv[:], W_v.rearrange("(h p) c -> p h c", p=128)),
        ]
        ffn_loads = [
            (s1w, sW1.rearrange("(h p) c -> p h c", p=128)),
            (s2w, sW2.rearrange("(h p) c -> p h c", p=128)),
            (s3w, sW3),
            (e2w, eW2.rearrange("e p c -> p e c")),
            (gw, gW.rearrange("(h p) c -> p h c", p=128)),
            (b35[0:EXPERTS, :], eb3), (b35[EXPERTS:EXPERTS + 1, :], sb3.rearrange("(o c) -> o c", o=1)),
        ]
        weight_loads += [
            (vec_rows[V_SB1:V_SB1 + 2, :], sb1.rearrange("(r c) -> r c", c=128)),
            (vec_rows[V_EB1:V_EB1 + 4, :], eb1),
            (vec_rows[V_SB2:V_SB2 + 1, :], sb2.rearrange("(r c) -> r c", c=128)),
            (vec_rows[V_EB2:V_EB2 + 2, :], eb2.rearrange("(r a) c -> r (a c)", a=2)),
            (vec_rows[V_GM:V_GM + 2, :], gamma_m.rearrange("(r c) -> r c", c=128)),
            (vec_rows[V_BM:V_BM + 2, :], beta_m.rearrange("(r c) -> r c", c=128)),
            (vec_rows[V_BQ:V_BQ + 2, :], b_qk[0:1].rearrange("o (r c) -> (o r) c", c=128)),
            (bc_row[:, 0:C], b_l.rearrange("(o c) -> o c", o=1)),
            (bc_row[:, C:2 * C], gamma_g.rearrange("(o c) -> o c", o=1)),
            (bc_row[:, 2 * C:3 * C], beta_g.rearrange("(o c) -> o c", o=1)),
            (bc_row[:, 3 * C:4 * C], b_v.rearrange("(o c) -> o c", o=1)),
            (bc_row[:, 4 * C:BC], gb.rearrange("(o c) -> o c", o=1)),
            (bk_row[:], b_qk[1:2, :]),
        ]
        ffn_loads += [(e1w[:, h], eW1.rearrange("e (h p) c -> h p e c", p=128)[h]) for h in range(HALVES)]
        ffn_loads += [(e3w[64 * q:64 * q + 64], eW3.rearrange("(r a) p c -> a p r c", a=2)[q]) for q in range(2)]
        WEIGHTS_IN = 16 * len(weight_loads)
        FFN_IN = 16 * len(ffn_loads)
        WHOLE = FULL // 128 * 128
        edge_loads = []
        for l, edges in enumerate((src, dst)):
            edge_loads.append((edge_i[:, l, 0:WHOLE // 128, :],
                               edges[0:WHOLE * EB].rearrange("(b p e) -> p b e", p=128, e=EB)))
            if FULL > WHOLE:
                edge_loads.append((edge_i[0:FULL - WHOLE, l, NB - 1, :],
                                   edges[WHOLE * EB:FULL * EB].rearrange("(p e) -> p e", e=EB)))
            if REST:
                edge_loads.append((edge_i[FULL - WHOLE:FULL - WHOLE + 1, l, NB - 1, 0:REST],
                                   edges[FULL * EB:E].rearrange("(o e) -> o e", o=1)))
        EDGES_IN = 16 * len(edge_loads)
        assert WHOLE // 128 == NB - 1

        block = ctx.enter_context(nc.Block())

        @block.sync
        def _(sp):
            def load_x(g, u, seen):
                for r0, r1 in ((0, ROWS_A), (ROWS_A, NT)):
                    sp.dma_start(xs[r0:r1, bass.ds(g * GROUP, GROUP), 0:C],
                                 tile_rows(x, g * GROUP, r0, r1, GROUP)).then_inc(a["x_in"][u], 16)

            for u in range(SLOTS):
                load_x(u, u, 0)
            sp.wait_ge(s["pad_made"], 2)
            for to, of in edge_loads:
                sp.dma_start(to, of).then_inc(s["edges_in"], 16)
            for to, of in weight_loads:
                sp.dma_start(to, of).then_inc(s["weights_in"], 16)
            for i in range(1, A_STEPS):
                for u in range(SLOTS):
                    sp.wait_ge(a["x_in"][u], 32 * i)
                    load_x(SLOTS * i + u, u, 32 * i)

            with sp.Fori(0, A_STEPS) as i:
                for u in range(SLOTS):
                    sp.wait_ge(a["low_made"][u], i + 1)
                    for r0, r1 in ((0, ROWS_A), (ROWS_A, NT)):
                        sp.dma_start(tile_rows(gather_rows, (i * SLOTS + u) * GROUP, r0, r1, GROUP),
                                     xhl[r0:r1, u]).then_inc(a["rows_stored"][u], 16)

            for u in range(SLOTS):
                sp.wait_ge(b["lam_added"][u], B_STEPS)
            for to, of in ffn_loads:
                sp.dma_start(to, of).then_inc(s["ffn_in"], 16)
            def load_tile(t, u):
                for r0, r1 in ((0, ROWS_A), (ROWS_A, NT)):
                    sp.dma_start(x_rows[r0:r1, u:u + 1, :], tile_rows(x, t, r0, r1)
                                 ).then_inc(x_row_in[u], 16)

            load_tile(0, 0)
            load_tile(1, 1)
            with sp.Fori(0, T // 2 - 1) as i:
                for u in range(2):
                    sp.wait_ge(s["ffn_in"], FFN_IN)
                    sp.wait_ge(s["x_row_used"], i * 2 + u + 1)
                    load_tile(i * 2 + u + 2, u)

        @block.gpsimd
        def _(pool):
            nc.gpsimd.memset(edge_i[:, 0, NB - 1, :], 0).then_inc(s["pad_made"], 1)
            nc.gpsimd.memset(edge_i[:, 1, NB - 1, :], int(NO_NODE)).then_inc(s["pad_made"], 1)
            nc.gpsimd.memset(ones[:], 1.0).then_inc(s["consts_made"], 1)
            nc.gpsimd.memset(zero16[:], 0.0).then_inc(s["consts_made"], 1)
            nc.gpsimd.memset(eps[:], EPS).then_inc(s["consts_made"], 1)
            pool.wait_ge(s["consts_made"], 3)
            nc.gpsimd.affine_select(out=ident[:], in_=ones[:], pattern=[[-1, 128]], compare_op=ALU.is_equal,
                                    fill=0.0, base=0, channel_multiplier=1).then_inc(s["ident_made"], 1)
            nc.gpsimd.affine_select(
                out=lower[:], in_=ones[0:NT, 0:EXPERTS * EXPERTS].rearrange("p (e f) -> p e f", e=EXPERTS),
                pattern=[[1, EXPERTS], [-1, EXPERTS]], compare_op=ALU.is_gt, fill=0.0, base=0,
                channel_multiplier=0).then_inc(s["ident_made"], 1)
            for r in range(2):
                nc.gpsimd.affine_select(
                    out=pick[:, r, :], in_=ones[0:EXPERTS + 1, :], pattern=[[-1, 2], [0, 64]],
                    compare_op=ALU.is_equal, fill=0.0, base=-2 * r, channel_multiplier=1).then_inc(s["ident_made"], 1)
            nc.gpsimd.iota(iota[:], pattern=[[1, NT]], base=0, channel_multiplier=0,
                           allow_small_or_imprecise_dtypes=True).then_inc(s["iota_made"], 1)
            nc.gpsimd.iota(tile_base[:], pattern=[[-NT, T + 1]], base=0, channel_multiplier=0,
                           allow_small_or_imprecise_dtypes=True).then_inc(s["iota_made"], 1)
            nc.gpsimd.memset(dst_in[:, J:J + HOTS * G], NO_NODE).then_inc(s["iota_made"], 1)
            nc.gpsimd.iota(chunk_no, pattern=[[1, CHUNKS]], base=0, channel_multiplier=0,
                           allow_small_or_imprecise_dtypes=True).then_inc(s["iota_made"], 1)
            nc.gpsimd.iota(limit, pattern=[[NT, T]], base=NT, channel_multiplier=0,
                           allow_small_or_imprecise_dtypes=True).then_inc(s["iota_made"], 1)
            with pool.Fori(0, A_STEPS) as i:
                for u in range(SLOTS):
                    pool.wait_ge(a["xn_made"][u], i + 1)
                    grp = xs[:, bass.ds((i * SLOTS + u) * GROUP, GROUP), :]
                    nc.gpsimd.tensor_copy(grp[:, :, 0:C], xn[:, u]).then_inc(a["rows_kept"][u], 1)
                for v in range(GROUP * SLOTS):
                    u = v % SLOTS
                    pool.wait_ge(a["evacuated"][u], i * GROUP + v // SLOTS + 1)
                    nc.gpsimd.tensor_copy(xnT[:, :, bass.ds((i * GROUP * SLOTS + v) * NT, NT)],
                                          xT[:, u]).then_inc(a["kept"][u], 1)

            for u in range(SLOTS):
                pool.wait_ge(a["rows_stored"][u], 32 * A_STEPS)
                pool.wait_ge(a["turned"][u], PER_SLOT)
                pool.wait_ge(a["high_made"][u], A_STEPS)
                pool.wait_ge(a["low_made"][u], A_STEPS)
            pool.wait_ge(s["src_copied"], NB)
            nc.gpsimd.memset(ring[:, :, 2 * C:ROW], 1.0).then_inc(s["ring_ones"], 1)
            with pool.Fori(0, CHUNKS // H) as i:
                for h in range(H):
                    pool.wait_ge(s["slots_freed"], i * H + h + 1)
                    nc.gpsimd.tensor_copy(idx[:, h * G:(h + 1) * G], srcT[:, bass.ds(i * RING + h * G, G)]
                                          ).then_inc(s["idx_copied"], 1)
                    pool.wait_ge(s["ring_ones"], 1)
                    pool.wait_ge(s["idx_copied"], i * H + h + 1)
                    for g in range(G):
                        k = h * G + g
                        nc.gpsimd.indirect_dma_start(
                            ring[:, k, 0:2 * C], None, gather_rows,
                            bass.IndirectOffsetOnAxis(idx[:, k:k + 1], 0)).then_inc(landed[h], 16)

        @block.tensor
        def _(pe):
            mm = nc.tensor.matmul
            pe.wait_ge(s["ident_made"], 4)
            pe.wait_ge(s["weights_in"], WEIGHTS_IN)
            for w in range(3):
                for h in range(HALVES):
                    for k in range(HALVES):
                        last = pe.transpose(ps_wide[:, w, k * C + h * 128:k * C + h * 128 + 128],
                                            w_nat[:, w, h, k * 128:(k + 1) * 128], ident[:])
                last.then_inc(s["nat_turned"], 1)
            pe.transpose(ps_wide[:, 3, 0:VEC], vec_rows[:], ident[0:VEC, 0:VEC]).then_inc(s["vec_turned"], 1)
            mm(ps_agg[:, 0, 0:512], ones[0:1, :], bc_row[:, 0:512], start=True, stop=True)
            mm(ps_agg[:, 1, 0:512], ones[0:1, :], bc_row[:, 512:1024], start=True, stop=True)
            mm(ps_hm[:, 0:EXPERTS], ones[0:1, :], bc_row[:, 1024:BC], start=True, stop=True).then_inc(s["bc_spread"], 1)
            pe.wait_ge(s["under_reduced"], 1)
            pe.wait_ge(s["bc_made"], 2)
            mm(ps_hm[0:1, 128:128 + T], ones[:, 0:1], n_under, start=True, stop=True)
            mm(ps_hm[0:T, 0:1], n_under, ones[:, 0:1], start=True, stop=True).then_inc(s["cuts_summed"], 1)
            pe.wait_ge(s["begun_made"], 1)
            mm(ps_hm[:, 256:256 + CHUNKS], ones[0:T, :], begun, start=True, stop=True).then_inc(s["begun_summed"], 1)
            pe.wait_ge(s["edges_float"], 2)
            pe.wait_ge(s["cuts_made"], 1)
            for blk in range(NB):
                if blk:
                    pe.wait_ge(s["src_copied"], blk)
                pe.transpose(ps_turn[:, 0:128], edge_f[:, 0, blk, :], ident[:]).then_inc(s["src_turned"], 1)
                if blk:
                    pe.wait_ge(s["dst_copied"], blk)
                pe.transpose(ps_hm[:, 0:128], edge_f[:, 1, blk, :], ident[:]).then_inc(s["dst_turned"], 1)

            pe.sem_inc(s["slots_freed"], H)
            pe.wait_ge(s["nat_copied"], 3)
            pe.wait_ge(s["vec_made"], 1)
            with pe.Fori(0, A_STEPS) as i:
                for v in range(GROUP * SLOTS + 1):
                    if v < GROUP * SLOTS:
                        u, t = v % SLOTS, v // SLOTS
                        if v % GROUP == 0:
                            pe.wait_ge(a["xn_made"][v // GROUP], i + 1)
                        pe.wait_ge(a["evacuated"][u], i * GROUP + t)
                        for h in range(HALVES):
                            last = pe.transpose(ps_wide[:, u, h * NT:(h + 1) * NT],
                                                xn[:, v // GROUP, v % GROUP, h * 128:(h + 1) * 128],
                                                ident[0:NT, 0:NT])
                        last.then_inc(a["turned"][u], 1)
                    if v:
                        u, t = (v - 1) % SLOTS, (v - 1) // SLOTS
                        pe.wait_ge(a["evacuated"][u], i * GROUP + t + 1)
                        pe.wait_ge(a["k_stored"][u], i * GROUP + t)
                        kk = ps_wide[0:NT, 2 + u, 0:C]
                        mm(kk, ones[0:1, 0:NT], bk_row[:], start=True, stop=False)
                        for h in range(HALVES):
                            last = mm(kk, xT[:, u, h, :], wk[:, h, :], start=False, stop=(h == HALVES - 1))
                        last.then_inc(a["k_summed"][u], 1)

            pe.wait_ge(s["kmax_merged"], A_STEPS + 1)
            pe.wait_ge(s["src_copied"], NB)
            pe.wait_ge(s["dst_copied"], NB)
            for h in range(HALVES):
                last = pe.transpose(ps_turn[:, h * NT:(h + 1) * NT], kmax[:, h * 128:(h + 1) * 128], ident[0:NT, 0:NT])
            last.then_inc(s["kmax_turned"], 1)
            pe.wait_ge(s["kmax_col_wide"], 1)
            for h in range(HALVES):
                last = mm(ps_hm[0:NT, h * 128:(h + 1) * 128], wide[:, h, :], ident[:], start=True, stop=True)
            last.then_inc(s["kmax_spread"], 1)
            for h in range(HALVES):
                mm(ps_agg[:, h, 0:C + 1], zero16[:, 0:128], zero16[:, 0:C + 1], start=True, stop=False,
                   skip_group_check=True)
            pe.wait_ge(s["xs_ones"], 1)
            for u in range(SLOTS):
                pe.wait_ge(a["rows_kept"][u], A_STEPS)
            with pe.Fori(0, B_STEPS) as i:
                for u in range(SLOTS):
                    pe.wait_ge(b["exp_made"][u], i + 1)
                    for h in range(HALVES):
                        last = mm(ps_agg[:, h, 0:C + 1], ek[:, u, h * 128:(h + 1) * 128],
                                  xs[:, bass.ds(i * SLOTS + u, 1), :].squeeze(1),
                                  start=False, stop=False, skip_group_check=True)
                    last.then_inc(b["lam_added"][u], 1)
            pe.wait_ge(s["lam_n_made"], 1)
            for k in range(HALVES):
                for h in range(HALVES):
                    last = pe.transpose(ps_turn[:, k * C + h * 128:k * C + (h + 1) * 128],
                                        lam_n[:, h, k * 128:(k + 1) * 128], ident[:])
            last.then_inc(s["lam_turned"], 1)
            pe.wait_ge(s["lam_nT_made"], 1)
            for h in range(HALVES):
                for k in range(HALVES):
                    last = mm(ps_wide[:, h, 0:C], lam_nT[:, k, h * 128:(h + 1) * 128], wv[:, k, :], start=(k == 0),
                              stop=(k == HALVES - 1))
            last.then_inc(s["lam_v"], 1)
            pe.wait_ge(s["lam_done"], 1)
            for k in range(HALVES):
                for h in range(HALVES):
                    last = mm(ps_wide[:, k, 0:C], wqT[:, h, k * 128:(k + 1) * 128], lam[:, h, :], start=(h == 0),
                              stop=(h == HALVES - 1))
            last.then_inc(s["wmix_done"], 1)
            for h in range(HALVES):
                last = mm(ps_wide[0:NT, 2, 0:C], wide[:, h, :], lam[:, h, :], start=(h == 0), stop=(h == HALVES - 1))
            last.then_inc(s["bmix_spread"], 1)
            pe.wait_ge(s["wmix_made"], 1)
            pe.wait_ge(s["bmix_made"], 1)

            nn, cut, bank, place = (pe.alloc_register(f"pe_{q}") for q in ("tile", "cut", "bank", "place"))
            pe.reg_mov(place, 0)
            pe.wait_ge(s["cuts_made"], 1)
            pe.wait_ge(s["ffn_in"], FFN_IN)
            pe.reg_mov(nn, 0)
            pe.reg_mov(bank, 0)
            pe.reg_load(cut, cuts[0:1, 0:1])
            sums = ps_agg.rearrange("p b c -> p (b c)")

            def clear(bank_v):
                return mm(sums[0:NT, bass.ds(bank_v, C + 1)], zero16[:, 0:NT], zero16[:, 0:C + 1],
                          start=True, stop=False, skip_group_check=True)

            def add_chunk(h, onehot, bank_v):
                for g in range(G):
                    w = onehot[:, g, 0:NT]
                    m = mm(sums[0:NT, bass.ds(bank_v, C)], w, ring[:, h * G + g, 0:C], start=False, stop=False,
                           skip_group_check=True)
                    last = mm(sums[0:NT, bass.ds(bank_v, C + 1)], w, ring[:, h * G + g, C:2 * C + 1], start=False,
                              stop=False, skip_group_check=True)
                return last

            def stage2_l1(v, prev):
                pe.wait_ge(s["both_made"], v)
                pe.wait_ge(s["sh1_made"], prev)
                for h in range(HALVES):
                    last = mm(ps_turn[0:NT, 500:500 + EXPERTS], x2T[:, h, :], gw[:, h, :], start=(h == 0), stop=(h == 1))
                last.then_inc(s["logits_done"], 1)
                for o in range(2):
                    for h in range(HALVES):
                        last = mm(ps_l1[:, 0, o * NT:(o + 1) * NT], s1w[:, h, o * 128:(o + 1) * 128], x2T[:, h, :],
                                  start=(h == 0), stop=(h == 1))
                last.then_inc(s["l1s_done"], 1)
                pe.wait_ge(s["eh1_made"], prev)
                for e in range(EXPERTS):
                    for h in range(HALVES):
                        last = mm(ps_l1[:, 1, e * NT:(e + 1) * NT], e1w[:, h, e, :], x2T[:, h, :],
                                  start=(h == 0), stop=(h == 1))
                last.then_inc(s["l1e_done"], 1)

            def stage2_l2(v, prev):
                pe.wait_ge(s["gate_made"], v)
                pe.transpose(ps_turn[0:EXPERTS + 1, 0:NT], gate5[:], ident[0:NT, 0:NT]).then_inc(s["gate_turned"], 1)
                pe.wait_ge(s["sh1_made"], v)
                for h in range(2):
                    last = mm(ps_l2[:, 0:NT], s2w[:, h, :], sh1[:, h, :], start=(h == 0), stop=(h == 1))
                pe.wait_ge(s["eh1_made"], v)
                for e in range(EXPERTS):
                    q = 64 * (e % 2)
                    c0 = NT * (1 + e // 2)
                    last = mm(ps_l2[q:q + 64, c0:c0 + NT], e2w[:, e, :], eh1[:, e, :], start=True, stop=True)
                last.then_inc(s["l2_done"], 1)
                pe.wait_ge(s["gateT_made"], v)
                pe.wait_ge(s["y_made"], prev)
                for r in range(2):
                    last = mm(ps_l3[:, C + r * NT:C + (r + 1) * NT], pick[:, r, :], gateT, start=True, stop=True)
                last.then_inc(s["gates_spread"], 1)

            def stage2_l3(v):
                o = ps_l3[0:NT, 0:C]
                pe.wait_ge(s["sh2_made"], v)
                pe.wait_ge(s["eh2g_made"], v)
                mm(o, gateT, b35, start=True, stop=False)
                mm(o, sh2, s3w, start=False, stop=False)
                for r in range(2):
                    last = mm(o, eh2g[:, r, :], e3w[:, r, :], start=False, stop=(r == 1))
                last.then_inc(s["l3_done"], 1)

            def turn_x2(v, prev):
                pe.wait_ge(s["x2_made"], v)
                pe.wait_ge(s["gateT_made"], prev)
                for h in range(HALVES):
                    last = pe.transpose(ps_turn[:, (2 + h) * NT:(3 + h) * NT], x2[:, h * 128:(h + 1) * 128],
                                        ident[0:NT, 0:NT])
                return last

            def node_tile(v, prev, h_c, bank_w):
                pe.wait_ge(s["hot_next_built"], v)
                add_chunk(h_c, hot_next, bank_w).then_inc(s["next_summed"], 1)
                pe.wait_ge(s["agg_scaled"], v)
                pe.wait_ge(s["gateT_made"], prev)
                for h in range(HALVES):
                    pe.transpose(ps_turn[:, h * NT:(h + 1) * NT], agg_mean[:, h * 128:(h + 1) * 128],
                                 ident[0:NT, 0:NT])
                turn_x2(v, prev).then_inc(s["both_turned"], 1)
                pe.wait_ge(s["xTc_made"], v)
                pe.wait_ge(s["h_made"], prev)
                for h in range(HALVES):
                    mm(ps_hm[0:NT, 0:C], xTc[:, h, :], wrT[:, h, :], start=(h == 0), stop=False)
                stage2_l1(v, prev)
                for h in range(HALVES):
                    last = mm(ps_hm[0:NT, 0:C], aggT[:, h, :], wlT[:, h, :], start=False, stop=(h == 1))
                last.then_inc(s["gnn_done"], 1)
                stage2_l2(v, prev)
                pe.wait_ge(s["x1_made"], prev)
                for h in range(HALVES):
                    last = mm(ps_mix, xTc[:, h, :], wmix[:, h, :], start=(h == 0), stop=(h == 1))
                last.then_inc(s["mix_done"], 1)
                stage2_l3(v)

            clear(0)
            with pe.Fori(0, CHUNKS // H) as i:
                for h in range(H):
                    bank_v = pe.snap(bank, min_val=0, max_val=512)
                    pe.wait_ge(landed[h], (i + 1) * (16 * G))
                    pe.wait_ge(s["hot_built"], i * H + h + 1)
                    place_v = pe.snap(place, min_val=0, max_val=(HOTS - 1) * G * 128)
                    add_chunk(h, hot_all[:, bass.ds(place_v, G * 128)].rearrange("p (g n) -> p g n", g=G), bank_v)
                    pe.reg_add(place, place, G * 128)
                    pe.reg_mod(place, place, HOTS * G * 128)
                    with pe.While(lambda: pe.snap(cut, min_val=-1, max_val=CHUNKS) == i * H + h):
                        prev = pe.snap(nn, min_val=0, max_val=T - 1)
                        v = pe.snap(prev + 1, min_val=1, max_val=T)
                        pe.reg_sub(bank, 512, bank)
                        bank_w = pe.snap(bank, min_val=0, max_val=512)
                        pe.wait_ge(s["agg_scaled"], prev)
                        pe.wait_ge(s["deg_read"], prev)
                        clear(bank_w).then_inc(s["tile_summed"], 1)
                        node_tile(v, prev, h, bank_w)
                        pe.reg_load(cut, cuts[0:1, bass.ds(v, 1)])
                        pe.reg_add(nn, nn, 1)
                    mm(sums[0:1, bass.ds(pe.snap(bank, min_val=0, max_val=512) + C + 2, 1)], zero16[:, 0:1],
                       zero16[:, 0:1], start=False, stop=False, skip_group_check=True).then_inc(s["slots_freed"], 1)
            turn_x2(T + 1, T).then_inc(s["both_turned"], 1)
            stage2_l1(T + 1, T)
            stage2_l2(T + 1, T)
            stage2_l3(T + 1)

        v2 = nc.vector
        op = v2.tensor_tensor

        @block.vector
        def _(dve):
            dve.wait_ge(s["edges_in"], EDGES_IN)
            v2.tensor_copy(edge_f[:, 1], edge_i[:, 1]).then_inc(s["edges_float"], 1)
            v2.tensor_copy(edge_f[:, 0], edge_i[:, 0]).then_inc(s["edges_float"], 1)
            v2.memset(cuts[:], -1).then_inc(s["cuts_clean"], 1)
            dve.wait_ge(s["ident_made"], 4)
            v2.tensor_reduce(keep, ident.rearrange("p (k g) -> p g k", g=G)[:, G - 1, :], AX.X, ALU.add
                             ).then_inc(s["keep_made"], 1)
            dve.wait_ge(s["keep_made"], 1)
            v2.tensor_scalar(keep, keep, -NO_NODE, NO_NODE, ALU.mult, ALU.add).then_inc(s["keep_neg"], 1)
            dve.wait_ge(s["keep_neg"], 1)
            dve.wait_ge(s["edges_float"], 1)
            v2.tensor_scalar(row_end, edge_f[:, 1, :, EB - 1], keep, None, ALU.max).then_inc(s["row_end_made"], 1)
            dve.wait_ge(s["row_end_made"], 1)
            dve.wait_ge(s["iota_made"], 5)
            op(under, row_end.unsqueeze(1).broadcast_to([128, T, NB]), limit.unsqueeze(2).broadcast_to([128, T, NB]),
               ALU.is_lt).then_inc(s["under_made"], 1)
            dve.wait_ge(s["under_made"], 1)
            v2.tensor_reduce(n_under, under, AX.X, ALU.add).then_inc(s["under_reduced"], 1)
            dve.wait_ge(s["vec_turned"], 1)
            v2.tensor_copy(vec[:], ps_wide[:, 3, 0:VEC]).then_inc(s["vec_made"], 1)
            dve.wait_ge(s["bc_spread"], 1)
            v2.tensor_copy(bc[:, 0:4 * C].rearrange("p (b c) -> p b c", b=2), ps_agg[:]).then_inc(s["bc_made"], 1)
            v2.tensor_copy(bc[:, 4 * C:BC], ps_hm[:, 0:EXPERTS]).then_inc(s["bc_made"], 1)
            dve.wait_ge(s["cuts_summed"], 1)
            dve.wait_ge(s["cuts_clean"], 1)
            v2.tensor_copy(cuts[:, 0:T], ps_hm[0:1, 128:128 + T]).then_inc(s["cuts_made"], 1)
            v2.tensor_copy(cut_col, ps_hm[0:T, 0:1]).then_inc(s["cut_col_made"], 1)
            dve.wait_ge(s["cut_col_made"], 1)
            v2.tensor_scalar(begun, chunk_no, cut_col, float(NT), ALU.is_gt, ALU.mult).then_inc(s["begun_made"], 1)
            for blk in range(NB):
                n = min(128, J - blk * 128)
                dve.wait_ge(s["src_turned"], blk + 1)
                v2.tensor_copy(srcT[:, blk * 128:blk * 128 + n], ps_turn[:, 0:n]).then_inc(s["src_copied"], 1)
            dve.wait_ge(s["begun_summed"], 1)
            dve.wait_ge(s["dst_copied"], NB)
            v2.tensor_copy(begun_all, ps_hm[:, 256:256 + CHUNKS]).then_inc(s["begun_copied"], 1)
            dve.wait_ge(s["begun_copied"], 1)
            by_chunk = dst_in[:, 0:J].rearrange("p (c g) -> p c g", g=G)
            op(by_chunk, by_chunk, begun_all.unsqueeze(2).broadcast_to([128, CHUNKS, G]), ALU.subtract
               ).then_inc(s["dst_shifted"], 1)

            var = mv[0:NT, :, :, 1]
            rstd_a = sm[0:NT, 1].rearrange("p (u k) -> p u k", u=SLOTS)

            def stage_a(i):
                for u in range(SLOTS):
                    t0 = (i * SLOTS + u) * GROUP
                    dve.wait_ge(a["x_in"][u], (i + 1) * 32)
                    for k in range(GROUP):
                        last = v2.bn_stats(stats[0:NT, u, k, :], xs[:, bass.ds(t0 + k, 1), 0:C])
                    last.then_inc(a["stats_made"][u], 1)
                    dve.wait_ge(s["iota_made"], 5)
                    dve.wait_ge(a["stats_made"][u], i + 1)
                    for k in range(GROUP):
                        last = v2.bn_aggr(mv[0:NT, u, k, :], stats[0:NT, u, k, :])
                    last.then_inc(a["mv_made"][u], 1)
                for u in range(SLOTS):
                    t0 = (i * SLOTS + u) * GROUP
                    dve.wait_ge(a["rstd_made"][u], i + 1)
                    dve.wait_ge(a["rows_kept"][u], i)
                    dve.wait_ge(a["high_made"][u], i)
                    dve.wait_ge(a["low_made"][u], i)
                    for w in range(SLOTS):
                        dve.wait_ge(a["turned"][w], i * GROUP)
                    for k in range(GROUP):
                        last = v2.tensor_scalar(xn[:, u, k, :], xs[:, bass.ds(t0 + k, 1), 0:C].squeeze(1),
                                                mv[0:NT, u, k, 0:1], rstd_a[:, u, k:k + 1], ALU.subtract, ALU.mult)
                    last.then_inc(a["xn_made"][u], 1)
                for u in range(SLOTS):
                    dve.wait_ge(a["high_made"][u], i + 1)
                    v2.scalar_tensor_tensor(xhl[:, u, :, C:2 * C], xn[:, u], SCALE, xhl[:, u, :, 0:C], ALU.mult,
                                            ALU.subtract).then_inc(a["low_made"][u], 1)

            def k_of_step(i, out_ap):
                for w in range(SLOTS):
                    dve.wait_ge(a["k_stored"][w], (i + 1) * GROUP)
                tiles = kst[:, bass.ds(i * GROUP * SLOTS, GROUP * SLOTS), :]
                return v2.tensor_reduce(out_ap, tiles.rearrange("p t c -> p c t"), AX.X, ALU.max)

            stage_a(0)
            v2.memset(kmax[:], -3.0e38).then_inc(s["kmax_merged"], 1)
            with dve.Fori(1, A_STEPS) as i:
                stage_a(i)
                dve.wait_ge(s["kmax_merged"], i)
                k_of_step(i - 1, kpart[:]).then_inc(s["kpart_made"], 1)
                dve.wait_ge(s["kpart_made"], i)
                op(kmax[:], kmax[:], kpart[:], ALU.max).then_inc(s["kmax_merged"], 1)
            dve.wait_ge(s["kmax_merged"], A_STEPS)
            k_of_step(A_STEPS - 1, kpart[:]).then_inc(s["kpart_made"], 1)
            dve.wait_ge(s["kpart_made"], A_STEPS)
            op(kmax[:], kmax[:], kpart[:], ALU.max).then_inc(s["kmax_merged"], 1)

            for u in range(SLOTS):
                dve.wait_ge(a["rows_kept"][u], A_STEPS)
                dve.wait_ge(a["k_summed"][u], PER_SLOT)
                dve.wait_ge(a["kept"][u], PER_SLOT)
            v2.memset(xs[:, :, C:C + 1], 1.0).then_inc(s["xs_ones"], 1)
            kcol = sm[:, 4, 0:HALVES]
            dve.wait_ge(s["kmax_turned"], 1)
            v2.tensor_reduce(kcol, ps_turn[:, 0:HALVES * NT].rearrange("p (h n) -> p h n", h=HALVES), AX.X, ALU.max
                             ).then_inc(s["kmax_reduced"], 1)
            dve.wait_ge(s["kmax_reduced"], 1)
            for h in range(HALVES):
                last = v2.tensor_scalar(wide[:, h, :], ones[:, 0:NT], kcol[:, h:h + 1], None, ALU.mult)
            last.then_inc(s["kmax_col_wide"], 1)
            dve.wait_ge(s["kmax_spread"], 1)
            v2.tensor_copy(kmax[:], ps_hm[0:NT, 0:C]).then_inc(s["kmax_made"], 1)
            dve.wait_ge(s["kmax_made"], 1)
            with dve.Fori(0, B_STEPS) as i:
                for u in range(SLOTS):
                    k_t = kst[:, bass.ds(i * SLOTS + u, 1), :].squeeze(1)
                    op(k_t, k_t, kmax[:], ALU.subtract).then_inc(b["k_shifted"][u], 1)

            links = [0]

            def link(ins):
                links[0] += 1
                ins.then_inc(s["lam_link"], 1)
                dve.wait_ge(s["lam_link"], links[0])

            for u in range(SLOTS):
                dve.wait_ge(b["lam_added"][u], B_STEPS)
            den, st, mvl = sm[:, 4, 2:4], stats[:, 0, 0:2, :], mv[:, 0, 0:2, :]
            guess_b, rstd_b = (sm[:, 5, 2 * q:2 * q + 2] for q in (1, 2))
            link(v2.reciprocal(den, ps_agg[:, :, C]))
            for h in range(HALVES):
                last = v2.tensor_scalar(lam_n[:, h, :], ps_agg[:, h, 0:C], den[:, h:h + 1], None, ALU.mult)
            last.then_inc(s["lam_n_made"], 1)
            dve.wait_ge(s["lam_turned"], 1)
            v2.tensor_copy(lam_nT, ps_turn[:].rearrange("p (k c) -> p k c", k=HALVES)).then_inc(s["lam_nT_made"], 1)
            dve.wait_ge(s["lam_v"], 1)
            for h in range(HALVES):
                link(op(lam[:, h, :], ps_wide[:, h, 0:C], bv_b, ALU.add))
                link(v2.bn_stats(st[:, h, :], lam[:, h, :]))
                v2.bn_aggr(mvl[:, h, :], st[:, h, :]).then_inc(s["lam_ln"], 1)
            dve.wait_ge(s["lam_guess"], 1)
            link(op(rstd_b, guess_b, vec[:, V_GM:V_GM + 2], ALU.mult))
            for h in range(HALVES):
                v2.tensor_scalar(wide[:, h, :], ones[:, 0:NT], vec[:, V_BQ + h:V_BQ + h + 1], None, ALU.mult)
                link(v2.tensor_scalar(lam[:, h, :], lam[:, h, :], mvl[:, h, 0:1], rstd_b[:, h:h + 1], ALU.subtract,
                                      ALU.mult))
                link(v2.tensor_scalar(lam[:, h, :], lam[:, h, :], vec[:, V_BM + h:V_BM + h + 1], None, ALU.add))
            dve.sem_inc(s["lam_done"], 1)
            dve.wait_ge(s["bmix_spread"], 1)
            v2.tensor_copy(bmix, ps_wide[0:NT, 2, 0:C]).then_inc(s["bmix_made"], 1)
            dve.wait_ge(s["wmix_done"], 1)
            for h in range(HALVES):
                o = h * 128
                op(wmix[:, h, o:o + 128], ps_wide[:, h, o:o + 128], ident[:], ALU.add)
                last = v2.tensor_copy(wmix[:, h, 128 - o:256 - o], ps_wide[:, h, 128 - o:256 - o])
            last.then_inc(s["wmix_made"], 1)

            v2.memset(x1, 0.0).then_inc(s["x2_zeroed"], 1)
            v2.memset(gate5, 1.0).then_inc(s["x2_zeroed"], 1)
            v2.memset(x2, 0.0).then_inc(s["x2_made"], 1)
            dve.wait_ge(s["dst_shifted"], 1)
            dve.wait_ge(s["x2_zeroed"], 2)
            dve.wait_ge(s["x2_made"], 1)
            dve.wait_ge(s["bmix_made"], 1)
            sums = ps_agg.rearrange("p b c -> p (b c)")

            def one_hot(to, rel):
                return op(to[:, :, 0:NT], iota[:].unsqueeze(1).broadcast_to([128, to.shape[1], NT]),
                          rel.unsqueeze(2).broadcast_to([128, to.shape[1], NT]), ALU.is_equal)

            def build_up_to(end):
                with dve.While(lambda: dve.snap(built, min_val=0, max_val=CHUNKS + HOTS) < end):
                    c = dve.snap(built, min_val=0, max_val=CHUNKS + HOTS - 2)
                    at = dve.snap(place, min_val=0, max_val=(HOTS - 2) * G * 128)
                    dve.wait_ge(s["slots_freed"], c + (2 + H - HOTS))
                    one_hot(hot_all[:, bass.ds(at, 2 * G * 128)].rearrange("p (g n) -> p g n", g=2 * G),
                            dst_in[:, bass.ds(c * G, 2 * G)]).then_inc(s["hot_built"], 2)
                    dve.reg_add(built, built, 2)
                    dve.reg_add(place, place, 2 * G * 128)
                    dve.reg_mod(place, place, HOTS * G * 128)

            def one_hot_next(c, tiles, v, prev):
                dve.wait_ge(s["next_summed"], prev)
                v2.tensor_scalar(dst_rel_next, dst_in[:, bass.ds(c * G, G)], tile_base[:, bass.ds(tiles, 1)], None,
                                 ALU.add).then_inc(s["rel_next_made"], 1)
                dve.wait_ge(s["rel_next_made"], v)
                one_hot(hot_next, dst_rel_next).then_inc(s["hot_next_built"], 1)

            done = [0]

            def after(base, ins):
                done[0] += 1
                ins.then_inc(s["dve_link"], 1)
                dve.wait_ge(s["dve_link"], base + done[0])

            def gates(v, prev, base):
                dve.wait_ge(s["logits_done"], v)
                op(lg, ps_turn[0:NT, 500:500 + EXPERTS], gb_b, ALU.add).then_inc(s["lg_made"], 1)
                dve.wait_ge(s["lg_made"], v)
                after(base, v2.tensor_reduce(lmax, lg, AX.X, ALU.max))
                v2.tensor_scalar(lg, lg, lmax, None, ALU.subtract).then_inc(s["lg_shifted"], 1)
                dve.wait_ge(s["lg_exp"], v)
                after(base, v2.reciprocal(rsum, esum))
                after(base, v2.tensor_scalar(gt, ex, rsum, None, ALU.mult))
                v2.tensor_scalar(ez, gt, rsum, None, ALU.subtract).then_inc(s["z_made"], 1)
                g_e = gt.unsqueeze(2).broadcast_to([NT, EXPERTS, EXPERTS])
                g_f = gt.unsqueeze(1).broadcast_to([NT, EXPERTS, EXPERTS])
                op(gt_m, g_f, g_e, ALU.is_gt)
                after(base, op(eq_m, g_f, g_e, ALU.is_equal))
                after(base, op(eq_m, eq_m, lower[:], ALU.mult))
                after(base, op(gt_m, gt_m, eq_m, ALU.add))
                after(base, v2.tensor_reduce(rank, gt_m, AX.X, ALU.add))
                dve.wait_ge(s["z_exp"], v)
                after(base, v2.scalar_tensor_tensor(ez, rank, float(TOPK), ez, ALU.is_lt, ALU.mult, accum_out=wsum))
                after(base, v2.reciprocal(rw, wsum))
                dve.wait_ge(s["gate_turned"], prev)
                v2.tensor_scalar(gate5[:, 0:EXPERTS], ez, rw, None, ALU.mult).then_inc(s["gate_made"], 1)

            def stage2_weigh(v, prev):
                dve.wait_ge(s["eh2_made"], v)
                dve.wait_ge(s["gates_spread"], v)
                dve.wait_ge(s["l3_done"], prev)
                op(eh2g, ps_l3[:, C:C + 2 * NT].rearrange("p (h n) -> p h n", h=2), eh2, ALU.mult
                   ).then_inc(s["eh2g_made"], 1)

            def stage2_out(v, prev):
                dve.wait_ge(s["l3_done"], v)
                dve.wait_ge(s["y_stored"], prev * 32)
                op(y, ps_l3[0:NT, 0:C], x1, ALU.add).then_inc(s["y_made"], 1)

            def node_tile(i, u, v, prev, c):
                done[0] = 0
                base = dve.snap(prev * DVE_LINKS, min_val=0, max_val=T * DVE_LINKS)
                dve.wait_ge(s["tile_summed"], v)
                dve.wait_ge(s["agg_scaled"], prev)
                v2.tensor_scalar(deg, ps_agg[0:NT, u, C:C + 1], 1.0, SCALE, ALU.max, ALU.mult
                                 ).then_inc(s["deg_read"], 1)
                dve.wait_ge(s["deg_read"], v)
                v2.reciprocal(rc, deg).then_inc(s["rc_made"], 1)
                build_up_to(c + HOTS - 1)
                gates(v, prev, base)
                dve.wait_ge(s["gnn_done"], v)
                op(hh, ps_hm[0:NT, 0:C], bl_b[0:NT], ALU.add).then_inc(s["h_made"], 1)
                dve.wait_ge(s["h_made"], v)
                v2.bn_stats(st1, hh).then_inc(s["st1_made"], 1)
                dve.wait_ge(s["x2_zeroed"], 2)
                dve.wait_ge(s["st1_made"], v)
                v2.bn_aggr(mv1, st1).then_inc(s["mv1_made"], 1)
                dve.wait_ge(s["mv1_made"], v)
                stage2_weigh(v, prev)
                after(base, v2.scalar_tensor_tensor(hn, hh, mv1[:, 0:1], gg_b[0:NT], ALU.subtract, ALU.mult))
                dve.wait_ge(s["rs1_made"], v)
                after(base, v2.scalar_tensor_tensor(hn, hn, rs1, bg_b[0:NT], ALU.mult, ALU.add))
                dve.reg_mov(last_cut, cut)
                dve.reg_load(cut, cuts[0:1, bass.ds(v, 1)])
                dve.reg_alu(last_cut, last_cut, cut, ALU.is_equal)
                dve.reg_mul(on, on, last_cut)
                dve.reg_add(on, on, 1)
                stage2_out(v, prev)
                dve.wait_ge(s["y_made"], v)
                dve.wait_ge(x_row_in[u], (i + 1) * 32)
                v2.scalar_tensor_tensor(x1, hn, 0.0, x_rows[:, u, :], ALU.max, ALU.add
                                        ).then_inc(s["x_row_used"], 1)
                dve.wait_ge(s["x_row_used"], v)
                dve.wait_ge(s["mix_done"], v)
                after(base, op(x1, ps_mix, x1, ALU.add))
                op(x1, x1, bmix, ALU.add).then_inc(s["x1_made"], 1)
                dve.wait_ge(s["x1_made"], v)
                v2.bn_stats(st2, x1).then_inc(s["st2_made"], 1)
                dve.wait_ge(s["x2_zeroed"], 2)
                dve.wait_ge(s["st2_made"], v)
                v2.bn_aggr(mv2, st2).then_inc(s["mv2_made"], 1)
                dve.wait_ge(s["rs2_made"], v)
                dve.wait_ge(s["both_turned"], v)
                v2.tensor_scalar(x2, x1, mv2[:, 0:1], rs2, ALU.subtract, ALU.mult).then_inc(s["x2_made"], 1)
                assert done[0] == DVE_LINKS, done

            cut, last_cut, on, built, place = (dve.alloc_register(f"dve_{q}") for q in (
                "cut", "last_cut", "on", "built", "place"))
            dve.reg_mov(built, 0)
            dve.reg_mov(place, 0)
            dve.reg_mov(on, 1)
            dve.wait_ge(s["cuts_made"], 1)
            dve.reg_load(cut, cuts[0:1, 0:1])
            with dve.Fori(0, T // 2) as i:
                for u in range(2):
                    prev = dve.snap(i * 2 + u, min_val=0, max_val=T - 1)
                    v = dve.snap(i * 2 + u + 1, min_val=1, max_val=T)
                    c = dve.snap(cut, min_val=0, max_val=CHUNKS - 1)
                    build_up_to(c + 1)
                    one_hot_next(c, dve.snap(on, min_val=1, max_val=T), v, prev)
                    node_tile(i, u, v, prev, c)
            v = T + 1
            done[0] = 0
            gates(v, T, T * DVE_LINKS)
            stage2_weigh(v, T)
            stage2_out(v, T)

        @block.scalar
        def _(act):
            f = nc.scalar.activation
            act.preload_act_table_set("natural_log_exp_and_others")
            for w, to in enumerate((wlT, wrT, wqT)):
                act.wait_ge(s["nat_turned"], w + 1)
                f(to[:], ps_wide[:, w, :].rearrange("p (k c) -> p k c", k=HALVES), ACT.Copy).then_inc(s["nat_copied"], 1)
            for blk in range(NB):
                n = min(128, J - blk * 128)
                act.wait_ge(s["dst_turned"], blk + 1)
                f(dst_in[:, blk * 128:blk * 128 + n], ps_hm[:, 0:n], ACT.Copy).then_inc(s["dst_copied"], 1)

            act.wait_ge(s["dst_shifted"], 1)
            var = mv[0:NT, :, :, 1]
            ln_a, rstd_a = (sm[0:NT, q].rearrange("p (u k) -> p u k", u=SLOTS) for q in range(2))
            act.wait_ge(s["consts_made"], 3)
            with act.Fori(0, A_STEPS) as i:
                for u in range(SLOTS):
                    act.wait_ge(a["mv_made"][u], i + 1)
                    f(ln_a[:, u], var[:, u], ACT.Ln, bias=eps[0:NT]).then_inc(a["ln_made"][u], 1)
                    act.wait_ge(a["ln_made"][u], i + 1)
                    act.wait_ge(a["xn_made"][u], i)
                    f(rstd_a[:, u], ln_a[:, u], ACT.Exp, scale=-0.5).then_inc(a["rstd_made"][u], 1)
                for v in range(GROUP * SLOTS + 1):
                    if v < GROUP * SLOTS:
                        u, t = v % SLOTS, v // SLOTS
                        if v % GROUP == 0:
                            g = v // GROUP
                            act.wait_ge(a["xn_made"][g], i + 1)
                            act.wait_ge(a["rows_stored"][g], i * 32)
                            f(xhl[:, g, :, 0:C], xn[:, g], ACT.Copy, scale=SCALE).then_inc(a["high_made"][g], 1)
                        act.wait_ge(a["turned"][u], i * GROUP + t + 1)
                        act.wait_ge(a["kept"][u], i * GROUP + t)
                        act.wait_ge(a["k_summed"][u], i * GROUP + t)
                        f(xT[:, u], ps_wide[:, u, 0:HALVES * NT].rearrange("p (h n) -> p h n", h=HALVES), ACT.Copy
                          ).then_inc(a["evacuated"][u], 1)
                    if v:
                        u, t = (v - 1) % SLOTS, (v - 1) // SLOTS
                        act.wait_ge(a["k_summed"][u], i * GROUP + t + 1)
                        f(kst[:, bass.ds(i * GROUP * SLOTS + v - 1, 1), :].squeeze(1), ps_wide[0:NT, 2 + u, 0:C],
                          ACT.Copy).then_inc(a["k_stored"][u], 1)

            with act.Fori(0, B_STEPS) as i:
                for u in range(SLOTS):
                    act.wait_ge(b["k_shifted"][u], i + 1)
                    act.wait_ge(b["lam_added"][u], i)
                    f(ek[:, u, :], kst[:, bass.ds(i * SLOTS + u, 1), :].squeeze(1), ACT.Exp
                      ).then_inc(b["exp_made"][u], 1)
            ln_b, guess_b = (sm[:, 5, 2 * q:2 * q + 2] for q in range(2))
            act.wait_ge(s["lam_ln"], 2)
            f(ln_b, mv[:, 0, 0:2, 1], ACT.Ln, bias=eps[:]).then_inc(s["lam_ln"], 1)
            act.wait_ge(s["lam_ln"], 3)
            f(guess_b, ln_b, ACT.Exp, scale=-0.5).then_inc(s["lam_guess"], 1)
            act.wait_ge(s["bmix_made"], 1)

            def rsqrt(v, variance, ln, to, ready, ln_made, made):
                act.wait_ge(ready, v)
                f(ln, variance, ACT.Ln, bias=eps[0:NT]).then_inc(ln_made, 1)
                act.wait_ge(ln_made, v)
                f(to, ln, ACT.Exp, scale=-0.5).then_inc(made, 1)

            def stage2_exps(v):
                act.wait_ge(s["lg_shifted"], v)
                f(ex, lg, ACT.Exp, accum_out=esum).then_inc(s["lg_exp"], 1)
                act.wait_ge(s["l1s_done"], v)
                act.wait_ge(s["l2_done"], v - 1)
                for o in range(2):
                    last = f(sh1[:, o, :], ps_l1[:, 0, o * NT:(o + 1) * NT], ACT.Relu, bias=vec[:, V_SB1 + o:V_SB1 + o + 1])
                last.then_inc(s["sh1_made"], 1)
                act.wait_ge(s["z_made"], v)
                f(ez, ez, ACT.Exp).then_inc(s["z_exp"], 1)
                act.wait_ge(s["l1e_done"], v)
                for e in range(EXPERTS):
                    last = f(eh1[:, e, :], ps_l1[:, 1, e * NT:(e + 1) * NT], ACT.Relu, bias=vec[:, V_EB1 + e:V_EB1 + e + 1])
                last.then_inc(s["eh1_made"], 1)
                act.wait_ge(s["gate_turned"], v)
                act.wait_ge(s["l3_done"], v - 1)
                f(gateT, ps_turn[0:EXPERTS + 1, 0:NT], ACT.Copy).then_inc(s["gateT_made"], 1)

            def stage2_relu(v):
                act.wait_ge(s["l2_done"], v)
                act.wait_ge(s["eh2g_made"], v - 1)
                for r in range(2):
                    last = f(eh2[:, r, :], ps_l2[:, (1 + r) * NT:(2 + r) * NT], ACT.Relu,
                             bias=vec[:, V_EB2 + r:V_EB2 + r + 1])
                last.then_inc(s["eh2_made"], 1)
                f(sh2, ps_l2[:, 0:NT], ACT.Relu, bias=vec[:, V_SB2:V_SB2 + 1]).then_inc(s["sh2_made"], 1)

            def turn_back(v):
                act.wait_ge(s["both_turned"], v)
                act.wait_ge(s["l1e_done"], v - 1)
                act.wait_ge(s["gnn_done"], v - 1)
                f(turned, ps_turn[:, 0:4 * NT].rearrange("p (h n) -> p h n", n=NT), ACT.Copy
                  ).then_inc(s["both_made"], 1)

            def store(v):
                act.wait_ge(s["y_made"], v)
                for r0, r1 in ((0, ROWS_A), (ROWS_A, NT)):
                    act.dma_start(tile_rows(out, v - 2, r0, r1), y[r0:r1].unsqueeze(1)).then_inc(s["y_stored"], 16)

            def node_tile(v, bank_v, first=False):
                act.wait_ge(s["mix_done"], v - 1)
                f(xTc, xnT[:, :, bass.ds((v - 1) * NT, NT)], ACT.Copy).then_inc(s["xTc_made"], 1)
                act.wait_ge(s["tile_summed"], v)
                act.wait_ge(s["rc_made"], v)
                act.wait_ge(s["both_turned"], v - 1)
                f(agg_mean, ps_agg[0:NT, bank_v, 0:C], ACT.Copy, scale=rc).then_inc(s["agg_scaled"], 1)
                turn_back(v)
                stage2_exps(v)
                stage2_relu(v)
                rsqrt(v, mv1[:, 1:2], lv1, rs1, s["mv1_made"], s["ln1"], s["rs1_made"])
                if first:
                    act.sem_inc(s["y_stored"], 32)
                else:
                    store(v)
                rsqrt(v, mv2[:, 1:2], lv2, rs2, s["mv2_made"], s["ln2"], s["rs2_made"])

            node_tile(1, 0, first=True)
            with act.Fori(0, T // 2 - 1) as i:
                for u in range(2):
                    node_tile(act.snap(i * 2 + 2 + u, min_val=2, max_val=T), 1 - u)
            node_tile(T, (T - 1) % 2)
            v = T + 1
            act.wait_ge(s["both_turned"], v)
            f(x2T, ps_turn[:, 2 * NT:4 * NT].rearrange("p (h n) -> p h n", n=NT), ACT.Copy).then_inc(s["both_made"], 1)
            stage2_exps(v)
            stage2_relu(v)
            store(v)
            act.wait_ge(s["y_stored"], 32 * (T + 1))


_INS = ["x", "src", "dst"] + [f"L0_gnn_{n}" for n in ("W_l", "b_l", "W_r", "gamma", "beta")] + \
       [f"L0_mix_{n}" for n in ("W_qk", "b_qk", "W_v", "b_v", "gamma", "beta")] + \
       [f"L0_ffn_{n}" for n in ("sW1", "sb1", "sW2", "sb2", "sW3", "sb3", "eW1", "eb1", "eW2", "eb2", "eW3", "eb3",
                                "gW", "gb")]


def kernel(**inputs):
    import numpy as _np
    import concourse.bacc as _bacc
    from concourse import mybir as _mybir
    from concourse.bass_utils import run_bass_kernel_spmd as _run

    nc = _bacc.Bacc("TRN2", target_bir_lowering=False, num_devices=1)
    arrays, args = {}, []
    for name in _INS:
        a = _np.ascontiguousarray(inputs[name])
        arrays[f"in_{name}_dram"] = a
        args.append(nc.dram_tensor(f"in_{name}_dram", a.shape, _mybir.dt.from_np(a.dtype), kind="ExternalInput").ap())
    args.append(nc.dram_tensor("out_dram", inputs["x"].shape, F32, kind="ExternalOutput").ap())
    gps_layer(nc, *args)
    r = _run(nc, [arrays], core_ids=[0])
    return r.results[0]["out_dram"]
```

```python
from contextlib import ExitStack

import concourse.bass as bass
from concourse import mybir
from concourse.alu_op_type import AluOpType as ALU

F32 = mybir.dt.float32
F16 = mybir.dt.float16
BF16 = mybir.dt.bfloat16
I32 = mybir.dt.int32
I16 = mybir.dt.int16
ACT = mybir.ActivationFunctionType
AX = mybir.AxisListType

C = 256
HALVES = C // 128
NT = 125
ROWS_A = 112
EB = 128
G = 4
H = 14
RING = G * H
PART = RING // 2
EARLY = 8
HOTS = H
GROUP = 5
SLOTS = 2
SCALE = 1024.0
ROW = 2 * C + 2
EPS = 1e-5
NO_NODE = 30000.0
EXPERTS = 4
TOPK = 2
DVE_LINKS = 18
BK_LINKS = 8


def gps_layer(nc, x, src, dst, W_l, b_l, W_r, gamma_g, beta_g, W_qk, b_qk, W_v, b_v, gamma_m, beta_m,
              sW1, sb1, sW2, sb2, sW3, sb3, eW1, eb1, eW2, eb2, eW3, eb3, gW, gb, out):
    N = x.shape[0]
    E = src.shape[0]
    T = N // NT
    FULL = E // EB
    REST = E - FULL * EB
    CHUNKS = -(-E // (EB * G * H)) * H
    J = CHUNKS * G
    NB = -(-J // 128)
    assert T * NT == N and T % (GROUP * SLOTS) == 0 and C == 256 and N < NO_NODE < 2 ** 15
    assert CHUNKS % (2 * H) == 0 and PART % G == 0 and EARLY + 4 <= HOTS and EARLY % 2 == 0
    EH1, EH2 = eW1.shape[2], eW2.shape[2]
    assert EH1 == 128 and EH2 == 64 and sW2.shape[1] == 128

    gather_rows = nc.dram_tensor("gather_rows", (N, 2 * C), F16).ap()

    with ExitStack() as ctx:
        def sb(name, shape, dt=F32):
            return ctx.enter_context(nc.sbuf_tensor(name, shape, dt))

        def ps(name, shape):
            return ctx.enter_context(nc.psum_tensor(name, shape, F32))

        ps_agg = ps("ps_agg", [128, 2, 512])
        ps_turn = ps("ps_turn", [128, 512])
        ps_hm = ps("ps_hm", [128, 512])
        ps_wide = ps("ps_wide", [128, 4, 512])
        ps_l1 = ps_wide[:, 0:2, :]
        ps_gates = ps_wide[:, 1, 0:2 * NT]
        ps_mix = ps_wide[0:NT, 0, C:2 * C]
        ps_l2 = ps_wide[:, 2, :]
        ps_l3 = ps_wide[:, 3, :]

        xs_all = sb("xs", [128, T * (C + 1)])
        xs = xs_all[0:NT].rearrange("p (t c) -> p t c", t=T)
        xnT = sb("xnT", [128, HALVES, N])
        arena = sb("arena", [128, T * C])
        kst = arena[0:NT, :].rearrange("p (t c) -> p t c", t=T)
        AREA = PART * ROW // 2
        GROUPS = SLOTS * GROUP * C
        area = sb("area", [128, AREA])
        assert 2 * GROUPS <= AREA
        xn = area[0:NT, 0:GROUPS].rearrange("p (s k c) -> p s k c", s=SLOTS, k=GROUP)
        xhl = area[0:NT, GROUPS:2 * GROUPS].bitcast(F16).rearrange("p (s k c) -> p s k c", s=SLOTS, k=GROUP)
        at_bk = 2 * GROUPS
        bk_b = area[:, at_bk:at_bk + C]
        bk3, bk_part = (area[:, at_bk + C + q * C // 2:at_bk + C + (q + 1) * C // 2].bitcast(BF16) for q in range(2))
        ones_a = area[:, at_bk + 2 * C:at_bk + 2 * C + 64].bitcast(BF16)
        assert at_bk + 2 * C + 64 <= AREA
        ring = [m.bitcast(F16).rearrange("p (r c) -> p r c", r=PART) for m in (area[:], xs_all[:, 0:AREA])]
        XS_TILES = -(-AREA // (C + 1))

        wlT = sb("wlT", [128, HALVES, C])
        wrT = sb("wrT", [128, HALVES, C])
        wk = sb("wk", [128, HALVES, C])
        wv = sb("wv", [128, HALVES, C])
        wqT = sb("wqT", [128, HALVES, C])
        wmix = sb("wmix", [128, HALVES, C])
        VEC = 15
        V_SB1, V_EB1, V_SB2, V_EB2, V_GM, V_BM, V_BQ = 0, 2, 6, 7, 9, 11, 13
        vec = sb("vec", [128, VEC])
        BC = 4 * C + EXPERTS
        bk_row = sb("bk_row", [1, C])
        bc = sb("bc", [128, BC])
        bl_b, gg_b, bg_b, bv_b = (bc[:, q * C:(q + 1) * C] for q in range(4))
        ident = sb("ident", [128, 128])
        ones = sb("ones", [128, 128])
        zero16 = sb("zero16", [128, 260], F16)
        eps = sb("eps", [128, 1])
        iota = sb("iota", [128, NT])
        tile_base = sb("tile_base", [128, T + 1])
        srcT = sb("srcT", [128, J], I16)
        dst_in = sb("dst_in", [128, J + HOTS * G])
        cuts = sb("cuts", [1, T + 1], I32)
        idx = sb("idx", [128, 2, RING], I32)
        lower = sb("lower", [NT, EXPERTS, EXPERTS])
        pick = sb("pick", [EXPERTS + 1, 2, 128])
        stats = sb("stats", [128, SLOTS, GROUP, 6])
        mv = sb("mv", [128, SLOTS, GROUP, 2])
        sm = sb("sm", [128, 8, SLOTS * GROUP])
        pad = sb("pad", [128, SLOTS * C])
        xT = pad[:, 0:SLOTS * HALVES * NT].rearrange("p (u h n) -> p u h n", u=SLOTS, h=HALVES)
        wide = xT[:, 0]
        ek = pad[0:NT, :].rearrange("p (u c) -> p u c", u=SLOTS)
        kmax = sb("kmax", [NT, C])
        kpart = sb("kpart", [NT, C])

        edge_i = arena[:, 0:2 * NB * EB].bitcast(I32).rearrange("p (l b e) -> p l b e", l=2, b=NB)
        edge_f = arena[:, 2 * NB * EB:4 * NB * EB].rearrange("p (l b e) -> p l b e", l=2, b=NB)
        nat0 = 4 * NB * EB
        w_nat = arena[:, nat0:nat0 + 3 * HALVES * C].rearrange("p (w h c) -> p w h c", w=3, h=HALVES)
        cut0 = nat0 + 3 * HALVES * C
        under = arena[:, cut0:cut0 + T * NB].rearrange("p (t b) -> p t b", t=T)
        n_under = arena[:, cut0 + T * NB:cut0 + T * NB + T]
        limit = arena[:, cut0 + T * NB + T:cut0 + T * NB + 2 * T]
        row_end = arena[:, cut0 + T * NB + 2 * T:cut0 + T * NB + 2 * T + NB]
        keep = arena[:, cut0 + T * NB + 2 * T + NB:cut0 + T * NB + 2 * T + NB + 1]
        row0 = cut0 + T * NB + 2 * T + NB + 1
        bc_row = arena[0:1, row0:row0 + BC]
        vec_rows = arena[0:VEC, row0 + BC:row0 + BC + 128]
        chunk0 = row0 + BC + 128
        chunk_no = arena[0:T, chunk0:chunk0 + CHUNKS]
        begun = arena[0:T, chunk0 + CHUNKS:chunk0 + 2 * CHUNKS]
        begun_all = arena[:, chunk0 + 2 * CHUNKS + 1:chunk0 + 3 * CHUNKS + 1]
        assert chunk0 + 3 * CHUNKS + 1 <= T * C
        cut_col = arena[0:T, chunk0 + 2 * CHUNKS:chunk0 + 2 * CHUNKS + 1]

        at = [0]

        def part(cols, rows=128, dt=F32):
            a = arena[0:rows, at[0]:at[0] + cols]
            at[0] += cols
            return a if dt == F32 else a.bitcast(dt)

        one_hots = part(HOTS * G * 64)
        hot_all = one_hots.bitcast(F16)
        hot = hot_all.rearrange("p (h g n) -> p h g n", h=HOTS, g=G)
        hot_next = part(G * 64, dt=F16).rearrange("p (g n) -> p g n", g=G)
        lam0 = EARLY * G * 64
        lam_n, lam_nT, lam = (one_hots[:, lam0 + q * HALVES * C:lam0 + (q + 1) * HALVES * C]
                              .rearrange("p (h c) -> p h c", h=HALVES) for q in range(3))
        x_rows = part(2 * C, NT).rearrange("p (u c) -> p u c", u=2)
        dst_rel_next = part(G)
        s1w = part(HALVES * C).rearrange("p (h c) -> p h c", h=HALVES)
        s2w = part(HALVES * 128).rearrange("p (h c) -> p h c", h=HALVES)
        s3w = part(C)
        e1w = part(HALVES * EXPERTS * EH1).rearrange("p (h e c) -> p h e c", h=HALVES, e=EXPERTS)
        e2w = part(EXPERTS * EH2).rearrange("p (e c) -> p e c", e=EXPERTS)
        e3w = part(EXPERTS // 2 * C).rearrange("p (r c) -> p r c", c=C)
        gw = part(HALVES * EXPERTS).rearrange("p (h e) -> p h e", h=HALVES)
        b35 = part(C, EXPERTS + 1)
        bl3, bmix3 = part(C // 2, dt=BF16), part(C // 2, dt=BF16)
        ones3 = part(64, dt=BF16)
        part16 = part(C // 2, dt=BF16)
        bmix = part(C, NT)
        agg_mean = part(C, NT)
        turned = part(4 * NT).rearrange("p (h n) -> p h n", h=4)
        aggT, x2T = turned[:, 0:2, :], turned[:, 2:4, :]
        xTc = part(2 * NT).rearrange("p (h n) -> p h n", h=2)
        hn = part(C, NT)
        x1 = part(C, NT)
        x2 = part(C, NT)
        sh1 = part(2 * NT).rearrange("p (h n) -> p h n", h=2)
        eh1 = part(EXPERTS * NT).rearrange("p (h n) -> p h n", h=EXPERTS)
        sh2 = part(NT)
        eh2 = part(2 * NT).rearrange("p (h n) -> p h n", h=2)
        eh2g = part(2 * NT).rearrange("p (h n) -> p h n", h=2)
        y = part(C, NT)
        gate5 = part(EXPERTS + 1, NT)
        gateT = part(NT, EXPERTS + 1)
        col = part(96, NT)
        (deg, rc, lmax, esum, rsum, wsum, rw) = (col[:, q:q + 1] for q in range(7))
        lv1, g1, nt1, rs1, lv2, g2, nt2, rs2 = (col[:, 8 + q:9 + q] for q in range(8))
        lg, ex, gt, ez, rank = (col[:, 20 + 4 * q:24 + 4 * q] for q in range(5))
        gt_m = col[:, 40:56].rearrange("p (e f) -> p e f", e=EXPERTS)
        eq_m = col[:, 56:72].rearrange("p (e f) -> p e f", e=EXPERTS)
        st1, st2 = col[:, 72:78], col[:, 78:84]
        mv1, mv2 = col[:, 84:86], col[:, 86:88]
        assert at[0] <= T * C

        names = """
            weights_in ffn_in xs_ones x_row_used lam_n_made lam_turned lam_nT_made lam_v edges_in
            ident_made pad_made consts_made iota_made edges_float edge_steps
            under_reduced cuts_clean cuts_summed cuts_made
            bk_spread bk_link cut_col_made begun_made begun_summed begun_copied dst_shifted vec_turned vec_made
            bc_spread bc_made nat_turned nat_copied src_turned src_copied dst_turned dst_copied
            kpart_made kmax_merged kmax_turned kmax_reduced kmax_col_wide kmax_spread kmax_made
            lam_link lam_ln lam_guess lam_done wmix_done wmix_made bmix_spread bmix_made
            ring_ones idx_copied slots_freed x2_zeroed
            hot_built rel_next_made hot_next_built tile_summed next_summed
            deg_read rc_made agg_scaled both_turned both_used xTc_made mix_done gnn_done h_used
            x2_made logits_done l1s_done l1e_done sh1_made eh1_made l2_done sh2_made eh2_made
            gate_made gate_turned gateT_made gates_spread eh2g_made l3_done y_made y_stored
            dve_link lg_shifted lg_exp z_made z_exp st1_made st2_made mv1_made ln1 guess1 x1_made mv2_made ln2 guess2
        """
        s = {name: ctx.enter_context(nc.semaphore(name)) for name in names.split()}

        def per_slot(names):
            return {n: [ctx.enter_context(nc.semaphore(f"{n}{u}")) for u in range(SLOTS)] for n in names.split()}

        a = per_slot("""x_in stats_made mv_made ln_made guess_made newton rstd_made xn_made high_used
                        low_made rows_stored rows_kept turned evacuated kept k_summed k_stored""")
        b = per_slot("k_shifted exp_made lam_added")
        x_row_in = [ctx.enter_context(nc.semaphore(f"x_row_in{u}")) for u in range(2)]
        landed = [ctx.enter_context(nc.semaphore(f"landed{h}")) for h in range(H)]

        A_STEPS = T // (GROUP * SLOTS)
        PER_SLOT = GROUP * A_STEPS
        B_STEPS = T // SLOTS

        def tile_rows(dram, t, r0, r1, count=1):
            return dram.rearrange("(t p) c -> p t c", p=NT)[r0:r1, bass.ds(t, count), :]

        weight_loads = [
            (w_nat[:, 0], W_l.rearrange("(h p) c -> p h c", p=128)),
            (w_nat[:, 1], W_r.rearrange("(h p) c -> p h c", p=128)),
            (w_nat[:, 2], W_qk[0].rearrange("(h p) c -> p h c", p=128)),
            (wk[:], W_qk[1].rearrange("(h p) c -> p h c", p=128)),
            (wv[:], W_v.rearrange("(h p) c -> p h c", p=128)),
        ]
        ffn_loads = [
            (s1w, sW1.rearrange("(h p) c -> p h c", p=128)),
            (s2w, sW2.rearrange("(h p) c -> p h c", p=128)),
            (s3w, sW3),
            (e2w, eW2.rearrange("e p c -> p e c")),
            (gw, gW.rearrange("(h p) c -> p h c", p=128)),
            (b35[0:EXPERTS, :], eb3), (b35[EXPERTS:EXPERTS + 1, :], sb3.rearrange("(o c) -> o c", o=1)),
        ]
        weight_loads += [
            (vec_rows[V_SB1:V_SB1 + 2, :], sb1.rearrange("(r c) -> r c", c=128)),
            (vec_rows[V_EB1:V_EB1 + 4, :], eb1),
            (vec_rows[V_SB2:V_SB2 + 1, :], sb2.rearrange("(r c) -> r c", c=128)),
            (vec_rows[V_EB2:V_EB2 + 2, :], eb2.rearrange("(r a) c -> r (a c)", a=2)),
            (vec_rows[V_GM:V_GM + 2, :], gamma_m.rearrange("(r c) -> r c", c=128)),
            (vec_rows[V_BM:V_BM + 2, :], beta_m.rearrange("(r c) -> r c", c=128)),
            (vec_rows[V_BQ:V_BQ + 2, :], b_qk[0:1].rearrange("o (r c) -> (o r) c", c=128)),
            (bc_row[:, 0:C], b_l.rearrange("(o c) -> o c", o=1)),
            (bc_row[:, C:2 * C], gamma_g.rearrange("(o c) -> o c", o=1)),
            (bc_row[:, 2 * C:3 * C], beta_g.rearrange("(o c) -> o c", o=1)),
            (bc_row[:, 3 * C:4 * C], b_v.rearrange("(o c) -> o c", o=1)),
            (bc_row[:, 4 * C:BC], gb.rearrange("(o c) -> o c", o=1)),
            (bk_row[:], b_qk[1:2, :]),
        ]
        ffn_loads += [(e1w[:, h], eW1.rearrange("e (h p) c -> h p e c", p=128)[h]) for h in range(HALVES)]
        ffn_loads += [(e3w[64 * q:64 * q + 64], eW3.rearrange("(r a) p c -> a p r c", a=2)[q]) for q in range(2)]
        WEIGHTS_IN = 16 * len(weight_loads)
        FFN_IN = 16 * len(ffn_loads)
        WHOLE = FULL // 128 * 128
        edge_loads = []
        for l, edges in enumerate((src, dst)):
            edge_loads.append((edge_i[:, l, 0:WHOLE // 128, :],
                               edges[0:WHOLE * EB].rearrange("(b p e) -> p b e", p=128, e=EB)))
            if FULL > WHOLE:
                edge_loads.append((edge_i[0:FULL - WHOLE, l, NB - 1, :],
                                   edges[WHOLE * EB:FULL * EB].rearrange("(p e) -> p e", e=EB)))
            if REST:
                edge_loads.append((edge_i[FULL - WHOLE:FULL - WHOLE + 1, l, NB - 1, 0:REST],
                                   edges[FULL * EB:E].rearrange("(o e) -> o e", o=1)))
        EDGES_IN = 16 * len(edge_loads)
        assert WHOLE // 128 == NB - 1

        block = ctx.enter_context(nc.Block())

        @block.sync
        def _(sp):
            def load_x(g, u, seen):
                for r0, r1 in ((0, ROWS_A), (ROWS_A, NT)):
                    sp.dma_start(xs[r0:r1, bass.ds(g * GROUP, GROUP), 0:C],
                                 tile_rows(x, g * GROUP, r0, r1, GROUP)).then_inc(a["x_in"][u], 16)

            for u in range(SLOTS):
                load_x(u, u, 0)
            sp.wait_ge(s["pad_made"], 2)
            for to, of in edge_loads:
                sp.dma_start(to, of).then_inc(s["edges_in"], 16)
            for to, of in weight_loads:
                sp.dma_start(to, of).then_inc(s["weights_in"], 16)
            for i in range(1, A_STEPS):
                for u in range(SLOTS):
                    sp.wait_ge(a["x_in"][u], 32 * i)
                    load_x(SLOTS * i + u, u, 32 * i)

            with sp.Fori(0, A_STEPS) as i:
                for u in range(SLOTS):
                    sp.wait_ge(a["low_made"][u], i + 1)
                    for r0, r1 in ((0, ROWS_A), (ROWS_A, NT)):
                        sp.dma_start(tile_rows(gather_rows, (i * SLOTS + u) * GROUP, r0, r1, GROUP),
                                     xhl[r0:r1, u]).then_inc(a["rows_stored"][u], 16)

            for u in range(SLOTS):
                sp.wait_ge(b["lam_added"][u], B_STEPS)
            for to, of in ffn_loads:
                sp.dma_start(to, of).then_inc(s["ffn_in"], 16)
            def load_tile(t, u):
                for r0, r1 in ((0, ROWS_A), (ROWS_A, NT)):
                    sp.dma_start(x_rows[r0:r1, u:u + 1, :], tile_rows(x, t, r0, r1)
                                 ).then_inc(x_row_in[u], 16)

            load_tile(0, 0)
            load_tile(1, 1)
            with sp.Fori(0, T // 2 - 1) as i:
                for u in range(2):
                    sp.wait_ge(s["ffn_in"], FFN_IN)
                    sp.wait_ge(s["x_row_used"], i * 2 + u + 1)
                    load_tile(i * 2 + u + 2, u)

        @block.gpsimd
        def _(pool):
            nc.gpsimd.memset(edge_i[:, 0, NB - 1, :], 0).then_inc(s["pad_made"], 1)
            nc.gpsimd.memset(edge_i[:, 1, NB - 1, :], int(NO_NODE)).then_inc(s["pad_made"], 1)
            nc.gpsimd.memset(ones[:], 1.0).then_inc(s["consts_made"], 1)
            nc.gpsimd.memset(zero16[:], 0.0).then_inc(s["consts_made"], 1)
            nc.gpsimd.memset(eps[:], EPS).then_inc(s["consts_made"], 1)
            pool.wait_ge(s["consts_made"], 3)
            nc.gpsimd.affine_select(out=ident[:], in_=ones[:], pattern=[[-1, 128]], compare_op=ALU.is_equal,
                                    fill=0.0, base=0, channel_multiplier=1).then_inc(s["ident_made"], 1)
            nc.gpsimd.affine_select(
                out=lower[:], in_=ones[0:NT, 0:EXPERTS * EXPERTS].rearrange("p (e f) -> p e f", e=EXPERTS),
                pattern=[[1, EXPERTS], [-1, EXPERTS]], compare_op=ALU.is_gt, fill=0.0, base=0,
                channel_multiplier=0).then_inc(s["ident_made"], 1)
            for r in range(2):
                nc.gpsimd.affine_select(
                    out=pick[:, r, :], in_=ones[0:EXPERTS + 1, :], pattern=[[-1, 2], [0, 64]],
                    compare_op=ALU.is_equal, fill=0.0, base=-2 * r, channel_multiplier=1).then_inc(s["ident_made"], 1)
            nc.gpsimd.iota(iota[:], pattern=[[1, NT]], base=0, channel_multiplier=0,
                           allow_small_or_imprecise_dtypes=True).then_inc(s["iota_made"], 1)
            nc.gpsimd.iota(tile_base[:], pattern=[[-NT, T + 1]], base=0, channel_multiplier=0,
                           allow_small_or_imprecise_dtypes=True).then_inc(s["iota_made"], 1)
            nc.gpsimd.memset(dst_in[:, J:J + HOTS * G], NO_NODE).then_inc(s["iota_made"], 1)
            nc.gpsimd.iota(chunk_no, pattern=[[1, CHUNKS]], base=0, channel_multiplier=0,
                           allow_small_or_imprecise_dtypes=True).then_inc(s["iota_made"], 1)
            nc.gpsimd.iota(limit, pattern=[[NT, T]], base=NT, channel_multiplier=0,
                           allow_small_or_imprecise_dtypes=True).then_inc(s["iota_made"], 1)
            with pool.Fori(0, A_STEPS) as i:
                for v in range(GROUP * SLOTS):
                    u = v % SLOTS
                    pool.wait_ge(a["evacuated"][u], i * GROUP + v // SLOTS + 1)
                    nc.gpsimd.tensor_copy(xnT[:, :, bass.ds((i * GROUP * SLOTS + v) * NT, NT)],
                                          xT[:, u]).then_inc(a["kept"][u], 1)

            for u in range(SLOTS):
                pool.wait_ge(a["rows_stored"][u], 32 * A_STEPS)
                pool.wait_ge(a["turned"][u], PER_SLOT)
                pool.wait_ge(a["k_summed"][u], PER_SLOT)
                pool.wait_ge(a["high_used"][u], A_STEPS)
                pool.wait_ge(a["low_made"][u], A_STEPS)
                pool.wait_ge(a["rows_kept"][u], A_STEPS)
            pool.wait_ge(s["src_copied"], NB)
            nc.gpsimd.memset(ring[0][:, :, 2 * C:ROW], 1.0).then_inc(s["ring_ones"], 1)
            nc.gpsimd.tensor_copy(idx[:, 0], srcT[:, 0:RING]).then_inc(s["idx_copied"], 1)

            def round_of_gathers(n, r, first=False, last=False):
                pool.reg_add(rounds, rounds, 1)
                for h in range(H):
                    pool.reg_add(chunk, chunk, 1)
                    if first and h * G == PART:
                        for u in range(SLOTS):
                            pool.wait_ge(b["lam_added"][u], -(-XS_TILES // SLOTS))
                        nc.gpsimd.memset(ring[1][:, :, 2 * C:ROW], 1.0).then_inc(s["ring_ones"], 1)
                    copied = pool.snap(rounds, min_val=1, max_val=ROUNDS) if h == 0 else None
                    free = None if first else pool.snap(chunk, min_val=1, max_val=CHUNKS)
                    pool.wait_ge(s["ring_ones"], 1 + h * G // PART)
                    if h == 0:
                        pool.wait_ge(s["idx_copied"], copied)
                    if not first:
                        pool.wait_ge(s["slots_freed"], free)
                    for g in range(G):
                        k = h * G + g
                        nc.gpsimd.indirect_dma_start(
                            ring[k // PART][:, k % PART, 0:2 * C], None, gather_rows,
                            bass.IndirectOffsetOnAxis(idx[:, r, k:k + 1], 0)).then_inc(landed[h], 16)
                if not last:
                    nc.gpsimd.tensor_copy(idx[:, 1 - r], srcT[:, bass.ds((n + 1) * RING, RING)]
                                          ).then_inc(s["idx_copied"], 1)

            ROUNDS = CHUNKS // H
            rounds, chunk = pool.alloc_register("pool_round"), pool.alloc_register("pool_chunk")
            pool.reg_mov(rounds, 0)
            pool.reg_mov(chunk, 0)
            round_of_gathers(0, 0, first=True)
            with pool.Fori(0, ROUNDS // 2 - 1) as i:
                for r in range(2):
                    round_of_gathers(i * 2 + 1 + r, 1 - r)
            round_of_gathers(ROUNDS - 1, 1, last=True)

        @block.tensor
        def _(pe):
            mm = nc.tensor.matmul
            pe.wait_ge(s["ident_made"], 4)
            pe.wait_ge(s["under_reduced"], 1)
            mm(ps_hm[0:1, 128:128 + T], ones[:, 0:1], n_under, start=True, stop=True)
            mm(ps_hm[0:T, 0:1], n_under, ones[:, 0:1], start=True, stop=True).then_inc(s["cuts_summed"], 1)
            pe.wait_ge(s["begun_made"], 1)
            mm(ps_hm[:, 256:256 + CHUNKS], ones[0:T, :], begun, start=True, stop=True).then_inc(s["begun_summed"], 1)
            pe.wait_ge(s["edges_float"], 2)
            pe.wait_ge(s["cuts_made"], 1)
            for blk in range(NB):
                if blk:
                    pe.wait_ge(s["src_copied"], blk)
                pe.transpose(ps_turn[:, 0:128], edge_f[:, 0, blk, :], ident[:]).then_inc(s["src_turned"], 1)
                if blk:
                    pe.wait_ge(s["dst_copied"], blk)
                pe.transpose(ps_hm[:, 0:128], edge_f[:, 1, blk, :], ident[:]).then_inc(s["dst_turned"], 1)

            pe.wait_ge(s["weights_in"], WEIGHTS_IN)
            for w in range(3):
                for h in range(HALVES):
                    for k in range(HALVES):
                        last = pe.transpose(ps_wide[:, w, k * C + h * 128:k * C + h * 128 + 128],
                                            w_nat[:, w, h, k * 128:(k + 1) * 128], ident[:])
                last.then_inc(s["nat_turned"], 1)
            pe.transpose(ps_wide[:, 3, 0:VEC], vec_rows[:], ident[0:VEC, 0:VEC]).then_inc(s["vec_turned"], 1)
            pe.wait_ge(s["dst_shifted"], 1)
            mm(ps_hm[:, 256:256 + C], ones[0:1, :], bk_row[:], start=True, stop=True).then_inc(s["bk_spread"], 1)
            mm(ps_agg[:, 0, 0:512], ones[0:1, :], bc_row[:, 0:512], start=True, stop=True)
            mm(ps_agg[:, 1, 0:512], ones[0:1, :], bc_row[:, 512:1024], start=True, stop=True)
            pe.wait_ge(s["bk_link"], 1)
            mm(ps_hm[:, 0:EXPERTS], ones[0:1, :], bc_row[:, 1024:BC], start=True, stop=True).then_inc(s["bc_spread"], 1)
            pe.sem_inc(s["slots_freed"], H - 1)
            pe.wait_ge(s["nat_copied"], 3)
            pe.wait_ge(s["vec_made"], 1)
            pe.wait_ge(s["bk_link"], BK_LINKS)
            with pe.Fori(0, A_STEPS) as i:
                for v in range(GROUP * SLOTS + 1):
                    if v < GROUP * SLOTS:
                        u, t = v % SLOTS, v // SLOTS
                        if v % GROUP == 0:
                            pe.wait_ge(a["xn_made"][v // GROUP], i + 1)
                        pe.wait_ge(a["evacuated"][u], i * GROUP + t)
                        for h in range(HALVES):
                            last = pe.transpose(ps_wide[:, u, h * NT:(h + 1) * NT],
                                                xn[:, v // GROUP, v % GROUP, h * 128:(h + 1) * 128],
                                                ident[0:NT, 0:NT])
                        last.then_inc(a["turned"][v // GROUP], 1)
                    if v:
                        u, t = (v - 1) % SLOTS, (v - 1) // SLOTS
                        pe.wait_ge(a["evacuated"][u], i * GROUP + t + 1)
                        pe.wait_ge(a["k_stored"][u], i * GROUP + t)
                        kk = ps_wide[0:NT, 2 + u, 0:C]
                        mm(kk, ones_a[0:65, 0:NT], bk3[0:65], start=True, stop=False)
                        for h in range(HALVES):
                            last = mm(kk, xT[:, u, h, :], wk[:, h, :], start=False, stop=(h == HALVES - 1))
                        last.then_inc(a["k_summed"][u], 1)

            pe.wait_ge(s["kmax_merged"], A_STEPS + 1)
            pe.wait_ge(s["src_copied"], NB)
            pe.wait_ge(s["dst_copied"], NB)
            for h in range(HALVES):
                last = pe.transpose(ps_turn[:, h * NT:(h + 1) * NT], kmax[:, h * 128:(h + 1) * 128], ident[0:NT, 0:NT])
            last.then_inc(s["kmax_turned"], 1)
            pe.wait_ge(s["kmax_col_wide"], 1)
            for h in range(HALVES):
                last = mm(ps_hm[0:NT, h * 128:(h + 1) * 128], wide[:, h, :], ident[:], start=True, stop=True)
            last.then_inc(s["kmax_spread"], 1)
            for h in range(HALVES):
                mm(ps_agg[:, h, 0:C + 1], zero16[:, 0:128], zero16[:, 0:C + 1], start=True, stop=False,
                   skip_group_check=True)
            pe.wait_ge(s["xs_ones"], 1)
            for u in range(SLOTS):
                pe.wait_ge(a["rows_kept"][u], A_STEPS)
            with pe.Fori(0, B_STEPS) as i:
                for u in range(SLOTS):
                    pe.wait_ge(b["exp_made"][u], i + 1)
                    for h in range(HALVES):
                        last = mm(ps_agg[:, h, 0:C + 1], ek[:, u, h * 128:(h + 1) * 128],
                                  xs[:, bass.ds(i * SLOTS + u, 1), :].squeeze(1),
                                  start=False, stop=False, skip_group_check=True)
                    last.then_inc(b["lam_added"][u], 1)
            pe.wait_ge(s["lam_n_made"], 1)
            for k in range(HALVES):
                for h in range(HALVES):
                    last = pe.transpose(ps_turn[:, k * C + h * 128:k * C + (h + 1) * 128],
                                        lam_n[:, h, k * 128:(k + 1) * 128], ident[:])
            last.then_inc(s["lam_turned"], 1)
            pe.wait_ge(s["lam_nT_made"], 1)
            for h in range(HALVES):
                for k in range(HALVES):
                    last = mm(ps_wide[:, h, 0:C], lam_nT[:, k, h * 128:(h + 1) * 128], wv[:, k, :], start=(k == 0),
                              stop=(k == HALVES - 1))
            last.then_inc(s["lam_v"], 1)
            pe.wait_ge(s["lam_done"], 1)
            for k in range(HALVES):
                for h in range(HALVES):
                    last = mm(ps_wide[:, k, 0:C], wqT[:, h, k * 128:(k + 1) * 128], lam[:, h, :], start=(h == 0),
                              stop=(h == HALVES - 1))
            last.then_inc(s["wmix_done"], 1)
            for h in range(HALVES):
                last = mm(ps_wide[0:NT, 2, 0:C], wide[:, h, :], lam[:, h, :], start=(h == 0), stop=(h == HALVES - 1))
            last.then_inc(s["bmix_spread"], 1)

            nn, cut, bank = (pe.alloc_register(f"pe_{q}") for q in ("tile", "cut", "bank"))
            pe.wait_ge(s["cuts_made"], 1)
            pe.wait_ge(s["ffn_in"], FFN_IN)
            pe.reg_mov(nn, 0)
            pe.reg_mov(bank, 0)
            pe.reg_load(cut, cuts[0:1, 0:1])
            sums = ps_agg.rearrange("p b c -> p (b c)")

            def clear(bank_v):
                return mm(sums[0:NT, bass.ds(bank_v, C + 1)], zero16[:, 0:NT], zero16[:, 0:C + 1],
                          start=True, stop=False, skip_group_check=True)

            def add_chunk(h, onehot, bank_v, frees=False):
                for g in range(G):
                    w = onehot[:, g, 0:NT]
                    k = h * G + g
                    rows = ring[k // PART][:, k % PART]
                    m = mm(sums[0:NT, bass.ds(bank_v, C)], w, rows[:, 0:C], start=False, stop=False,
                           skip_group_check=True)
                    if frees and g == 0:
                        m.then_inc(s["slots_freed"], 1)
                    last = mm(sums[0:NT, bass.ds(bank_v, C + 1)], w, rows[:, C:2 * C + 1], start=False,
                              stop=False, skip_group_check=True)
                return last

            def stage2_l1(v, prev):
                pe.wait_ge(s["both_used"], v)
                pe.wait_ge(s["sh1_made"], prev)
                logits = ps_turn[0:NT, 500:500 + EXPERTS]
                mm(logits, ones[0:1, 0:NT], bc[0:1, 4 * C:BC], start=True, stop=False)
                for h in range(HALVES):
                    last = mm(logits, x2T[:, h, :], gw[:, h, :], start=False, stop=(h == 1))
                last.then_inc(s["logits_done"], 1)
                for o in range(2):
                    for h in range(HALVES):
                        last = mm(ps_l1[:, 0, o * NT:(o + 1) * NT], s1w[:, h, o * 128:(o + 1) * 128], x2T[:, h, :],
                                  start=(h == 0), stop=(h == 1))
                last.then_inc(s["l1s_done"], 1)
                pe.wait_ge(s["eh1_made"], prev)
                for e in range(EXPERTS):
                    for h in range(HALVES):
                        last = mm(ps_l1[:, 1, e * NT:(e + 1) * NT], e1w[:, h, e, :], x2T[:, h, :],
                                  start=(h == 0), stop=(h == 1))
                last.then_inc(s["l1e_done"], 1)

            def stage2_l2(v, prev):
                pe.wait_ge(s["gate_made"], v)
                pe.transpose(ps_turn[0:EXPERTS + 1, 0:NT], gate5[:], ident[0:NT, 0:NT]).then_inc(s["gate_turned"], 1)
                pe.wait_ge(s["sh1_made"], v)
                for h in range(2):
                    last = mm(ps_l2[:, 0:NT], s2w[:, h, :], sh1[:, h, :], start=(h == 0), stop=(h == 1))
                pe.wait_ge(s["eh1_made"], v)
                for e in range(EXPERTS):
                    q = 64 * (e % 2)
                    c0 = NT * (1 + e // 2)
                    last = mm(ps_l2[q:q + 64, c0:c0 + NT], e2w[:, e, :], eh1[:, e, :], start=True, stop=True)
                last.then_inc(s["l2_done"], 1)
                pe.wait_ge(s["gateT_made"], v)
                for r in range(2):
                    last = mm(ps_gates[:, r * NT:(r + 1) * NT], pick[:, r, :], gateT, start=True, stop=True)
                last.then_inc(s["gates_spread"], 1)

            def stage2_l3(v, prev):
                o = ps_l3[0:NT, 0:C]
                pe.wait_ge(s["y_made"], prev)
                mm(o, gateT, b35, start=True, stop=False)
                pe.wait_ge(s["sh2_made"], v)
                mm(o, sh2, s3w, start=False, stop=False)
                pe.wait_ge(s["eh2g_made"], v)
                for r in range(2):
                    last = mm(o, eh2g[:, r, :], e3w[:, r, :], start=False, stop=(r == 1))
                last.then_inc(s["l3_done"], 1)

            def turn_x2(v, prev):
                pe.wait_ge(s["x2_made"], v)
                pe.wait_ge(s["gateT_made"], prev)
                for h in range(HALVES):
                    last = pe.transpose(ps_turn[:, (2 + h) * NT:(3 + h) * NT], x2[:, h * 128:(h + 1) * 128],
                                        ident[0:NT, 0:NT])
                return last

            def node_tile(v, prev, h_c, bank_w):
                pe.wait_ge(s["wmix_made"], 1)
                pe.wait_ge(s["hot_next_built"], v)
                add_chunk(h_c, hot_next, bank_w).then_inc(s["next_summed"], 1)
                pe.wait_ge(s["agg_scaled"], v)
                pe.wait_ge(s["gateT_made"], prev)
                for h in range(HALVES):
                    pe.transpose(ps_turn[:, h * NT:(h + 1) * NT], agg_mean[:, h * 128:(h + 1) * 128],
                                 ident[0:NT, 0:NT])
                turn_x2(v, prev).then_inc(s["both_turned"], 1)
                pe.wait_ge(s["xTc_made"], v)
                pe.wait_ge(s["h_used"], prev)
                mm(ps_hm[0:NT, 0:C], ones3[0:65, 0:NT], bl3[0:65], start=True, stop=False)
                for h in range(HALVES):
                    mm(ps_hm[0:NT, 0:C], xTc[:, h, :], wrT[:, h, :], start=False, stop=False)
                stage2_l1(v, prev)
                for h in range(HALVES):
                    last = mm(ps_hm[0:NT, 0:C], aggT[:, h, :], wlT[:, h, :], start=False, stop=(h == 1))
                last.then_inc(s["gnn_done"], 1)
                stage2_l2(v, prev)
                pe.wait_ge(s["x1_made"], prev)
                mm(ps_mix, ones3[0:65, 0:NT], bmix3[0:65], start=True, stop=False)
                for h in range(HALVES):
                    last = mm(ps_mix, xTc[:, h, :], wmix[:, h, :], start=False, stop=(h == 1))
                last.then_inc(s["mix_done"], 1)
                stage2_l3(v, prev)

            clear(0)
            with pe.Fori(0, CHUNKS // HOTS) as i:
                for h in range(HOTS):
                    bank_v = pe.snap(bank, min_val=0, max_val=512)
                    pe.wait_ge(landed[h], (i + 1) * (16 * G))
                    pe.wait_ge(s["hot_built"], i * HOTS + h + 1)
                    add_chunk(h, hot[:, h], bank_v, frees=True)
                    with pe.While(lambda: pe.snap(cut, min_val=0, max_val=CHUNKS) == i * HOTS + h):
                        prev = pe.snap(nn, min_val=0, max_val=T - 1)
                        v = pe.snap(prev + 1, min_val=1, max_val=T)
                        pe.reg_sub(bank, 512, bank)
                        bank_w = pe.snap(bank, min_val=0, max_val=512)
                        pe.wait_ge(s["agg_scaled"], prev)
                        pe.wait_ge(s["deg_read"], prev)
                        clear(bank_w).then_inc(s["tile_summed"], 1)
                        node_tile(v, prev, h, bank_w)
                        pe.reg_load(cut, cuts[0:1, bass.ds(v, 1)])
                        pe.reg_add(nn, nn, 1)
            turn_x2(T + 1, T).then_inc(s["both_turned"], 1)
            stage2_l1(T + 1, T)
            stage2_l2(T + 1, T)
            stage2_l3(T + 1, T)

        v2 = nc.vector
        op = v2.tensor_tensor

        @block.vector
        def _(dve):
            var = mv[0:NT, :, :, 1]
            guess_a, tmp_a, rstd_a = (sm[0:NT, q].rearrange("p (u k) -> p u k", u=SLOTS) for q in (1, 2, 3))

            def moments(i, u):
                t0 = (i * SLOTS + u) * GROUP
                dve.wait_ge(a["x_in"][u], (i + 1) * 32)
                for k in range(GROUP):
                    last = v2.bn_stats(stats[0:NT, u, k, :], xs[:, bass.ds(t0 + k, 1), 0:C])
                last.then_inc(a["stats_made"][u], 1)
                dve.wait_ge(s["iota_made"], 5)
                dve.wait_ge(a["stats_made"][u], i + 1)
                for k in range(GROUP):
                    last = v2.bn_aggr(mv[0:NT, u, k, :], stats[0:NT, u, k, :])
                last.then_inc(a["mv_made"][u], 1)

            def normalize(i, u):
                t0 = (i * SLOTS + u) * GROUP
                dve.wait_ge(a["guess_made"][u], i + 1)
                op(tmp_a[:, u], guess_a[:, u], guess_a[:, u], ALU.mult).then_inc(a["newton"][u], 1)
                dve.wait_ge(a["newton"][u], i * 3 + 1)
                v2.scalar_tensor_tensor(tmp_a[:, u], var[:, u], EPS, tmp_a[:, u], ALU.add, ALU.mult
                                        ).then_inc(a["newton"][u], 1)
                dve.wait_ge(a["newton"][u], i * 3 + 2)
                v2.tensor_scalar(tmp_a[:, u], tmp_a[:, u], -0.5, 1.5, ALU.mult, ALU.add).then_inc(a["newton"][u], 1)
                dve.wait_ge(a["newton"][u], i * 3 + 3)
                op(rstd_a[:, u], guess_a[:, u], tmp_a[:, u], ALU.mult).then_inc(a["rstd_made"][u], 1)
                dve.wait_ge(a["rstd_made"][u], i + 1)
                dve.wait_ge(a["rows_kept"][u], i)
                dve.wait_ge(a["high_used"][u], i)
                dve.wait_ge(a["low_made"][u], i)
                dve.wait_ge(a["turned"][u], i * GROUP)
                for k in range(GROUP):
                    last = v2.tensor_scalar(xn[:, u, k, :], xs[:, bass.ds(t0 + k, 1), 0:C].squeeze(1),
                                            mv[0:NT, u, k, 0:1], rstd_a[:, u, k:k + 1], ALU.subtract, ALU.mult)
                last.then_inc(a["xn_made"][u], 1)

            def split(row, to, part, link):
                link(v2.tensor_copy(to[0:1], row[0:1]))
                for q in (32, 64):
                    link(v2.tensor_copy(part, row))
                    link(op(row, row, part, ALU.subtract))
                    link(v2.tensor_copy(to[q:q + 1], row[q:q + 1]))

            bk_links = [0]

            def bk_link(ins):
                bk_links[0] += 1
                ins.then_inc(s["bk_link"], 1)
                dve.wait_ge(s["bk_link"], bk_links[0])

            moments(0, 0)
            dve.wait_ge(s["edges_in"], EDGES_IN)
            v2.tensor_copy(edge_f[:, 1], edge_i[:, 1]).then_inc(s["edges_float"], 1)
            v2.tensor_copy(edge_f[:, 0], edge_i[:, 0]).then_inc(s["edges_float"], 1)
            v2.memset(cuts[:], 0).then_inc(s["cuts_clean"], 1)
            dve.wait_ge(s["ident_made"], 4)
            v2.tensor_reduce(keep, ident.rearrange("p (k g) -> p g k", g=G)[:, G - 1, :], AX.X, ALU.add
                             ).then_inc(s["edge_steps"], 1)
            dve.wait_ge(s["edge_steps"], 1)
            v2.tensor_scalar(keep, keep, -NO_NODE, NO_NODE, ALU.mult, ALU.add).then_inc(s["edge_steps"], 1)
            dve.wait_ge(s["edge_steps"], 2)
            dve.wait_ge(s["edges_float"], 1)
            v2.tensor_scalar(row_end, edge_f[:, 1, :, EB - 1], keep, None, ALU.max).then_inc(s["edge_steps"], 1)
            dve.wait_ge(s["edge_steps"], 3)
            dve.wait_ge(s["iota_made"], 5)
            op(under, row_end.unsqueeze(1).broadcast_to([128, T, NB]), limit.unsqueeze(2).broadcast_to([128, T, NB]),
               ALU.is_lt).then_inc(s["edge_steps"], 1)
            dve.wait_ge(s["edge_steps"], 4)
            v2.tensor_reduce(n_under, under, AX.X, ALU.add).then_inc(s["under_reduced"], 1)
            dve.wait_ge(s["cuts_summed"], 1)
            dve.wait_ge(s["cuts_clean"], 1)
            v2.tensor_copy(cuts[:, 0:T], ps_hm[0:1, 128:128 + T]).then_inc(s["cuts_made"], 1)
            v2.tensor_copy(cut_col, ps_hm[0:T, 0:1]).then_inc(s["cut_col_made"], 1)
            dve.wait_ge(s["cut_col_made"], 1)
            v2.tensor_scalar(begun, chunk_no, cut_col, float(NT), ALU.is_gt, ALU.mult).then_inc(s["begun_made"], 1)
            normalize(0, 0)
            for blk in range(NB):
                n = min(128, J - blk * 128)
                dve.wait_ge(s["src_turned"], blk + 1)
                v2.tensor_copy(srcT[:, blk * 128:blk * 128 + n], ps_turn[:, 0:n]).then_inc(s["src_copied"], 1)
            dve.wait_ge(s["begun_summed"], 1)
            dve.wait_ge(s["dst_copied"], NB)
            v2.tensor_copy(begun_all, ps_hm[:, 256:256 + CHUNKS]).then_inc(s["begun_copied"], 1)
            dve.wait_ge(s["begun_copied"], 1)
            by_chunk = dst_in[:, 0:J].rearrange("p (c g) -> p c g", g=G)
            op(by_chunk, by_chunk, begun_all.unsqueeze(2).broadcast_to([128, CHUNKS, G]), ALU.subtract
               ).then_inc(s["dst_shifted"], 1)
            v2.memset(ones_a, 1.0)
            v2.memset(bk3, 0.0)
            dve.wait_ge(s["bk_spread"], 1)
            bk_link(v2.tensor_copy(bk_b, ps_hm[:, 256:256 + C]))
            split(bk_b, bk3, bk_part, bk_link)
            assert bk_links[0] == BK_LINKS
            dve.wait_ge(s["vec_turned"], 1)
            v2.tensor_copy(vec[:], ps_wide[:, 3, 0:VEC]).then_inc(s["vec_made"], 1)
            dve.wait_ge(s["bc_spread"], 1)
            v2.tensor_copy(bc[:, 0:4 * C].rearrange("p (b c) -> p b c", b=2), ps_agg[:]).then_inc(s["bc_made"], 1)
            v2.tensor_copy(bc[:, 4 * C:BC], ps_hm[:, 0:EXPERTS]).then_inc(s["bc_made"], 1)

            def low_halves(i, u):
                dve.wait_ge(a["xn_made"][u], i + 1)
                dve.wait_ge(a["high_used"][u], i + 1)
                v2.scalar_tensor_tensor(xhl[:, u, :, C:2 * C], xn[:, u], SCALE, xhl[:, u, :, 0:C], ALU.mult,
                                        ALU.subtract).then_inc(a["low_made"][u], 1)

            def stage_a(i, first=False, last=False):
                if not first:
                    normalize(i, 0)
                moments(i, 1)
                low_halves(i, 0)
                normalize(i, 1)
                if not last:
                    moments(i + 1, 0)
                low_halves(i, 1)

            def k_of_step(i, out_ap):
                for w in range(SLOTS):
                    dve.wait_ge(a["k_stored"][w], (i + 1) * GROUP)
                tiles = kst[:, bass.ds(i * GROUP * SLOTS, GROUP * SLOTS), :]
                return v2.tensor_reduce(out_ap, tiles.rearrange("p t c -> p c t"), AX.X, ALU.max)

            def merge(i):
                dve.wait_ge(s["kmax_merged"], i + 1)
                k_of_step(i, kpart[:]).then_inc(s["kpart_made"], 1)
                dve.wait_ge(s["kpart_made"], i + 1)
                op(kmax[:], kmax[:], kpart[:], ALU.max).then_inc(s["kmax_merged"], 1)

            v2.memset(kmax[:], -3.0e38).then_inc(s["kmax_merged"], 1)
            stage_a(0, first=True)
            with dve.Fori(1, A_STEPS - 1) as i:
                stage_a(i)
                merge(i - 1)
            stage_a(A_STEPS - 1, last=True)
            merge(A_STEPS - 2)
            merge(A_STEPS - 1)

            for u in range(SLOTS):
                dve.wait_ge(a["rows_kept"][u], A_STEPS)
                dve.wait_ge(a["k_summed"][u], PER_SLOT)
                dve.wait_ge(a["kept"][u], PER_SLOT)
            v2.memset(xs[:, :, C:C + 1], 1.0).then_inc(s["xs_ones"], 1)
            kcol = sm[:, 4, 0:HALVES]
            dve.wait_ge(s["kmax_turned"], 1)
            v2.tensor_reduce(kcol, ps_turn[:, 0:HALVES * NT].rearrange("p (h n) -> p h n", h=HALVES), AX.X, ALU.max
                             ).then_inc(s["kmax_reduced"], 1)
            dve.wait_ge(s["kmax_reduced"], 1)
            for h in range(HALVES):
                last = v2.tensor_scalar(wide[:, h, :], ones[:, 0:NT], kcol[:, h:h + 1], None, ALU.mult)
            last.then_inc(s["kmax_col_wide"], 1)
            dve.wait_ge(s["kmax_spread"], 1)
            v2.tensor_copy(kmax[:], ps_hm[0:NT, 0:C]).then_inc(s["kmax_made"], 1)
            dve.wait_ge(s["kmax_made"], 1)
            with dve.Fori(0, B_STEPS) as i:
                for u in range(SLOTS):
                    k_t = kst[:, bass.ds(i * SLOTS + u, 1), :].squeeze(1)
                    op(k_t, k_t, kmax[:], ALU.subtract).then_inc(b["k_shifted"][u], 1)

            links = [0]

            def link(ins):
                links[0] += 1
                ins.then_inc(s["lam_link"], 1)
                dve.wait_ge(s["lam_link"], links[0])

            for u in range(SLOTS):
                dve.wait_ge(b["lam_added"][u], B_STEPS)
            den, st, mvl = sm[:, 4, 2:4], stats[:, 0, 0:2, :], mv[:, 0, 0:2, :]
            guess_b, tmp_b, rstd_b = (sm[:, 5, 2 * q:2 * q + 2] for q in (1, 2, 3))
            link(v2.reciprocal(den, ps_agg[:, :, C]))
            for h in range(HALVES):
                last = v2.tensor_scalar(lam_n[:, h, :], ps_agg[:, h, 0:C], den[:, h:h + 1], None, ALU.mult)
            last.then_inc(s["lam_n_made"], 1)
            dve.wait_ge(s["lam_turned"], 1)
            v2.tensor_copy(lam_nT, ps_turn[:].rearrange("p (k c) -> p k c", k=HALVES)).then_inc(s["lam_nT_made"], 1)
            v2.memset(ones3, 1.0)
            v2.memset(bl3, 0.0)
            link(v2.memset(bmix3, 0.0))
            split(bl_b[0:NT], bl3, part16[0:NT], link)
            dve.wait_ge(s["lam_v"], 1)
            for h in range(HALVES):
                link(op(lam[:, h, :], ps_wide[:, h, 0:C], bv_b, ALU.add))
                link(v2.bn_stats(st[:, h, :], lam[:, h, :]))
                v2.bn_aggr(mvl[:, h, :], st[:, h, :]).then_inc(s["lam_ln"], 1)
            dve.wait_ge(s["lam_guess"], 1)
            link(op(tmp_b, guess_b, guess_b, ALU.mult))
            link(v2.scalar_tensor_tensor(tmp_b, mvl[:, :, 1], EPS, tmp_b, ALU.add, ALU.mult))
            link(v2.tensor_scalar(tmp_b, tmp_b, -0.5, 1.5, ALU.mult, ALU.add))
            link(op(tmp_b, tmp_b, guess_b, ALU.mult))
            link(op(rstd_b, tmp_b, vec[:, V_GM:V_GM + 2], ALU.mult))
            for h in range(HALVES):
                v2.tensor_scalar(wide[:, h, :], ones[:, 0:NT], vec[:, V_BQ + h:V_BQ + h + 1], None, ALU.mult)
                link(v2.tensor_scalar(lam[:, h, :], lam[:, h, :], mvl[:, h, 0:1], rstd_b[:, h:h + 1], ALU.subtract,
                                      ALU.mult))
                link(v2.tensor_scalar(lam[:, h, :], lam[:, h, :], vec[:, V_BM + h:V_BM + h + 1], None, ALU.add))
            dve.sem_inc(s["lam_done"], 1)
            v2.memset(x1, 0.0).then_inc(s["x2_zeroed"], 1)
            v2.memset(gate5, 1.0).then_inc(s["x2_zeroed"], 1)
            v2.memset(x2, 0.0).then_inc(s["x2_made"], 1)
            dve.wait_ge(s["dst_shifted"], 1)
            dve.wait_ge(s["x2_zeroed"], 2)
            dve.wait_ge(s["x2_made"], 1)
            sums = ps_agg.rearrange("p b c -> p (b c)")

            def one_hot(to, rel):
                return op(to[:, :, 0:NT], iota[:].unsqueeze(1).broadcast_to([128, to.shape[1], NT]),
                          rel.unsqueeze(2).broadcast_to([128, to.shape[1], NT]), ALU.is_equal)

            def build_up_to(end, waits=True):
                with dve.While(lambda: dve.snap(built, min_val=0, max_val=CHUNKS + HOTS) < end):
                    c = dve.snap(built, min_val=0, max_val=CHUNKS + HOTS - 2)
                    at = dve.snap(place, min_val=0, max_val=(HOTS - 2) * G * 128)
                    if waits:
                        dve.wait_ge(s["slots_freed"], c + 2)
                    one_hot(hot_all[:, bass.ds(at, 2 * G * 128)].rearrange("p (g n) -> p g n", g=2 * G),
                            dst_in[:, bass.ds(c * G, 2 * G)]).then_inc(s["hot_built"], 2)
                    dve.reg_add(built, built, 2)
                    dve.reg_add(place, place, 2 * G * 128)
                    dve.reg_mod(place, place, HOTS * G * 128)

            for c in range(0, EARLY, 2):
                one_hot(hot_all[:, c * G * 128:(c + 2) * G * 128].rearrange("p (g n) -> p g n", g=2 * G),
                        dst_in[:, c * G:(c + 2) * G]).then_inc(s["hot_built"], 2)

            def one_hot_next(c, tiles, v, prev):
                if prev is not None:
                    dve.wait_ge(s["next_summed"], prev)
                v2.tensor_scalar(dst_rel_next, dst_in[:, bass.ds(c * G, G)], tile_base[:, bass.ds(tiles, 1)], None,
                                 ALU.add).then_inc(s["rel_next_made"], 1)
                dve.wait_ge(s["rel_next_made"], v)
                one_hot(hot_next, dst_rel_next).then_inc(s["hot_next_built"], 1)

            done = [0]

            def after(base, ins):
                done[0] += 1
                ins.then_inc(s["dve_link"], 1)
                dve.wait_ge(s["dve_link"], base + done[0])

            def gates(v, prev, base):
                dve.wait_ge(s["logits_done"], v)
                logits = ps_turn[0:NT, 500:500 + EXPERTS]
                after(base, v2.tensor_reduce(lmax, logits, AX.X, ALU.max))
                v2.tensor_scalar(lg, logits, lmax, None, ALU.subtract).then_inc(s["lg_shifted"], 1)
                dve.wait_ge(s["lg_exp"], v)
                after(base, v2.reciprocal(rsum, esum))
                after(base, v2.tensor_scalar(gt, ex, rsum, None, ALU.mult))
                v2.tensor_scalar(ez, gt, rsum, None, ALU.subtract).then_inc(s["z_made"], 1)
                g_e = gt.unsqueeze(2).broadcast_to([NT, EXPERTS, EXPERTS])
                g_f = gt.unsqueeze(1).broadcast_to([NT, EXPERTS, EXPERTS])
                op(gt_m, g_f, g_e, ALU.is_gt)
                after(base, op(eq_m, g_f, g_e, ALU.is_equal))
                after(base, op(eq_m, eq_m, lower[:], ALU.mult))
                after(base, op(gt_m, gt_m, eq_m, ALU.add))
                after(base, v2.tensor_reduce(rank, gt_m, AX.X, ALU.add))
                dve.wait_ge(s["z_exp"], v)
                after(base, v2.scalar_tensor_tensor(ez, rank, float(TOPK), ez, ALU.is_lt, ALU.mult, accum_out=wsum))
                after(base, v2.reciprocal(rw, wsum))
                dve.wait_ge(s["gate_turned"], prev)
                v2.tensor_scalar(gate5[:, 0:EXPERTS], ez, rw, None, ALU.mult).then_inc(s["gate_made"], 1)

            def stage2_weigh(v, prev):
                dve.wait_ge(s["eh2_made"], v)
                dve.wait_ge(s["gates_spread"], v)
                dve.wait_ge(s["l3_done"], prev)
                op(eh2g, ps_gates.rearrange("p (h n) -> p h n", h=2), eh2, ALU.mult
                   ).then_inc(s["eh2g_made"], 1)

            def stage2_out(v, prev):
                dve.wait_ge(s["l3_done"], v)
                dve.wait_ge(s["y_stored"], prev * 32)
                op(y, ps_l3[0:NT, 0:C], x1, ALU.add).then_inc(s["y_made"], 1)

            def newton(base, guess, variance, tmp, to):
                after(base, op(tmp, guess, guess, ALU.mult))
                after(base, v2.scalar_tensor_tensor(tmp, variance, EPS, tmp, ALU.add, ALU.mult))
                after(base, v2.tensor_scalar(tmp, tmp, -0.5, 1.5, ALU.mult, ALU.add))
                after(base, op(to, guess, tmp, ALU.mult))

            def node_tile(i, u, v, prev, c):
                done[0] = 0
                base = dve.snap(prev * DVE_LINKS, min_val=0, max_val=T * DVE_LINKS)
                dve.wait_ge(s["tile_summed"], v)
                dve.wait_ge(s["agg_scaled"], prev)
                v2.tensor_scalar(deg, ps_agg[0:NT, u, C:C + 1], 1.0, SCALE, ALU.max, ALU.mult
                                 ).then_inc(s["deg_read"], 1)
                dve.wait_ge(s["deg_read"], v)
                v2.reciprocal(rc, deg).then_inc(s["rc_made"], 1)
                build_up_to(c + EARLY + 2, waits=False)
                gates(v, prev, base)
                dve.wait_ge(s["gnn_done"], v)
                v2.bn_stats(st1, ps_hm[0:NT, 0:C]).then_inc(s["st1_made"], 1)
                dve.wait_ge(s["x2_zeroed"], 2)
                dve.wait_ge(s["st1_made"], v)
                v2.bn_aggr(mv1, st1).then_inc(s["mv1_made"], 1)
                dve.reg_mov(last_cut, cut)
                dve.reg_load(cut, cuts[0:1, bass.ds(v, 1)])
                dve.reg_alu(last_cut, last_cut, cut, ALU.is_equal)
                dve.reg_mul(on, on, last_cut)
                dve.reg_add(on, on, 1)
                dve.wait_ge(s["mv1_made"], v)
                stage2_weigh(v, prev)
                v2.scalar_tensor_tensor(hn, ps_hm[0:NT, 0:C], mv1[:, 0:1], gg_b[0:NT], ALU.subtract, ALU.mult
                                        ).then_inc(s["h_used"], 1)
                dve.wait_ge(s["guess1"], v)
                newton(base, g1, mv1[:, 1:2], nt1, rs1)
                dve.wait_ge(s["h_used"], v)
                after(base, v2.scalar_tensor_tensor(hn, hn, rs1, bg_b[0:NT], ALU.mult, ALU.add))
                stage2_out(v, prev)
                dve.wait_ge(s["y_made"], v)
                dve.wait_ge(x_row_in[u], (i + 1) * 32)
                v2.scalar_tensor_tensor(x1, hn, 0.0, x_rows[:, u, :], ALU.max, ALU.add
                                        ).then_inc(s["x_row_used"], 1)
                dve.wait_ge(s["x_row_used"], v)
                dve.wait_ge(s["mix_done"], v)
                op(x1, ps_mix, x1, ALU.add).then_inc(s["x1_made"], 1)
                dve.wait_ge(s["x1_made"], v)
                v2.bn_stats(st2, x1).then_inc(s["st2_made"], 1)
                dve.wait_ge(s["x2_zeroed"], 2)
                dve.wait_ge(s["st2_made"], v)
                v2.bn_aggr(mv2, st2).then_inc(s["mv2_made"], 1)
                one_hot_next(dve.snap(cut, min_val=0, max_val=CHUNKS - 1), dve.snap(on, min_val=1, max_val=T),
                             v + 1, v)
                dve.wait_ge(s["guess2"], v)
                newton(base, g2, mv2[:, 1:2], nt2, rs2)
                dve.wait_ge(s["both_turned"], v)
                v2.tensor_scalar(x2, x1, mv2[:, 0:1], rs2, ALU.subtract, ALU.mult).then_inc(s["x2_made"], 1)
                assert done[0] == DVE_LINKS, done

            cut, last_cut, on, built, place = (dve.alloc_register(f"dve_{q}") for q in (
                "cut", "last_cut", "on", "built", "place"))
            dve.reg_mov(built, EARLY)
            dve.reg_mov(place, EARLY * G * 128)
            dve.reg_mov(on, 1)
            dve.wait_ge(s["cuts_made"], 1)
            dve.reg_load(cut, cuts[0:1, 0:1])
            one_hot_next(dve.snap(cut, min_val=0, max_val=CHUNKS - 1), 1, 1, None)
            dve.wait_ge(s["bmix_spread"], 1)
            v2.tensor_copy(bmix, ps_wide[0:NT, 2, 0:C]).then_inc(s["bmix_made"], 1)
            dve.wait_ge(s["bmix_made"], 1)
            split(bmix, bmix3, part16[0:NT], link)
            dve.wait_ge(s["wmix_done"], 1)
            for h in range(HALVES):
                o = h * 128
                op(wmix[:, h, o:o + 128], ps_wide[:, h, o:o + 128], ident[:], ALU.add)
                last = v2.tensor_copy(wmix[:, h, 128 - o:256 - o], ps_wide[:, h, 128 - o:256 - o])
            last.then_inc(s["wmix_made"], 1)

            with dve.Fori(0, T // 2) as i:
                for u in range(2):
                    prev = dve.snap(i * 2 + u, min_val=0, max_val=T - 1)
                    v = dve.snap(i * 2 + u + 1, min_val=1, max_val=T)
                    c = dve.snap(cut, min_val=0, max_val=CHUNKS - 1)
                    build_up_to(c + 1)
                    node_tile(i, u, v, prev, c)
            v = T + 1
            done[0] = 0
            gates(v, T, T * DVE_LINKS)
            stage2_weigh(v, T)
            stage2_out(v, T)

        @block.scalar
        def _(act):
            f = nc.scalar.activation
            act.preload_act_table_set("natural_log_exp_and_others")
            var = mv[0:NT, :, :, 1]
            ln_a, guess_a = (sm[0:NT, q].rearrange("p (u k) -> p u k", u=SLOTS) for q in range(2))
            act.wait_ge(s["consts_made"], 3)

            def guess(i, u):
                act.wait_ge(a["mv_made"][u], i + 1)
                f(ln_a[:, u], var[:, u], ACT.Ln, bias=eps[0:NT]).then_inc(a["ln_made"][u], 1)
                act.wait_ge(a["ln_made"][u], i + 1)
                act.wait_ge(a["rstd_made"][u], i)
                f(guess_a[:, u], ln_a[:, u], ACT.Exp, scale=-0.5).then_inc(a["guess_made"][u], 1)

            guess(0, 0)
            for blk in range(NB):
                n = min(128, J - blk * 128)
                act.wait_ge(s["dst_turned"], blk + 1)
                f(dst_in[:, blk * 128:blk * 128 + n], ps_hm[:, 0:n], ACT.Copy).then_inc(s["dst_copied"], 1)
            for w, to in enumerate((wlT, wrT, wqT)):
                act.wait_ge(s["nat_turned"], w + 1)
                f(to[:], ps_wide[:, w, :].rearrange("p (k c) -> p k c", k=HALVES), ACT.Copy).then_inc(s["nat_copied"], 1)

            def stage_a(i, last=False):
                for v in range(GROUP * SLOTS + 1):
                    if v < GROUP * SLOTS:
                        g, k = v // GROUP, v % GROUP
                        u, t = v % SLOTS, v // SLOTS
                        if k == 0:
                            act.wait_ge(a["xn_made"][g], i + 1)
                            act.wait_ge(a["rows_stored"][g], i * 32)
                            f(xhl[:, g, :, 0:C], xn[:, g], ACT.Copy, scale=SCALE).then_inc(a["high_used"][g], 1)
                        act.wait_ge(a["turned"][g], i * GROUP + k + 1)
                        act.wait_ge(a["kept"][u], i * GROUP + t)
                        act.wait_ge(a["k_summed"][u], i * GROUP + t)
                        f(xT[:, u], ps_wide[:, u, 0:HALVES * NT].rearrange("p (h n) -> p h n", h=HALVES), ACT.Copy
                          ).then_inc(a["evacuated"][u], 1)
                        if k == 1 and not (last and g == 1):
                            guess(i + g, 1 - g)
                        if k == 2:
                            f(xs[:, bass.ds((i * SLOTS + g) * GROUP, GROUP), 0:C], xn[:, g], ACT.Copy
                              ).then_inc(a["rows_kept"][g], 1)
                    if v:
                        u, t = (v - 1) % SLOTS, (v - 1) // SLOTS
                        act.wait_ge(a["k_summed"][u], i * GROUP + t + 1)
                        f(kst[:, bass.ds(i * GROUP * SLOTS + v - 1, 1), :].squeeze(1), ps_wide[0:NT, 2 + u, 0:C],
                          ACT.Copy).then_inc(a["k_stored"][u], 1)

            act.wait_ge(s["dst_shifted"], 1)
            with act.Fori(0, A_STEPS - 1) as i:
                stage_a(i)
            stage_a(A_STEPS - 1, last=True)

            with act.Fori(0, B_STEPS) as i:
                for u in range(SLOTS):
                    act.wait_ge(b["k_shifted"][u], i + 1)
                    act.wait_ge(b["lam_added"][u], i)
                    f(ek[:, u, :], kst[:, bass.ds(i * SLOTS + u, 1), :].squeeze(1), ACT.Exp
                      ).then_inc(b["exp_made"][u], 1)
            ln_b, guess_b = (sm[:, 5, 2 * q:2 * q + 2] for q in range(2))
            act.wait_ge(s["lam_ln"], 2)
            f(ln_b, mv[:, 0, 0:2, 1], ACT.Ln, bias=eps[:]).then_inc(s["lam_ln"], 1)
            act.wait_ge(s["lam_ln"], 3)
            f(guess_b, ln_b, ACT.Exp, scale=-0.5).then_inc(s["lam_guess"], 1)
            act.wait_ge(s["bmix_made"], 1)

            def rsqrt(v, variance, ln, to, ready, ln_made, made):
                act.wait_ge(ready, v)
                f(ln, variance, ACT.Ln, bias=eps[0:NT]).then_inc(ln_made, 1)
                act.wait_ge(ln_made, v)
                f(to, ln, ACT.Exp, scale=-0.5).then_inc(made, 1)

            def stage2_exps(v):
                act.wait_ge(s["lg_shifted"], v)
                f(ex, lg, ACT.Exp, accum_out=esum).then_inc(s["lg_exp"], 1)
                act.wait_ge(s["l1s_done"], v)
                act.wait_ge(s["l2_done"], v - 1)
                for o in range(2):
                    last = f(sh1[:, o, :], ps_l1[:, 0, o * NT:(o + 1) * NT], ACT.Relu,
                             bias=vec[:, V_SB1 + o:V_SB1 + o + 1])
                last.then_inc(s["sh1_made"], 1)
                act.wait_ge(s["z_made"], v)
                f(ez, ez, ACT.Exp).then_inc(s["z_exp"], 1)
                act.wait_ge(s["l1e_done"], v)
                for e in range(EXPERTS):
                    last = f(eh1[:, e, :], ps_l1[:, 1, e * NT:(e + 1) * NT], ACT.Relu,
                             bias=vec[:, V_EB1 + e:V_EB1 + e + 1])
                last.then_inc(s["eh1_made"], 1)
                act.wait_ge(s["gate_turned"], v)
                act.wait_ge(s["l3_done"], v - 1)
                f(gateT, ps_turn[0:EXPERTS + 1, 0:NT], ACT.Copy).then_inc(s["gateT_made"], 1)

            def stage2_relu(v):
                act.wait_ge(s["l2_done"], v)
                act.wait_ge(s["eh2g_made"], v - 1)
                for r in range(2):
                    last = f(eh2[:, r, :], ps_l2[:, (1 + r) * NT:(2 + r) * NT], ACT.Relu,
                             bias=vec[:, V_EB2 + r:V_EB2 + r + 1])
                last.then_inc(s["eh2_made"], 1)
                f(sh2, ps_l2[:, 0:NT], ACT.Relu, bias=vec[:, V_SB2:V_SB2 + 1]).then_inc(s["sh2_made"], 1)

            def turn_back(v):
                act.wait_ge(s["both_turned"], v)
                act.wait_ge(s["l1e_done"], v - 1)
                act.wait_ge(s["gnn_done"], v - 1)
                f(turned, ps_turn[:, 0:4 * NT].rearrange("p (h n) -> p h n", n=NT), ACT.Copy
                  ).then_inc(s["both_used"], 1)

            def store(v):
                act.wait_ge(s["y_made"], v)
                for r0, r1 in ((0, ROWS_A), (ROWS_A, NT)):
                    act.dma_start(tile_rows(out, v - 2, r0, r1), y[r0:r1].unsqueeze(1)).then_inc(s["y_stored"], 16)

            def node_tile(v, bank_v, first=False):
                act.wait_ge(s["mix_done"], v - 1)
                f(xTc, xnT[:, :, bass.ds((v - 1) * NT, NT)], ACT.Copy).then_inc(s["xTc_made"], 1)
                act.wait_ge(s["tile_summed"], v)
                act.wait_ge(s["rc_made"], v)
                act.wait_ge(s["both_turned"], v - 1)
                f(agg_mean, ps_agg[0:NT, bank_v, 0:C], ACT.Copy, scale=rc).then_inc(s["agg_scaled"], 1)
                turn_back(v)
                stage2_exps(v)
                stage2_relu(v)
                rsqrt(v, mv1[:, 1:2], lv1, g1, s["mv1_made"], s["ln1"], s["guess1"])
                if first:
                    act.sem_inc(s["y_stored"], 32)
                else:
                    store(v)
                rsqrt(v, mv2[:, 1:2], lv2, g2, s["mv2_made"], s["ln2"], s["guess2"])

            node_tile(1, 0, first=True)
            with act.Fori(0, T // 2 - 1) as i:
                for u in range(2):
                    node_tile(act.snap(i * 2 + 2 + u, min_val=2, max_val=T), 1 - u)
            node_tile(T, (T - 1) % 2)
            v = T + 1
            act.wait_ge(s["both_turned"], v)
            f(x2T, ps_turn[:, 2 * NT:4 * NT].rearrange("p (h n) -> p h n", n=NT), ACT.Copy).then_inc(s["both_used"], 1)
            stage2_exps(v)
            stage2_relu(v)
            store(v)
            act.wait_ge(s["y_stored"], 32 * (T + 1))


_INS = ["x", "src", "dst"] + [f"L0_gnn_{n}" for n in ("W_l", "b_l", "W_r", "gamma", "beta")] + \
       [f"L0_mix_{n}" for n in ("W_qk", "b_qk", "W_v", "b_v", "gamma", "beta")] + \
       [f"L0_ffn_{n}" for n in ("sW1", "sb1", "sW2", "sb2", "sW3", "sb3", "eW1", "eb1", "eW2", "eb2", "eW3", "eb3",
                                "gW", "gb")]


def kernel(**inputs):
    import numpy as _np
    import concourse.bacc as _bacc
    from concourse import mybir as _mybir
    from concourse.bass_utils import run_bass_kernel_spmd as _run

    nc = _bacc.Bacc("TRN2", target_bir_lowering=False, num_devices=1)
    arrays, args = {}, []
    for name in _INS:
        a = _np.ascontiguousarray(inputs[name])
        arrays[f"in_{name}_dram"] = a
        args.append(nc.dram_tensor(f"in_{name}_dram", a.shape, _mybir.dt.from_np(a.dtype), kind="ExternalInput").ap())
    args.append(nc.dram_tensor("out_dram", inputs["x"].shape, F32, kind="ExternalOutput").ap())
    gps_layer(nc, *args)
    r = _run(nc, [arrays], core_ids=[0])
    return r.results[0]["out_dram"]
```
